# Optimizing a Trainium2 kernel written in Bass

```python
import numpy as np
import jax
import jax.numpy as jnp

def _softmax(x, axis=-1):
    return jax.nn.softmax(x, axis=axis)

def _gelu(x):
    return jax.nn.gelu(x, approximate=True)

def _silu(x):
    return jax.nn.silu(x)

def _sigmoid(x):
    return jax.nn.sigmoid(x)

def _layernorm(x, axis=-1, eps=1e-05):
    m = jnp.mean(x, axis=axis, keepdims=True)
    v = jnp.var(x, axis=axis, keepdims=True)
    return (x - m) / jnp.sqrt(v + eps)

def _scatter_add(tgt, idx, src, axis=0):
    return tgt.at[idx].add(src)

def _segment_sum(src, seg, n):
    return jax.ops.segment_sum(src, seg, n)
kernel_name = 'mk_adaln_ffn_d2_seqx_r4_3f4676'

def setup_inputs(seed: int=0):
    np.random.seed(seed)
    _w = jnp.asarray

    def _rec_inputs():
        import jax
        import jax.numpy as jnp
        _rk = jax.random.key(seed)
        x = -0.0002928 + 1 * jax.random.normal(jax.random.fold_in(_rk, 1), (2, 1024, 256), jnp.float32)
        _lenS = 1024 - jax.random.randint(jax.random.fold_in(_rk, 7), (2,), 0, max(1, 1024 // 4) + 1, jnp.int32)
        _lenS2 = 1024 - jax.random.randint(jax.random.fold_in(_rk, 8), (2,), 0, max(1, 1024 // 4) + 1, jnp.int32)
        fside_16xSxS_0 = -5.72187e-05 + 0.999849 * jax.random.normal(jax.random.fold_in(_rk, 11), (16, 1024, 1024), jnp.float32)
        cond_64 = -0.0265395 + 0.99382 * jax.random.normal(jax.random.fold_in(_rk, 13), (2, 64), jnp.float32)
        _validS = jnp.arange(1024)[None, :] < _lenS[:, None]
        _validS2 = jnp.arange(1024)[None, :] < _lenS2[:, None]
        _causal = jnp.tril(jnp.ones((1024, 1024), dtype=bool))
        mask_BxS_bk0 = jnp.logical_not(jnp.broadcast_to(_validS[:, :], (2, 1024)))
        return (x, fside_16xSxS_0, cond_64, mask_BxS_bk0)
    x, fside_16xSxS_0, cond_64, mask_BxS_bk0 = _rec_inputs()

    def _L0_cond_setup():
        import jax, jax.numpy as jnp
        import numpy as np
        B, N, DIM, H, DH = (2, 512, 256, 16, 64)
        INNER = H * DH
        EPS = 1e-05

        def layernorm(x, g):
            mean = jnp.mean(x, axis=-1, keepdims=True)
            var = jnp.var(x, axis=-1, keepdims=True)
            return (x - mean) * jax.lax.rsqrt(var + EPS) * g
        key = jax.random.key(seed)
        ks = jax.random.split(key, 10)
        x = jax.random.normal(ks[0], (B, N, DIM), dtype=jnp.float32)
        attn_bias = jax.random.normal(ks[1], (H, N, N), dtype=jnp.float32)
        mask = jax.random.randint(ks[2], (B, N), 0, 2).astype(bool)
        g_in = jnp.ones((DIM,), dtype=jnp.float32)
        null_attn_bias = jax.random.normal(ks[3], (H,), dtype=jnp.float32)
        null_kv = jax.random.normal(ks[4], (2, DH), dtype=jnp.float32)
        Wq = jax.random.normal(ks[5], (DIM, INNER), dtype=jnp.float32) * 0.02
        Wkv = jax.random.normal(ks[6], (DIM, 2 * DH), dtype=jnp.float32) * 0.02
        Wo = jax.random.normal(ks[7], (INNER, DIM), dtype=jnp.float32) * 0.02
        g_out = jnp.ones((DIM,), dtype=jnp.float32)
        return {'x': x, 'attn_bias': attn_bias, 'mask': mask, 'g_in': g_in, 'null_attn_bias': null_attn_bias, 'null_kv': null_kv, 'Wq': Wq, 'Wkv': Wkv, 'Wo': Wo, 'g_out': g_out}
    _L0_cond_all = _L0_cond_setup()
    _L0_cond_in = {k: v for k, v in _L0_cond_all.items() if k in ('g_in', 'null_attn_bias', 'Wq', 'Wkv', 'Wo', 'g_out')}
    del _L0_cond_all

    def _L0_ffn_setup():
        import jax, jax.numpy as jnp
        import numpy as np
        EPS = 1e-08
        key = jax.random.key(seed)
        kx, kw = jax.random.split(key)
        x = jax.random.normal(kx, (8, 1024, 256), dtype=jnp.float32)
        weight = jax.random.normal(kw, (256, 256), dtype=jnp.float32) * (1.0 / np.sqrt(256))
        return {'x': x, 'weight': weight}
    _L0_ffn_all = _L0_ffn_setup()
    _L0_ffn_in = {k: v for k, v in _L0_ffn_all.items() if k in ('weight',)}
    del _L0_ffn_all

    def _L1_cond_setup():
        import jax, jax.numpy as jnp
        import numpy as np
        B, S, H = (4, 512, 256)
        E = 8
        M = 128
        K = 2
        N_SHARED = 2
        SM = M * N_SHARED
        G = 64
        GE_TEMP = 1.0
        ALPHA = 0.001
        SEQ_AUX = True
        NORM_TOPK = True
        COS_TEMP = 0.78
        CONS_ALPHA = 0.01
        LEAKY_SLOPE = 0.01
        EPS_COS = 1e-08

        def _leaky(x):
            return jnp.where(x >= 0, x, LEAKY_SLOPE * x)

        def _moe_forward(hidden_states, g, wt, wg, w_gate, w_up, w_down, sw_gate, sw_up, sw_down):
            b, s, h = hidden_states.shape
            x = hidden_states.reshape(-1, h)
            T = x.shape[0]
            logits_h = x @ wt.T
            logits_g = g @ wg.T
            logits_g = jnp.repeat(logits_g, s, axis=0)
            logits = (logits_h + logits_g / GE_TEMP) / (1.0 + 1.0 / GE_TEMP)
            scores = jax.nn.softmax(logits, axis=-1)
            topk_w, topk_idx = jax.lax.top_k(scores, K)
            if K > 1 and NORM_TOPK:
                topk_w = topk_w / (topk_w.sum(-1, keepdims=True) + 1e-20)
            onehot = jax.nn.one_hot(topk_idx.reshape(b, s * K), E, dtype=jnp.float32)
            ce = onehot.sum(1) / (s * K / E)
            aux_loss = (ce * scores.reshape(b, s, E).mean(1)).sum(1).mean() * ALPHA
            gp = _leaky(jnp.einsum('th,ehm->etm', x, w_gate))
            up = jnp.einsum('th,ehm->etm', x, w_up)
            y_all = jnp.einsum('etm,emh->eth', gp * up, w_down)
            y_sel = y_all[topk_idx, jnp.arange(T)[:, None], :]
            y = (y_sel * topk_w[..., None]).sum(1).reshape(b, s, h)
            p = _leaky(hidden_states @ sw_gate) * (hidden_states @ sw_up) @ sw_down
            y = y + p
            num = jnp.sum(y * p, -1)
            den = jnp.maximum(jnp.linalg.norm(y, axis=-1), EPS_COS) * jnp.maximum(jnp.linalg.norm(p, axis=-1), EPS_COS)
            closs = CONS_ALPHA * jnp.mean(num / den / (1.0 + COS_TEMP))
            return (y, aux_loss + closs)
        key = jax.random.key(seed)
        ks = jax.random.split(key, 12)
        sh = 1.0 / np.sqrt(H)
        sm = 1.0 / np.sqrt(M)
        ssm = 1.0 / np.sqrt(SM)
        sg = 1.0 / np.sqrt(G)
        return {'hidden_states': jax.random.normal(ks[0], (B, S, H), jnp.float32), 'g': jax.random.normal(ks[1], (B, G), jnp.float32), 'wt': jax.random.uniform(ks[2], (E, H), jnp.float32, -sh, sh), 'wg': jax.random.uniform(ks[3], (E, G), jnp.float32, -sg, sg), 'w_gate': jax.random.uniform(ks[4], (E, H, M), jnp.float32, -sh, sh), 'w_up': jax.random.uniform(ks[5], (E, H, M), jnp.float32, -sh, sh), 'w_down': jax.random.uniform(ks[6], (E, M, H), jnp.float32, -sm, sm), 'sw_gate': jax.random.uniform(ks[7], (H, SM), jnp.float32, -sh, sh), 'sw_up': jax.random.uniform(ks[8], (H, SM), jnp.float32, -sh, sh), 'sw_down': jax.random.uniform(ks[9], (SM, H), jnp.float32, -ssm, ssm)}
    _L1_cond_all = _L1_cond_setup()
    _L1_cond_in = {k: v for k, v in _L1_cond_all.items() if k in ('wt', 'wg', 'w_gate', 'w_up', 'w_down', 'sw_gate', 'sw_up', 'sw_down')}
    del _L1_cond_all

    def _L1_ffn_setup():
        import jax, jax.numpy as jnp
        import numpy as np
        EPS = 1e-05
        NUM_HEADS = 16
        NUM_KV_HEADS = 4
        NUM_EXPERTS = 8
        TOP_K = 2

        def _layernorm(x, w, b):
            mu = jnp.mean(x, axis=-1, keepdims=True)
            var = jnp.mean((x - mu) ** 2, axis=-1, keepdims=True)
            return (x - mu) * jax.lax.rsqrt(var + EPS) * w + b
        key = jax.random.key(seed)
        ks = jax.random.split(key, 8)
        S, B, H = (256, 4, 256)
        F = 512
        hd = H // NUM_HEADS
        qkv_out = (NUM_HEADS + 2 * NUM_KV_HEADS) * hd
        w_scale = 0.02
        return {'hidden_states': jax.random.normal(ks[0], (S, B, H), jnp.float32), 'ln1_weight': jnp.ones((H,), jnp.float32), 'ln1_bias': jnp.zeros((H,), jnp.float32), 'ln2_weight': jnp.ones((H,), jnp.float32), 'ln2_bias': jnp.zeros((H,), jnp.float32), 'qkv_weight': jax.random.normal(ks[1], (qkv_out, H), jnp.float32) * w_scale, 'proj_weight': jax.random.normal(ks[2], (H, H), jnp.float32) * w_scale, 'router_weight': jax.random.normal(ks[3], (NUM_EXPERTS, H), jnp.float32) * w_scale, 'moe_w1': jax.random.normal(ks[4], (NUM_EXPERTS, H, F), jnp.float32) * w_scale, 'moe_w2': jax.random.normal(ks[5], (NUM_EXPERTS, F, H), jnp.float32) * w_scale}
    _L1_ffn_all = _L1_ffn_setup()
    _L1_ffn_in = {k: v for k, v in _L1_ffn_all.items() if k in ('ln1_weight', 'ln1_bias', 'ln2_weight', 'ln2_bias', 'qkv_weight', 'proj_weight', 'router_weight', 'moe_w1', 'moe_w2')}
    del _L1_ffn_all
    return {'x': x, 'fside_16xSxS_0': fside_16xSxS_0, 'cond_64': cond_64, 'mask_BxS_bk0': mask_BxS_bk0, 'L0_cond_g_in': _L0_cond_in['g_in'], 'L0_cond_null_attn_bias': _L0_cond_in['null_attn_bias'], 'L0_cond_Wq': _L0_cond_in['Wq'], 'L0_cond_Wkv': _L0_cond_in['Wkv'], 'L0_cond_Wo': _L0_cond_in['Wo'], 'L0_cond_g_out': _L0_cond_in['g_out'], 'L0_ffn_weight': _L0_ffn_in['weight'], 'L1_cond_wt': _L1_cond_in['wt'], 'L1_cond_wg': _L1_cond_in['wg'], 'L1_cond_w_gate': _L1_cond_in['w_gate'], 'L1_cond_w_up': _L1_cond_in['w_up'], 'L1_cond_w_down': _L1_cond_in['w_down'], 'L1_cond_sw_gate': _L1_cond_in['sw_gate'], 'L1_cond_sw_up': _L1_cond_in['sw_up'], 'L1_cond_sw_down': _L1_cond_in['sw_down'], 'L1_ffn_ln1_weight': _L1_ffn_in['ln1_weight'], 'L1_ffn_ln1_bias': _L1_ffn_in['ln1_bias'], 'L1_ffn_ln2_weight': _L1_ffn_in['ln2_weight'], 'L1_ffn_ln2_bias': _L1_ffn_in['ln2_bias'], 'L1_ffn_qkv_weight': _L1_ffn_in['qkv_weight'], 'L1_ffn_proj_weight': _L1_ffn_in['proj_weight'], 'L1_ffn_router_weight': _L1_ffn_in['router_weight'], 'L1_ffn_moe_w1': _L1_ffn_in['moe_w1'], 'L1_ffn_moe_w2': _L1_ffn_in['moe_w2']}

def reference(x, fside_16xSxS_0, cond_64, mask_BxS_bk0, L0_cond_g_in, L0_cond_null_attn_bias, L0_cond_Wq, L0_cond_Wkv, L0_cond_Wo, L0_cond_g_out, L0_ffn_weight, L1_cond_wt, L1_cond_wg, L1_cond_w_gate, L1_cond_w_up, L1_cond_w_down, L1_cond_sw_gate, L1_cond_sw_up, L1_cond_sw_down, L1_ffn_ln1_weight, L1_ffn_ln1_bias, L1_ffn_ln2_weight, L1_ffn_ln2_bias, L1_ffn_qkv_weight, L1_ffn_proj_weight, L1_ffn_router_weight, L1_ffn_moe_w1, L1_ffn_moe_w2):
    import jax
    import jax.numpy as jnp

    def _L0_cond_ref(x, attn_bias, mask, g_in, null_attn_bias, null_kv, Wq, Wkv, Wo, g_out):
        import jax, jax.numpy as jnp
        import numpy as np
        B, N, DIM, H, DH = (2, 512, 256, 16, 64)
        INNER = H * DH
        EPS = 1e-05

        def layernorm(x, g):
            mean = jnp.mean(x, axis=-1, keepdims=True)
            var = jnp.var(x, axis=-1, keepdims=True)
            return (x - mean) * jax.lax.rsqrt(var + EPS) * g
        b, n, _ = x.shape
        scale = DH ** (-0.5)
        xn = layernorm(x, g_in)
        q = (xn @ Wq).reshape(b, n, H, DH).transpose(0, 2, 1, 3) * scale
        kv = xn @ Wkv
        k, v = (kv[..., :DH], kv[..., DH:])
        nk = jnp.broadcast_to(null_kv[0], (b, 1, DH))
        nv = jnp.broadcast_to(null_kv[1], (b, 1, DH))
        k = jnp.concatenate([nk, k], axis=1)
        v = jnp.concatenate([nv, v], axis=1)
        sim = jnp.einsum('bhid,bjd->bhij', q, k)
        null_col = jnp.broadcast_to(null_attn_bias[:, None, None], (H, n, 1))
        bias = jnp.concatenate([null_col, attn_bias], axis=-1)
        sim = sim + bias
        neg = -jnp.finfo(sim.dtype).max
        j = n + 1
        causal_mask = jnp.triu(jnp.ones((n, j), dtype=bool), k=j - n + 1)
        sim = jnp.where(causal_mask, neg, sim)
        mask_p = jnp.pad(mask, ((0, 0), (1, 0)), constant_values=True)
        sim = jnp.where(mask_p[:, None, None, :], sim, neg)
        attn = jax.nn.softmax(sim, axis=-1)
        out = jnp.einsum('bhij,bjd->bhid', attn, v)
        out = out.transpose(0, 2, 1, 3).reshape(b, n, INNER)
        out = out @ Wo
        return layernorm(out, g_out)

    def _L0_ffn_ref(x, weight):
        import jax, jax.numpy as jnp
        import numpy as np
        EPS = 1e-08
        w_scale = jnp.mean(jnp.abs(weight)) + EPS
        u = weight / w_scale
        w_quant = u + jax.lax.stop_gradient(jnp.clip(jnp.round(u), -1.0, 1.0) - u)
        a_scale = jnp.max(jnp.abs(x), axis=-1, keepdims=True) + EPS
        z = jnp.clip(x / a_scale * 127.0, -128.0, 127.0)
        a_quant = z + jax.lax.stop_gradient(jnp.round(z) - z)
        y = jnp.einsum('bsi,oi->bso', a_quant, w_quant)
        y = y * (w_scale * a_scale / 127.0)
        return y

    def _L1_cond_ref(hidden_states, g, wt, wg, w_gate, w_up, w_down, sw_gate, sw_up, sw_down):
        import jax, jax.numpy as jnp
        import numpy as np
        B, S, H = (4, 512, 256)
        E = 8
        M = 128
        K = 2
        N_SHARED = 2
        SM = M * N_SHARED
        G = 64
        GE_TEMP = 1.0
        ALPHA = 0.001
        SEQ_AUX = True
        NORM_TOPK = True
        COS_TEMP = 0.78
        CONS_ALPHA = 0.01
        LEAKY_SLOPE = 0.01
        EPS_COS = 1e-08

        def _leaky(x):
            return jnp.where(x >= 0, x, LEAKY_SLOPE * x)

        def _moe_forward(hidden_states, g, wt, wg, w_gate, w_up, w_down, sw_gate, sw_up, sw_down):
            b, s, h = hidden_states.shape
            x = hidden_states.reshape(-1, h)
            T = x.shape[0]
            logits_h = x @ wt.T
            logits_g = g @ wg.T
            logits_g = jnp.repeat(logits_g, s, axis=0)
            logits = (logits_h + logits_g / GE_TEMP) / (1.0 + 1.0 / GE_TEMP)
            scores = jax.nn.softmax(logits, axis=-1)
            topk_w, topk_idx = jax.lax.top_k(scores, K)
            if K > 1 and NORM_TOPK:
                topk_w = topk_w / (topk_w.sum(-1, keepdims=True) + 1e-20)
            onehot = jax.nn.one_hot(topk_idx.reshape(b, s * K), E, dtype=jnp.float32)
            ce = onehot.sum(1) / (s * K / E)
            aux_loss = (ce * scores.reshape(b, s, E).mean(1)).sum(1).mean() * ALPHA
            gp = _leaky(jnp.einsum('th,ehm->etm', x, w_gate))
            up = jnp.einsum('th,ehm->etm', x, w_up)
            y_all = jnp.einsum('etm,emh->eth', gp * up, w_down)
            y_sel = y_all[topk_idx, jnp.arange(T)[:, None], :]
            y = (y_sel * topk_w[..., None]).sum(1).reshape(b, s, h)
            p = _leaky(hidden_states @ sw_gate) * (hidden_states @ sw_up) @ sw_down
            y = y + p
            num = jnp.sum(y * p, -1)
            den = jnp.maximum(jnp.linalg.norm(y, axis=-1), EPS_COS) * jnp.maximum(jnp.linalg.norm(p, axis=-1), EPS_COS)
            closs = CONS_ALPHA * jnp.mean(num / den / (1.0 + COS_TEMP))
            return (y, aux_loss + closs)
        y, _ = _moe_forward(hidden_states, g, wt, wg, w_gate, w_up, w_down, sw_gate, sw_up, sw_down)
        return y

    def _L1_ffn_ref(hidden_states, ln1_weight, ln1_bias, ln2_weight, ln2_bias, qkv_weight, proj_weight, router_weight, moe_w1, moe_w2):
        import jax, jax.numpy as jnp
        import numpy as np
        EPS = 1e-05
        NUM_HEADS = 16
        NUM_KV_HEADS = 4
        NUM_EXPERTS = 8
        TOP_K = 2

        def _layernorm(x, w, b):
            mu = jnp.mean(x, axis=-1, keepdims=True)
            var = jnp.mean((x - mu) ** 2, axis=-1, keepdims=True)
            return (x - mu) * jax.lax.rsqrt(var + EPS) * w + b
        S, B, H = hidden_states.shape
        hd = H // NUM_HEADS
        rep = NUM_HEADS // NUM_KV_HEADS
        scale = 1.0 / hd ** 0.5
        ln1_out = _layernorm(hidden_states, ln1_weight, ln1_bias)
        qkv = jnp.einsum('sbh,oh->sbo', ln1_out, qkv_weight)
        q = qkv[..., :NUM_HEADS * hd].reshape(S, B, NUM_HEADS, hd)
        k = qkv[..., NUM_HEADS * hd:(NUM_HEADS + NUM_KV_HEADS) * hd].reshape(S, B, NUM_KV_HEADS, hd)
        v = qkv[..., (NUM_HEADS + NUM_KV_HEADS) * hd:].reshape(S, B, NUM_KV_HEADS, hd)
        k = jnp.repeat(k, rep, axis=2)
        v = jnp.repeat(v, rep, axis=2)
        scores = jnp.einsum('sbhd,tbhd->bhst', q, k) * scale
        causal = jnp.tril(jnp.ones((S, S), bool))
        scores = jnp.where(causal, scores, jnp.finfo(scores.dtype).min)
        probs = jax.nn.softmax(scores, axis=-1)
        attn = jnp.einsum('bhst,tbhd->sbhd', probs, v).reshape(S, B, H)
        proj_out = jnp.einsum('sbh,oh->sbo', attn, proj_weight)
        hidden_after_attn = hidden_states + proj_out
        ln2_out = _layernorm(hidden_after_attn, ln2_weight, ln2_bias)
        x = ln2_out.reshape(-1, H)
        logits = jnp.einsum('th,eh->te', x, router_weight)
        gate = jax.nn.softmax(logits, axis=-1)
        top_probs, top_idx = jax.lax.top_k(gate, TOP_K)
        h_mid = jax.nn.gelu(jnp.einsum('th,ehf->etf', x, moe_w1))
        expert_out = jnp.einsum('etf,efh->eth', h_mid, moe_w2)
        e_ids = jnp.arange(NUM_EXPERTS)[:, None, None]
        weights = jnp.sum(jnp.where(top_idx[None] == e_ids, top_probs[None], 0.0), axis=-1)
        moe_out = jnp.einsum('eth,et->th', expert_out, weights).reshape(S, B, H)
        return hidden_after_attn + moe_out
    x = x + _L0_ffn_ref(_L0_cond_ref(x, fside_16xSxS_0, mask_BxS_bk0, L0_cond_g_in, L0_cond_null_attn_bias, cond_64, L0_cond_Wq, L0_cond_Wkv, L0_cond_Wo, L0_cond_g_out), L0_ffn_weight)
    x = x + _L1_ffn_ref(_L1_cond_ref(x, cond_64, L1_cond_wt, L1_cond_wg, L1_cond_w_gate, L1_cond_w_up, L1_cond_w_down, L1_cond_sw_gate, L1_cond_sw_up, L1_cond_sw_down), L1_ffn_ln1_weight, L1_ffn_ln1_bias, L1_ffn_ln2_weight, L1_ffn_ln2_bias, L1_ffn_qkv_weight, L1_ffn_proj_weight, L1_ffn_router_weight, L1_ffn_moe_w1, L1_ffn_moe_w2)
    return x

_drawn_inputs = setup_inputs


def setup_inputs(seed=0):
    import zlib

    import numpy as np

    out = dict(_drawn_inputs(seed))
    spreads = {'L0_cond_g_in': (1.0, 0.2),
     'L0_cond_g_out': (1.0, 0.2),
     'L1_ffn_ln1_weight': (1.0, 0.6),
     'L1_ffn_ln1_bias': (0.0, 0.8),
     'L1_ffn_ln2_weight': (1.0, 0.6),
     'L1_ffn_ln2_bias': (0.0, 0.8)}
    factors = {'L1_ffn_router_weight': 3.886, 'L1_ffn_moe_w1': 3.487, 'L1_ffn_moe_w2': 3.36}
    for name, (base, spread) in spreads.items():
        noise = np.random.default_rng([zlib.crc32(name.encode()), seed]).standard_normal(out[name].shape)
        drawn = base * np.exp(spread * noise) if base else spread * noise
        out[name] = jnp.asarray(drawn.astype(out[name].dtype))
    for name, factor in factors.items():
        out[name] = (out[name] * factor).astype(out[name].dtype)
    return out
```

```python
import concourse.bass as bass
from concourse import mybir
from contextlib import ExitStack

F32 = mybir.dt.float32
F32R = mybir.dt.float32r
BF16 = mybir.dt.bfloat16
U8 = mybir.dt.uint8
ALU = mybir.AluOpType
ACT = mybir.ActivationFunctionType
AX = mybir.AxisListType

P = 128
B, S, D = 2, 1024, 256
T = B * S
NT = T // P
DC = D // P
H, DH = 16, 64
QT = S // P
PAIRS = H // 2
UNITS = 2 * QT * B
CW = 512
MASKED = 1.0e30
EPS = 1e-5
ROUND = 1.5 * 2 ** 23
E = 8
M1 = 128
EXPERTS = E + 2
LEAKY = 0.01
COND = 64
KV, HD = 4, 16
QKV = (H + 2 * KV) * HD
F2 = 512


class Steps:

    def __init__(self, per_body):
        self.per_body = per_body
        self.n = 0

    def up(self):
        self.n += 1
        return 1

    def here(self, it):
        return self.per_body * it + self.n


def flat(tiles):
    return tiles[:].rearrange("p t d -> p (t d)")


def gate_top_two(dve, step, steps, it, gate, scratch, weights):
    above, same, order, rank = scratch
    this = gate.unsqueeze(3).broadcast_to([P, 4, E, E])
    other = gate.unsqueeze(2).broadcast_to([P, 4, E, E])
    dve.tensor_tensor(above, other, this, ALU.is_gt)
    dve.tensor_tensor(same, other, this, ALU.is_equal).then_inc(step, steps.up())
    dve.wait_ge(step, steps.here(it))
    dve.tensor_tensor(same, same, order.unsqueeze(1).broadcast_to([P, 4, E, E]), ALU.mult).then_inc(step, steps.up())
    dve.wait_ge(step, steps.here(it))
    dve.tensor_tensor(above, above, same, ALU.add).then_inc(step, steps.up())
    dve.wait_ge(step, steps.here(it))
    dve.tensor_reduce(rank, above, AX.X, ALU.add).then_inc(step, steps.up())
    dve.wait_ge(step, steps.here(it))
    return dve.scalar_tensor_tensor(weights, rank, 1.5, gate, ALU.is_lt, ALU.mult)


def feed_forward_stage(nc, sbuf, psum, sem, aps, keep):
    xs, yacc, ident, ident_bf, xT_hi, xT_lo, gates, power4 = keep
    with ExitStack() as st:
        g_out = sbuf(st, "g_out", [P, D])
        w_raw = sbuf(st, "ff_w_raw", [P, DC, D])
        w_u = sbuf(st, "ff_w_u", [P, DC, D])
        w_ter = sbuf(st, "ff_w_ter", [P, DC, D], BF16)
        w_abs = sbuf(st, "ff_w_abs", [P, 1])
        w_scale = sbuf(st, "ff_w_scale", [P, 1])
        w_inv = sbuf(st, "ff_w_inv", [P, 1])
        w_scale127 = sbuf(st, "ff_w_scale127", [P, 1])
        ones = sbuf(st, "ff_ones", [P, P])
        cond_c = sbuf(st, "cond_c", [COND, B])
        cond_b = sbuf(st, "cond_b", [COND, B, P])
        wg = sbuf(st, "wg", [COND, E])
        wt = sbuf(st, "wt", [P, DC, E])
        order = sbuf(st, "ff_order", [P, E, E])
        half_cond = sbuf(st, "half_cond", [P, B, E])
        stats = [sbuf(st, f"ff_stats{r}", [P, 4, 6]) for r in range(2)]
        mv = [sbuf(st, f"ff_mv{r}", [P, 4, 2]) for r in range(2)]
        rstd = [sbuf(st, f"ff_rstd{r}", [P, 4]) for r in range(2)]
        yl = [sbuf(st, f"ff_yl{r}", [P, 4, D]) for r in range(2)]
        a_scale = [sbuf(st, f"a_scale{r}", [P, 4]) for r in range(2)]
        a_inv = [sbuf(st, f"a_inv{r}", [P, 4]) for r in range(2)]
        out_scale = [sbuf(st, f"out_scale{r}", [P, 4]) for r in range(2)]
        z = [sbuf(st, f"z{r}", [P, 4, D], BF16) for r in range(2)]
        zT = [sbuf(st, f"zT{r}", [P, DC, CW], BF16) for r in range(2)]
        x1 = [sbuf(st, f"x1_{r}", [P, 4, D]) for r in range(2)]
        x1T = [sbuf(st, f"x1T{r}", [P, DC, CW]) for r in range(2)]
        gate = [sbuf(st, f"ff_gate{r}", [P, 4, E]) for r in range(2)]
        top = [sbuf(st, f"ff_top{r}", [P, 4, E]) for r in range(2)]
        row = [sbuf(st, f"ff_row{r}", [P, 4]) for r in range(2)]
        above = sbuf(st, "ff_above", [P, 4, E, E])
        same = sbuf(st, "ff_same", [P, 4, E, E])
        rank = sbuf(st, "ff_rank", [P, 4, E])
        zT_ps = psum(st, "zT_ps", [P, DC, CW], BF16)
        f_ps = [psum(st, f"f_ps{r}", [P, 4, D]) for r in range(2)]
        x_ps = [psum(st, f"x_ps{c}", [P, CW]) for c in range(DC)]
        logits = [f_ps[r][:, 0, 0:4 * E].rearrange("p (t e) -> p t e", e=E) for r in range(2)]
        w_total = x_ps[0][:, 0:1]
        cond_ps = x_ps[1][:, 0:B * E].rearrange("p (b e) -> p b e", e=E)

        loaded, step, ones_set = sem("ff_loaded"), sem("ff_step"), sem("ff_ones_set")
        w_abs_ready, totals_ready, w_ready, cond_ready = (sem(f"ff_{n}") for n in ("w_abs_ready", "totals_ready", "w_ready", "cond_ready"))
        var_ready, rstd_ready, z_ready, z_turned, zT_ready, f_ready = (
            sem(f"ff_{n}") for n in ("var_ready", "rstd_ready", "z_ready", "z_turned", "zT_ready", "f_ready"))
        x1_ready, x1_turned, x1T_ready, xs_ready, hi_ready, lo_ready = (
            sem(f"ff_{n}") for n in ("x1_ready", "x1_turned", "x1T_ready", "xs_ready", "hi_ready", "lo_ready"))
        logits_ready, logits_read, exp_ready = (sem(f"ff_{n}") for n in ("logits_ready", "logits_read", "exp_ready"))
        marks = sem("ff_marks")
        LOADS = 16 * 6
        SETUP, PER_BODY = 5, 46
        xs_f, yacc_f = flat(xs), flat(yacc)

        def tile(it, r, t):
            return bass.ds(D * (QT * it + 4 * r + t), D)

        with nc.Block() as block:
            @block.sync
            def _(sp):
                sp.dma_start(w_raw[:], aps["ffT"].rearrange("(c p) o -> p c o", p=P)).then_inc(loaded, 16)
                sp.dma_start(g_out[:], aps["g_out"].broadcast_to([P, D])).then_inc(loaded, 16)
                sp.dma_start(wt[:], aps["wtT"].rearrange("(c p) e -> p c e", p=P)).then_inc(loaded, 16)
                sp.dma_start(wg[:], aps["wgT"]).then_inc(loaded, 16)
                sp.dma_start(cond_c[:], aps["condT"]).then_inc(loaded, 16)
                sp.dma_start(order[:], aps["order"].broadcast_to([P, E * E])).then_inc(loaded, 16)

            @block.gpsimd
            def _(pool):
                pool.memset(ones[:], 1.0).then_inc(ones_set, 1)
                with pool.Fori(0, B) as it:
                    for r in range(2):
                        pool.wait_ge(var_ready, 2 * it + r + 1)
                        pool.tensor_tensor(rstd[r][:], rstd[r][:], power4, ALU.pow).then_inc(rstd_ready, 1)

            @block.vector
            def _(dve):
                dve.wait_ge(loaded, LOADS)
                dve.tensor_reduce(w_abs[:], w_raw[:].rearrange("p c o -> p (c o)"), AX.X, ALU.add,
                                  apply_absolute_value=True).then_inc(w_abs_ready, 1)
                for b in range(B):
                    last = dve.tensor_copy(cond_b[:, b, :], cond_c[:, b:b + 1].broadcast_to([COND, P]))
                last.then_inc(cond_ready, 1)
                dve.wait_ge(totals_ready, 1)
                dve.tensor_scalar(w_scale[:], w_total, 1.0 / (D * D), 1e-8, ALU.mult, ALU.add).then_inc(step, 1)
                dve.wait_ge(step, 1)
                dve.reciprocal(w_inv[:], w_scale[:]).then_inc(step, 1)
                dve.wait_ge(step, 2)
                dve.tensor_scalar(w_u[:], w_raw[:], w_inv[:, 0:1], None, ALU.mult)
                dve.tensor_scalar(w_scale127[:], w_scale[:], 1.0 / 127.0, None, ALU.mult).then_inc(step, 1)
                dve.wait_ge(step, 3)
                dve.tensor_scalar(w_u[:], w_u[:], ROUND, ROUND, ALU.add, ALU.subtract).then_inc(step, 1)
                dve.wait_ge(step, 4)
                dve.tensor_scalar(w_ter[:], w_u[:], 1.0, -1.0, ALU.min, ALU.max).then_inc(w_ready, 1)
                dve.wait_ge(totals_ready, 2)
                dve.tensor_scalar(half_cond[:], cond_ps, 0.5, None, ALU.mult).then_inc(step, 1)
                dve.wait_ge(step, 5)

                with dve.Fori(0, B) as it:
                    steps = Steps(PER_BODY)
                    steps.n = SETUP
                    dve.wait_ge(exp_ready, 2 * it + 1)
                    for r in range(2):
                        for t in range(4):
                            last = dve.bn_stats(stats[r][:, t, :], yacc_f[:, tile(it, r, t)])
                        last.then_inc(step, steps.up())
                        dve.wait_ge(step, steps.here(it))
                        apart(dve, marks)
                        for t in range(4):
                            last = dve.bn_aggr(mv[r][:, t, :], stats[r][:, t, :])
                        last.then_inc(step, steps.up())
                        dve.wait_ge(step, steps.here(it))
                        dve.tensor_scalar(rstd[r][:], mv[r][:, :, 1], EPS, None, ALU.add).then_inc(var_ready, 1)
                    for r in range(2):
                        dve.wait_ge(rstd_ready, 2 * it + r + 1)
                        for t in range(4):
                            last = dve.tensor_scalar(yl[r][:, t, :], yacc_f[:, tile(it, r, t)], mv[r][:, t, 0:1],
                                                     rstd[r][:, t:t + 1], ALU.subtract, ALU.mult)
                        last.then_inc(step, steps.up())
                        dve.wait_ge(step, steps.here(it))
                        dve.tensor_tensor(yl[r][:], yl[r][:], g_out[:].unsqueeze(1).broadcast_to([P, 4, D]),
                                          ALU.mult).then_inc(step, steps.up())
                        dve.wait_ge(step, steps.here(it))
                        dve.tensor_reduce(a_scale[r][:], yl[r][:], AX.X, ALU.max, apply_absolute_value=True).then_inc(step, steps.up())
                        dve.wait_ge(step, steps.here(it))
                        dve.tensor_scalar(a_scale[r][:], a_scale[r][:], 1e-8, None, ALU.add).then_inc(step, steps.up())
                        dve.wait_ge(step, steps.here(it))
                        dve.tensor_scalar(out_scale[r][:], a_scale[r][:], w_scale127[:, 0:1], None, ALU.mult)
                        dve.reciprocal(a_inv[r][:], a_scale[r][:]).then_inc(step, steps.up())
                        dve.wait_ge(step, steps.here(it))
                        for t in range(4):
                            last = dve.tensor_scalar(yl[r][:, t, :], yl[r][:, t, :], a_inv[r][:, t:t + 1], 127.0,
                                                     ALU.mult, ALU.mult)
                        last.then_inc(step, steps.up())
                        dve.wait_ge(step, steps.here(it))
                        dve.tensor_scalar(yl[r][:], yl[r][:], 127.0, -128.0, ALU.min, ALU.max).then_inc(step, steps.up())
                        dve.wait_ge(step, steps.here(it))
                        dve.tensor_scalar(z[r][:], yl[r][:], ROUND, ROUND, ALU.add, ALU.subtract).then_inc(z_ready, 1)
                    for r in range(2):
                        dve.wait_ge(f_ready, 2 * it + r + 1)
                        for t in range(4):
                            last = dve.scalar_tensor_tensor(x1[r][:, t, :], f_ps[r][:, t, :], out_scale[r][:, t:t + 1],
                                                            xs_f[:, tile(it, r, t)], ALU.mult, ALU.add)
                        last.then_inc(x1_ready, 1)
                    for r in range(2):
                        for c in range(DC):
                            dve.wait_ge(hi_ready, 2 * DC * it + DC * r + c + 1)
                            cols = bass.ds(2 * CW * it + CW * r, CW)
                            last = dve.tensor_tensor(xT_lo[:, c, cols], x1T[r][:, c, :], xT_hi[:, c, cols].bitcast(F32), ALU.subtract)
                        last.then_inc(lo_ready, 1)
                    for r in range(2):
                        dve.wait_ge(logits_ready, 2 * it + r + 1)
                        dve.scalar_tensor_tensor(gate[r][:], logits[r], 0.5,
                                                 half_cond[:, bass.ds(it, 1), :].broadcast_to([P, 4, E]),
                                                 ALU.mult, ALU.add).then_inc(step, steps.up())
                        dve.wait_ge(step, steps.here(it))
                        dve.tensor_reduce(row[r][:], gate[r][:], AX.X, ALU.max).then_inc(step, steps.up())
                        dve.wait_ge(step, steps.here(it))
                        dve.tensor_tensor(gate[r][:], gate[r][:], row[r][:].unsqueeze(2).broadcast_to([P, 4, E]),
                                          ALU.subtract).then_inc(logits_read, 1)
                    for r in range(2):
                        dve.wait_ge(exp_ready, 2 * it + r + 2)
                        dve.tensor_reduce(row[r][:], gate[r][:], AX.X, ALU.add).then_inc(step, steps.up())
                        dve.wait_ge(step, steps.here(it))
                        dve.reciprocal(row[r][:], row[r][:]).then_inc(step, steps.up())
                        dve.wait_ge(step, steps.here(it))
                        dve.tensor_tensor(gate[r][:], gate[r][:], row[r][:].unsqueeze(2).broadcast_to([P, 4, E]),
                                          ALU.mult).then_inc(step, steps.up())
                        dve.wait_ge(step, steps.here(it))
                        gate_top_two(dve, step, steps, it, gate[r][:], (above[:], same[:], order[:], rank[:]), top[r][:]
                                     ).then_inc(step, steps.up())
                        dve.wait_ge(step, steps.here(it))
                        dve.tensor_reduce(row[r][:], top[r][:], AX.X, ALU.add).then_inc(step, steps.up())
                        dve.wait_ge(step, steps.here(it))
                        dve.tensor_scalar(row[r][:], row[r][:], 1e-20, None, ALU.add).then_inc(step, steps.up())
                        dve.wait_ge(step, steps.here(it))
                        dve.reciprocal(row[r][:], row[r][:]).then_inc(step, steps.up())
                        dve.wait_ge(step, steps.here(it))
                        dve.tensor_tensor(gates[:, bass.ds(QT * it + 4 * r, 4), 0:E], top[r][:],
                                          row[r][:].unsqueeze(2).broadcast_to([P, 4, E]), ALU.mult).then_inc(step, steps.up())
                    assert steps.n == SETUP + PER_BODY, steps.n - SETUP
                dve.memset(gates[:, :, E:EXPERTS], 1.0)

            @block.scalar
            def _(act):
                act.wait_ge(loaded, LOADS)
                act.sem_inc(exp_ready, 1)
                with act.Fori(0, B) as it:
                    for r in range(2):
                        act.wait_ge(z_turned, 2 * it + r + 1)
                        act.activation(zT[r][:], zT_ps[:], ACT.Copy).then_inc(zT_ready, 1)
                    for r in range(2):
                        for c in range(DC):
                            act.wait_ge(x1_turned, 2 * DC * it + DC * r + c + 1)
                            act.activation(x1T[r][:, c, :], x_ps[c][:], ACT.Copy).then_inc(x1T_ready, 1)
                        for c in range(DC):
                            act.wait_ge(x1T_ready, 2 * DC * it + DC * r + c + 1)
                            act.activation(xT_hi[:, c, bass.ds(2 * CW * it + CW * r, CW)], x1T[r][:, c, :],
                                           ACT.Copy).then_inc(hi_ready, 1)
                        act.wait_ge(x1_ready, 2 * it + r + 1)
                        act.activation(xs_f[:, bass.ds(D * (QT * it + 4 * r), 4 * D)], flat(x1[r]), ACT.Copy).then_inc(xs_ready, 1)
                    for r in range(2):
                        act.wait_ge(logits_read, 2 * it + r + 1)
                        act.activation(gate[r][:], gate[r][:], ACT.Exp).then_inc(exp_ready, 1)

            @block.tensor
            def _(pe):
                pe.wait_ge(ones_set, 1)
                pe.wait_ge(w_abs_ready, 1)
                pe.matmul(w_total, ones[:], w_abs[:], start=True, stop=True).then_inc(totals_ready, 1)
                pe.wait_ge(cond_ready, 1)
                for b in range(B):
                    last = pe.matmul(cond_ps[:, b, :], cond_b[:, b, :], wg[:], start=True, stop=True)
                last.then_inc(totals_ready, 1)
                pe.wait_ge(w_ready, 1)
                with pe.Fori(0, B) as it:
                    for r in range(2):
                        pe.wait_ge(z_ready, 2 * it + r + 1)
                        if r:
                            pe.wait_ge(zT_ready, 2 * it + r)
                        for c in range(DC):
                            for t in range(4):
                                last = pe.transpose(zT_ps[:, c, P * t:P * t + P], z[r][:, t, P * c:P * c + P], ident_bf)
                        last.then_inc(z_turned, 1)
                    for r in range(2):
                        pe.wait_ge(zT_ready, 2 * it + r + 1)
                        for t in range(4):
                            for c in range(DC):
                                last = pe.matmul(f_ps[r][:, t, :], zT[r][:, c, P * t:P * t + P], w_ter[:, c, :],
                                                 start=(c == 0), stop=(c == DC - 1))
                        last.then_inc(f_ready, 1)
                    for r in range(2):
                        pe.wait_ge(x1_ready, 2 * it + r + 1)
                        for c in range(DC):
                            if r:
                                pe.wait_ge(x1T_ready, 2 * DC * it + c + 1)
                            for t in range(4):
                                last = pe.transpose(x_ps[c][:, P * t:P * t + P], x1[r][:, t, P * c:P * c + P], ident)
                            last.then_inc(x1_turned, 1)
                    for r in range(2):
                        pe.wait_ge(x1T_ready, 2 * DC * it + DC * (r + 1))
                        for t in range(4):
                            for c in range(DC):
                                last = pe.matmul(logits[r][:, t, :], x1T[r][:, c, P * t:P * t + P], wt[:, c, :],
                                                 start=(c == 0), stop=(c == DC - 1))
                        last.then_inc(logits_ready, 1)


def first_mixture_stage(nc, sbuf, psum, sem, aps, keep):
    yacc, xT_hi, xT_lo, gates = keep
    GU = 2 * M1
    WCOLS = DC * GU + D
    LAST = EXPERTS // 2 - 1
    with ExitStack() as st:
        w_raw = [sbuf(st, f"m1_raw{i}", [P, WCOLS]) for i in range(2)]
        w_hi = [sbuf(st, f"m1_hi{i}", [P, WCOLS], F32R) for i in range(2)]
        w_lo = [sbuf(st, f"m1_lo{i}", [P, WCOLS], F32R) for i in range(2)]
        slope = sbuf(st, "m1_slope", [P, CW])
        leaky = sbuf(st, "m1_leaky", [P, CW])
        h = [sbuf(st, f"m1_h{i}", [P, CW]) for i in range(2)]
        h_hi = [sbuf(st, f"m1_h_hi{i}", [P, CW], F32R) for i in range(2)]
        h_lo = [sbuf(st, f"m1_h_lo{i}", [P, CW], F32R) for i in range(2)]
        g_ps = [psum(st, f"m1_g_ps{i}", [P, CW]) for i in range(2)]
        u_ps = [psum(st, f"m1_u_ps{i}", [P, CW]) for i in range(2)]
        o_ps = [psum(st, f"m1_o_ps{i}", [P, 4, D]) for i in range(2)]
        w_in = [sem(f"m1_w_in{i}") for i in range(2)]
        w_hi_ready, w_lo_ready = sem("m1_w_hi_ready"), sem("m1_w_lo_ready")
        up_ready, slope_ready, leaky_ready, h_ready, h_hi_ready, h_lo_ready = (
            sem(f"m1_{n}") for n in ("up_ready", "slope_ready", "leaky_ready", "h_ready", "h_hi_ready", "h_lo_ready"))
        down_ready, added = sem("m1_down_ready"), sem("m1_added")
        STEPS = 8

        def experts(eng, body):
            with eng.Fori(0, LAST) as ep:
                body(ep)
            body(LAST)

        def final(ep):
            return isinstance(ep, int) and ep == LAST

        with nc.Block() as block:
            @block.sync
            def _(sp):
                sp.dma_start(w_raw[0][:], aps["m1_w"][0]).then_inc(w_in[0], 16)

                def body(ep):
                    for i in range(2):
                        if i and final(ep):
                            continue
                        e = 2 * ep + 1 + i
                        sp.wait_ge(w_lo_ready, 2 * ep + 1)
                        sp.dma_start(w_raw[1 - i][:], aps["m1_w"][e]).then_inc(w_in[1 - i], 16)
                experts(sp, body)

            @block.scalar
            def _(act):
                def split(i, loads, steps_done):
                    act.wait_ge(w_in[i], 16 * loads)
                    wait(act, down_ready, steps_done)
                    act.activation(w_hi[i][:], w_raw[i][:], ACT.Copy).then_inc(w_hi_ready, 1)

                def slopes(j, i):
                    act.wait_ge(up_ready, j + 1)
                    wait(act, leaky_ready, j)
                    act.activation(slope[:], g_ps[i][:], ACT.Copy, scale=LEAKY).then_inc(slope_ready, 1)

                split(0, 1, 0)
                slopes(0, 0)
                act.wait_ge(h_ready, 1)
                act.activation(h_hi[0][:], h[0][:], ACT.Copy).then_inc(h_hi_ready, 1)

                def body(ep):
                    for s in range(STEPS):
                        if s == 1:
                            split(1, ep + 1, STEPS * ep + 1)
                        if s == 5 and not final(ep):
                            split(0, ep + 2, STEPS * ep + 4)
                        if s == STEPS - 1 and final(ep):
                            continue
                        j = STEPS * ep + s + 1
                        slopes(j, (s + 1) % 2)
                        act.wait_ge(down_ready, STEPS * ep + max(s, 1))
                        act.wait_ge(h_ready, j + 1)
                        act.activation(h_hi[(s + 1) % 2][:], h[(s + 1) % 2][:], ACT.Copy).then_inc(h_hi_ready, 1)
                experts(act, body)

            @block.vector
            def _(dve):
                def split(i, n):
                    dve.wait_ge(w_hi_ready, n)
                    dve.tensor_tensor(w_lo[i][:], w_raw[i][:], w_hi[i][:].bitcast(F32), ALU.subtract).then_inc(w_lo_ready, 1)

                def hidden(j, i):
                    dve.wait_ge(slope_ready, j + 1)
                    dve.tensor_tensor(leaky[:], slope[:], g_ps[i][:], ALU.max).then_inc(leaky_ready, 1)
                    dve.wait_ge(leaky_ready, j + 1)
                    dve.tensor_tensor(h[i][:], leaky[:], u_ps[i][:], ALU.mult).then_inc(h_ready, 1)

                def low(j, i):
                    dve.wait_ge(h_hi_ready, j + 1)
                    dve.tensor_tensor(h_lo[i][:], h[i][:], h_hi[i][:].bitcast(F32), ALU.subtract).then_inc(h_lo_ready, 1)

                dve.memset(yacc[:], 0.0).then_inc(added, 2)
                split(0, 1)
                hidden(0, 0)
                low(0, 0)

                def body(ep):
                    for s in range(STEPS):
                        if s == 1:
                            split(1, 2 * ep + 2)
                        if s == 5 and not final(ep):
                            split(0, 2 * ep + 3)
                        more = not (s == STEPS - 1 and final(ep))
                        if more:
                            hidden(STEPS * ep + s + 1, (s + 1) % 2)
                        dve.wait_ge(added, STEPS * ep + max(s - 1, 2))
                        dve.wait_ge(down_ready, STEPS * ep + s + 1)
                        for t in range(4):
                            n = 4 * (s % 4) + t
                            last = dve.scalar_tensor_tensor(yacc[:, n, :], o_ps[s % 2][:, t, :], gates[:, n, bass.ds(2 * ep + s // 4, 1)],
                                                            yacc[:, n, :], ALU.mult, ALU.add)
                        last.then_inc(added, 1)
                        if more:
                            low(STEPS * ep + s + 1, (s + 1) % 2)
                experts(dve, body)

            @block.tensor
            def _(pe):
                def up(j, e, s):
                    i, x = (s // 4) % 2, slice(CW * (s % 4), CW * (s % 4) + CW)
                    pe.wait_ge(w_lo_ready, e + 1)
                    for ps, first in ((g_ps[s % 2], 0), (u_ps[s % 2], M1)):
                        for c in range(DC):
                            cols = slice(GU * c + first, GU * c + first + M1)
                            pe.matmul(ps[:], w_hi[i][:, cols], xT_hi[:, c, x], start=(c == 0), stop=False)
                            pe.matmul(ps[:], w_hi[i][:, cols], xT_lo[:, c, x], start=False, stop=False)
                            last = pe.matmul(ps[:], w_lo[i][:, cols], xT_hi[:, c, x], start=False, stop=(c == DC - 1))
                    last.then_inc(up_ready, 1)

                def down(j, s):
                    i = s // 4
                    cols = slice(DC * GU, WCOLS)
                    pe.wait_ge(added, j + 1)
                    pe.wait_ge(h_lo_ready, j + 1)
                    for t in range(4):
                        rows = slice(P * t, P * t + P)
                        pe.matmul(o_ps[s % 2][:, t, :], h_hi[s % 2][:, rows], w_hi[i][:, cols], start=True, stop=False)
                        pe.matmul(o_ps[s % 2][:, t, :], h_hi[s % 2][:, rows], w_lo[i][:, cols], start=False, stop=False)
                        last = pe.matmul(o_ps[s % 2][:, t, :], h_lo[s % 2][:, rows], w_hi[i][:, cols], start=False, stop=True)
                    last.then_inc(down_ready, 1)

                up(0, 0, 0)

                def body(ep):
                    for s in range(STEPS):
                        j = STEPS * ep + s
                        if not (s == STEPS - 1 and final(ep)):
                            up(j + 1, 2 * ep + (s + 1) // 4, s + 1)
                        down(j, s)
                experts(pe, body)


def pair_attention_stage(nc, sbuf, psum, sem, aps, keep):
    xs, yacc, ident, xT_hi, xT_lo, gates, power4 = keep
    with ExitStack() as st:
        ln_w = [sbuf(st, f"ln{i}_w", [P, DC]) for i in (1, 2)]
        ln_b = [sbuf(st, f"ln{i}_b", [P, DC]) for i in (1, 2)]
        w_qkv = sbuf(st, "w_qkv", [P, DC, QKV])
        w_proj = sbuf(st, "w_proj", [P, DC, D])
        w_router = sbuf(st, "w_router", [P, DC, E])
        order = sbuf(st, "pa_order", [P, E, E])
        stats = [sbuf(st, f"pa_stats{r}", [P, 4, 6]) for r in range(2)]
        mv = [sbuf(st, f"pa_mv{r}", [P, 4, 2]) for r in range(2)]
        rstd = [sbuf(st, f"pa_rstd{r}", [P, 4]) for r in range(2)]
        xh = [sbuf(st, f"pa_xh{r}", [P, 4, D]) for r in range(2)]
        lT = [sbuf(st, f"pa_lT{r}", [P, DC, CW]) for r in range(2)]
        qkv_sb = [sbuf(st, f"pa_qkv{r}", [P, 4, QKV]) for r in range(2)]
        prod = sbuf(st, "pa_prod", [P, 2, 2, H, HD])
        score = [sbuf(st, f"pa_score{r}", [P, 2, 2, H]) for r in range(2)]
        peak = [sbuf(st, f"pa_peak{r}", [P, 2, H]) for r in range(2)]
        attn = [sbuf(st, f"pa_attn{r}", [P, 4, D]) for r in range(2)]
        attnT = [sbuf(st, f"pa_attnT{r}", [P, DC, CW]) for r in range(2)]
        ha = [sbuf(st, f"pa_ha{r}", [P, 4, D]) for r in range(2)]
        gate = [sbuf(st, f"pa_gate{r}", [P, 4, E]) for r in range(2)]
        row = [sbuf(st, f"pa_row{r}", [P, 4]) for r in range(2)]
        above = sbuf(st, "pa_above", [P, 4, E, E])
        same = sbuf(st, "pa_same", [P, 4, E, E])
        rank = sbuf(st, "pa_rank", [P, 4, E])
        x_ps = [psum(st, f"pa_x_ps{c}", [P, CW]) for c in range(DC)]
        q_ps = [psum(st, f"pa_q_ps{j}", [P, CW]) for j in range(4)]
        p_ps = psum(st, "pa_p_ps", [P, 4, D])
        logits = [p_ps[:, 2 * r, 0:4 * E].rearrange("p (j e) -> p j e", e=E) for r in range(2)]
        names = ("loaded step var_ready rstd_ready xh_ready turned lT_ready qkv_ready qkv_read prod_ready first_ready scores_ready "
                 "exp_ready attn_ready attnT_ready proj_ready ha_ready summed hi_ready lo_ready logits_ready logits_read gate_exp_ready").split()
        (loaded, step, var_ready, rstd_ready, xh_ready, turned, lT_ready, qkv_ready, qkv_read, prod_ready, first_ready, scores_ready,
         exp_ready, attn_ready, attnT_ready, proj_ready, ha_ready, summed, hi_ready, lo_ready, logits_ready, logits_read,
         gate_exp_ready) = (sem("pa_" + n) for n in names)
        marks = sem("pa_marks")
        LOADS = 16 * 8
        PER_BODY = 38
        POS = QT // 4

        def group_tiles(tiles, it, r):
            return tiles[:].rearrange("p (b i) d -> p b i d", b=B)[:, :, bass.ds(4 * it + 2 * r, 2), :]

        def tile(it, r, j):
            return bass.ds(D * (4 * it + QT * (j // 2) + 2 * r + j % 2), D)

        def heads(ap):
            return ap.rearrange("p (k d) -> p k d", d=HD).unsqueeze(2).broadcast_to([P, KV, H // KV, HD])

        def by_kv(ap):
            return ap.rearrange("p (k r d) -> p k r d", k=KV, d=HD)

        def per_head(ap):
            return ap.rearrange("p (k r) -> p k r", k=KV).unsqueeze(3).broadcast_to([P, KV, H // KV, HD])

        def qkv(r, b, i, part):
            first, last = ((0, D), (D, D + KV * HD), (D + KV * HD, QKV))[part]
            return qkv_sb[r][:, 2 * b + i, first:last]

        with nc.Block() as block:
            @block.sync
            def _(sp):
                for i in range(2):
                    sp.dma_start(ln_w[i][:], aps[f"ln{i + 1}_w"]).then_inc(loaded, 16)
                    sp.dma_start(ln_b[i][:], aps[f"ln{i + 1}_b"]).then_inc(loaded, 16)
                sp.dma_start(w_qkv[:], aps["qkvT"].rearrange("(c p) o -> p c o", p=P)).then_inc(loaded, 16)
                sp.dma_start(w_proj[:], aps["projT"].rearrange("(c p) o -> p c o", p=P)).then_inc(loaded, 16)
                sp.dma_start(w_router[:], aps["routerT"].rearrange("(c p) e -> p c e", p=P)).then_inc(loaded, 16)
                sp.dma_start(order[:], aps["order"].broadcast_to([P, E * E])).then_inc(loaded, 16)

            @block.gpsimd
            def _(pool):
                pool.sem_inc(summed, 1)
                with pool.Fori(0, POS) as it:
                    for norm in range(2):
                        for r in range(2):
                            pool.wait_ge(var_ready, 4 * it + 2 * norm + r + 1)
                            pool.tensor_tensor(rstd[r][:], rstd[r][:], power4, ALU.pow).then_inc(rstd_ready, 1)
                    for r in range(2):
                        pool.wait_ge(ha_ready, 2 * it + r + 1)
                        pool.tensor_tensor(group_tiles(xs, it, r), group_tiles(xs, it, r),
                                           ha[r][:].rearrange("p (b i) d -> p b i d", b=B), ALU.add).then_inc(summed, 1)

            @block.vector
            def _(dve):
                yacc_f = flat(yacc)
                dve.wait_ge(loaded, LOADS)
                with dve.Fori(0, POS) as it:
                    steps = Steps(PER_BODY)
                    dve.wait_ge(gate_exp_ready, 2 * it + 1)
                    dve.wait_ge(summed, 2 * it + 1)

                    def moments(source, r):
                        for j in range(4):
                            last = dve.bn_stats(stats[r][:, j, :], source(j))
                        last.then_inc(step, steps.up())
                        dve.wait_ge(step, steps.here(it))
                        apart(dve, marks)
                        for j in range(4):
                            last = dve.bn_aggr(mv[r][:, j, :], stats[r][:, j, :])
                        last.then_inc(step, steps.up())
                        dve.wait_ge(step, steps.here(it))
                        dve.tensor_scalar(rstd[r][:], mv[r][:, :, 1], EPS, None, ALU.add).then_inc(var_ready, 1)

                    def normalise(source, r, norm):
                        dve.wait_ge(rstd_ready, 4 * it + 2 * norm + r + 1)
                        for j in range(4):
                            last = dve.tensor_scalar(xh[r][:, j, :], source(j), mv[r][:, j, 0:1], rstd[r][:, j:j + 1],
                                                     ALU.subtract, ALU.mult)
                        last.then_inc(xh_ready, 1)

                    for r in range(2):
                        moments(lambda j: yacc_f[:, tile(it, r, j)], r)
                    for r in range(2):
                        normalise(lambda j: yacc_f[:, tile(it, r, j)], r, 0)
                    for r in range(2):
                        if r:
                            dve.wait_ge(attn_ready, 2 * it + r)
                        dve.wait_ge(qkv_read, 2 * it + r + 1)
                        for i in range(2):
                            for b in range(B):
                                last = dve.tensor_tensor(prod[:, i, b].rearrange("p (k r) d -> p k r d", k=KV),
                                                         by_kv(qkv(r, 1, i, 0)), heads(qkv(r, b, i, 1)), ALU.mult)
                        last.then_inc(step, steps.up())
                        dve.wait_ge(step, steps.here(it))
                        dve.tensor_reduce(score[r][:], prod[:], AX.X, ALU.add).then_inc(step, steps.up())
                        dve.wait_ge(step, steps.here(it))
                        dve.tensor_tensor(peak[r][:], score[r][:, :, 0, :], score[r][:, :, 1, :], ALU.max).then_inc(step, steps.up())
                        dve.wait_ge(step, steps.here(it))
                        dve.tensor_tensor(score[r][:], score[r][:], peak[r][:].unsqueeze(2).broadcast_to([P, 2, 2, H]),
                                          ALU.subtract).then_inc(scores_ready, 1)
                        dve.wait_ge(exp_ready, 2 * it + r + 1)
                        dve.tensor_tensor(peak[r][:], score[r][:, :, 0, :], score[r][:, :, 1, :], ALU.add).then_inc(step, steps.up())
                        dve.wait_ge(step, steps.here(it))
                        dve.reciprocal(peak[r][:], peak[r][:]).then_inc(step, steps.up())
                        dve.wait_ge(step, steps.here(it))
                        dve.tensor_tensor(score[r][:], score[r][:], peak[r][:].unsqueeze(2).broadcast_to([P, 2, 2, H]),
                                          ALU.mult).then_inc(step, steps.up())
                        dve.wait_ge(step, steps.here(it))
                        for i in range(2):
                            for b in range(B):
                                last = dve.tensor_tensor(prod[:, i, b].rearrange("p (k r) d -> p k r d", k=KV),
                                                         heads(qkv(r, b, i, 2)), per_head(score[r][:, i, b]), ALU.mult)
                        last.then_inc(prod_ready, 1)
                        dve.wait_ge(prod_ready, 2 * it + r + 1)
                        dve.tensor_tensor(attn[r][:, 2:4, :], prod[:, :, 0].rearrange("p i h d -> p i (h d)"),
                                          prod[:, :, 1].rearrange("p i h d -> p i (h d)"), ALU.add).then_inc(attn_ready, 1)
                    for r in range(2):
                        dve.wait_ge(proj_ready, 2 * it + r + 1)
                        dve.tensor_tensor(ha[r][:].rearrange("p (b i) d -> p b i d", b=B),
                                          p_ps[:].rearrange("p (b i) d -> p b i d", b=B),
                                          group_tiles(yacc, it, r), ALU.add).then_inc(ha_ready, 1)
                        dve.wait_ge(ha_ready, 2 * it + r + 1)
                        moments(lambda j: ha[r][:, j, :], r)
                    for r in range(2):
                        normalise(lambda j: ha[r][:, j, :], r, 1)
                    for r in range(2):
                        for c in range(DC):
                            dve.wait_ge(hi_ready, 2 * DC * it + DC * r + c + 1)
                            cols = bass.ds(2 * CW * it + CW * r, CW)
                            last = dve.tensor_tensor(xT_lo[:, c, cols], lT[r][:, c, :], xT_hi[:, c, cols].bitcast(F32), ALU.subtract)
                        last.then_inc(lo_ready, 1)
                    for r in range(2):
                        dve.wait_ge(logits_ready, 2 * it + r + 1)
                        dve.tensor_reduce(row[r][:], logits[r], AX.X, ALU.max).then_inc(step, steps.up())
                        dve.wait_ge(step, steps.here(it))
                        dve.tensor_tensor(gate[r][:], logits[r], row[r][:].unsqueeze(2).broadcast_to([P, 4, E]),
                                          ALU.subtract).then_inc(logits_read, 1)
                    for r in range(2):
                        dve.wait_ge(gate_exp_ready, 2 * it + r + 2)
                        dve.tensor_reduce(row[r][:], gate[r][:], AX.X, ALU.add).then_inc(step, steps.up())
                        dve.wait_ge(step, steps.here(it))
                        dve.reciprocal(row[r][:], row[r][:]).then_inc(step, steps.up())
                        dve.wait_ge(step, steps.here(it))
                        dve.tensor_tensor(gate[r][:], gate[r][:], row[r][:].unsqueeze(2).broadcast_to([P, 4, E]),
                                          ALU.mult).then_inc(step, steps.up())
                        dve.wait_ge(step, steps.here(it))
                        gate_top_two(dve, step, steps, it, gate[r][:], (above[:], same[:], order[:], rank[:]),
                                     gates[:, bass.ds(8 * it + 4 * r, 4), :]).then_inc(step, steps.up())
                    assert steps.n == PER_BODY, steps.n

            @block.scalar
            def _(act):
                act.wait_ge(loaded, LOADS)
                act.sem_inc(gate_exp_ready, 1)
                with act.Fori(0, POS) as it:
                    def evacuate(r, norm, out, n):
                        for c in range(DC):
                            act.wait_ge(turned, 6 * DC * it + n + DC * r + c + 1)
                            if norm is None:
                                act.activation(out[r][:, c, :], x_ps[c][:], ACT.Copy).then_inc(attnT_ready, 1)
                            else:
                                act.activation(out[r][:, c, :], x_ps[c][:], ACT.Identity, scale=ln_w[norm][:, c:c + 1],
                                               bias=ln_b[norm][:, c:c + 1]).then_inc(lT_ready, 1)

                    for r in range(2):
                        evacuate(r, 0, lT, 0)
                    for r in range(2):
                        act.wait_ge(qkv_ready, 2 * it + r + 1)
                        for j in range(4):
                            last = act.activation(qkv_sb[r][:, j, :], q_ps[j][:, 0:QKV], ACT.Copy)
                        last.then_inc(qkv_read, 1)
                        act.wait_ge(qkv_read, 2 * it + r + 1)
                        for i in range(2):
                            last = act.activation(by_kv(attn[r][:, i, :]), heads(qkv(r, 0, i, 2)), ACT.Copy)
                        last.then_inc(first_ready, 1)
                        act.wait_ge(scores_ready, 2 * it + r + 1)
                        act.activation(score[r][:], score[r][:], ACT.Exp, scale=HD ** -0.5).then_inc(exp_ready, 1)
                    for r in range(2):
                        evacuate(r, None, attnT, 2 * DC)
                    for r in range(2):
                        act.wait_ge(qkv_ready, 2 * it + 2)
                        evacuate(r, 1, lT, 4 * DC)
                        for c in range(DC):
                            act.wait_ge(lT_ready, 4 * DC * it + 2 * DC + DC * r + c + 1)
                            act.activation(xT_hi[:, c, bass.ds(2 * CW * it + CW * r, CW)], lT[r][:, c, :],
                                           ACT.Copy).then_inc(hi_ready, 1)
                    for r in range(2):
                        act.wait_ge(logits_read, 2 * it + r + 1)
                        act.activation(gate[r][:], gate[r][:], ACT.Exp).then_inc(gate_exp_ready, 1)

            @block.tensor
            def _(pe):
                pe.wait_ge(loaded, LOADS)
                with pe.Fori(0, POS) as it:
                    def turn(source, r, read):
                        for c in range(DC):
                            if read(c):
                                pe.wait_ge(*read(c))
                            for j in range(4):
                                last = pe.transpose(x_ps[c][:, P * j:P * j + P], source[r][:, j, P * c:P * c + P], ident)
                            last.then_inc(turned, 1)

                    for r in range(2):
                        pe.wait_ge(xh_ready, 4 * it + r + 1)
                        turn(xh, r, lambda c: (lT_ready, 4 * DC * it + c + 1) if r else None)
                    for r in range(2):
                        if r:
                            pe.wait_ge(qkv_read, 2 * it + r)
                        pe.wait_ge(lT_ready, 4 * DC * it + DC * (r + 1))
                        for j in range(4):
                            for c in range(DC):
                                last = pe.matmul(q_ps[j][:, 0:QKV], lT[r][:, c, P * j:P * j + P], w_qkv[:, c, :],
                                                 start=(c == 0), stop=(c == DC - 1))
                        last.then_inc(qkv_ready, 1)
                    for r in range(2):
                        pe.wait_ge(first_ready, 2 * it + r + 1)
                        pe.wait_ge(attn_ready, 2 * it + r + 1)
                        turn(attn, r, lambda c: (attnT_ready, 2 * DC * it + DC * (r - 1) + c + 1) if r else
                             (lT_ready, 4 * DC * it + DC + c + 1))
                    for r in range(2):
                        if r:
                            pe.wait_ge(ha_ready, 2 * it + r)
                        pe.wait_ge(attnT_ready, 2 * DC * it + DC * (r + 1))
                        for j in range(4):
                            for c in range(DC):
                                last = pe.matmul(p_ps[:, j, :], attnT[r][:, c, P * j:P * j + P], w_proj[:, c, :],
                                                 start=(c == 0), stop=(c == DC - 1))
                        last.then_inc(proj_ready, 1)
                    for r in range(2):
                        pe.wait_ge(xh_ready, 4 * it + 2 + r + 1)
                        turn(xh, r, lambda c: (lT_ready, 4 * DC * it + 2 * DC + c + 1) if r else
                             (attnT_ready, 2 * DC * it + DC + c + 1))
                    for r in range(2):
                        pe.wait_ge(lT_ready, 4 * DC * it + 2 * DC + DC * (r + 1))
                        for j in range(4):
                            for c in range(DC):
                                last = pe.matmul(logits[r][:, j, :], lT[r][:, c, P * j:P * j + P],
                                                 w_router[:, c, :], start=(c == 0), stop=(c == DC - 1))
                        last.then_inc(logits_ready, 1)


def second_mixture_stage(nc, sbuf, psum, sem, aps, keep):
    xs, xT_hi, xT_lo, gates, out = keep
    FC = F2 // P
    W1 = DC * F2
    WCOLS = W1 + FC * D
    LAST = E // 2 - 1
    STEPS = 8
    with ExitStack() as st:
        w_raw = [sbuf(st, f"m2_raw{i}", [P, WCOLS]) for i in range(2)]
        w_hi = [sbuf(st, f"m2_hi{i}", [P, WCOLS], F32R) for i in range(2)]
        w_lo = [sbuf(st, f"m2_lo{i}", [P, WCOLS], F32R) for i in range(2)]
        h = sbuf(st, "m2_h", [P, FC, CW])
        h_hi = [sbuf(st, f"m2_h_hi{i}", [P, FC, CW], F32R) for i in range(2)]
        h_lo = [sbuf(st, f"m2_h_lo{i}", [P, FC, CW], F32R) for i in range(2)]
        u_ps = [psum(st, f"m2_u_ps{f}", [P, CW]) for f in range(FC)]
        o_ps = [psum(st, f"m2_o_ps{i}", [P, 4, D]) for i in range(2)]
        w_in = [sem(f"m2_w_in{i}") for i in range(2)]
        w_hi_ready, w_lo_ready = sem("m2_w_hi_ready"), sem("m2_w_lo_ready")
        up_ready, h_ready, h_hi_ready, h_lo_ready = (sem(f"m2_{n}") for n in ("up_ready", "h_ready", "h_hi_ready", "h_lo_ready"))
        down_ready, added, stored = sem("m2_down_ready"), sem("m2_added"), sem("stored")

        def experts(eng, body):
            with eng.Fori(0, LAST) as ep:
                body(ep)
            body(LAST)

        def final(ep):
            return isinstance(ep, int) and ep == LAST

        with nc.Block() as block:
            @block.sync
            def _(sp):
                sp.dma_start(w_raw[0][:], aps["m2_w"][0]).then_inc(w_in[0], 16)

                def body(ep):
                    for i in range(2):
                        if i and final(ep):
                            continue
                        e = 2 * ep + 1 + i
                        sp.wait_ge(w_lo_ready, 2 * ep + 1)
                        sp.dma_start(w_raw[1 - i][:], aps["m2_w"][e]).then_inc(w_in[1 - i], 16)
                experts(sp, body)
                rows = out.rearrange("(b i p) d -> p b i d", b=B, p=P)
                for g in range(4):
                    sp.wait_ge(added, STEPS * LAST + 4 + g + 3)
                    for b in range(B):
                        sp.dma_start(rows[:, b, 2 * g:2 * g + 2, :],
                                     xs[:, QT * b + 2 * g:QT * b + 2 * g + 2, :]).then_inc(stored, 16)
                sp.wait_ge(stored, 16 * 4 * B)

            @block.scalar
            def _(act):
                def split(i, loads, steps_done):
                    act.wait_ge(w_in[i], 16 * loads)
                    wait(act, down_ready, steps_done)
                    act.activation(w_hi[i][:], w_raw[i][:], ACT.Copy).then_inc(w_hi_ready, 1)

                def hidden(j, i, multiplied):
                    for f in range(FC):
                        act.wait_ge(up_ready, FC * j + f + 1)
                        wait(act, h_lo_ready, FC * (j - 1) + f + 1)
                        act.activation(h[:, f, :], u_ps[f][:], ACT.Gelu_apprx_tanh).then_inc(h_ready, 1)
                        if f == 0:
                            wait(act, down_ready, multiplied)
                        act.wait_ge(h_ready, FC * j + f + 1)
                        act.activation(h_hi[i][:, f, :], h[:, f, :], ACT.Copy).then_inc(h_hi_ready, 1)

                split(0, 1, 0)
                hidden(0, 0, 0)

                def body(ep):
                    for s in range(STEPS):
                        if s == 1:
                            split(1, ep + 1, STEPS * ep + 1)
                        if s == 5 and not final(ep):
                            split(0, ep + 2, STEPS * ep + 4)
                        if not (s == STEPS - 1 and final(ep)):
                            hidden(STEPS * ep + s + 1, (s + 1) % 2, STEPS * ep + max(s, 1))
                experts(act, body)

            @block.vector
            def _(dve):
                def split(i, n):
                    dve.wait_ge(w_hi_ready, n)
                    dve.tensor_tensor(w_lo[i][:], w_raw[i][:], w_hi[i][:].bitcast(F32), ALU.subtract).then_inc(w_lo_ready, 1)

                def low(j, i):
                    for f in range(FC):
                        dve.wait_ge(h_hi_ready, FC * j + f + 1)
                        dve.tensor_tensor(h_lo[i][:, f, :], h[:, f, :], h_hi[i][:, f, :].bitcast(F32),
                                          ALU.subtract).then_inc(h_lo_ready, 1)

                split(0, 1)
                dve.sem_inc(added, 2)
                low(0, 0)

                def body(ep):
                    for s in range(STEPS):
                        if s == 1:
                            split(1, 2 * ep + 2)
                        if s == 5 and not final(ep):
                            split(0, 2 * ep + 3)
                        if not (s == STEPS - 1 and final(ep)):
                            low(STEPS * ep + s + 1, (s + 1) % 2)
                        dve.wait_ge(added, STEPS * ep + max(s - 1, 2))
                        dve.wait_ge(down_ready, STEPS * ep + s + 1)
                        for j in range(4):
                            g = s % 4
                            n = QT * (j // 2) + 2 * g + j % 2
                            last = dve.scalar_tensor_tensor(xs[:, n, :], o_ps[s % 2][:, j, :], gates[:, 4 * g + j, bass.ds(2 * ep + s // 4, 1)],
                                                            xs[:, n, :], ALU.mult, ALU.add)
                        last.then_inc(added, 1)
                experts(dve, body)

            @block.tensor
            def _(pe):
                def up(j, e, s):
                    i, x = (s // 4) % 2, slice(CW * (s % 4), CW * (s % 4) + CW)
                    pe.wait_ge(w_lo_ready, e + 1)
                    for f in range(FC):
                        wait(pe, h_ready, FC * (j - 1) + f + 1)
                        for c in range(DC):
                            cols = slice(F2 * c + P * f, F2 * c + P * f + P)
                            pe.matmul(u_ps[f][:], w_hi[i][:, cols], xT_hi[:, c, x], start=(c == 0), stop=False)
                            pe.matmul(u_ps[f][:], w_hi[i][:, cols], xT_lo[:, c, x], start=False, stop=False)
                            last = pe.matmul(u_ps[f][:], w_lo[i][:, cols], xT_hi[:, c, x], start=False, stop=(c == DC - 1))
                        last.then_inc(up_ready, 1)

                def down(j, s):
                    i = s // 4
                    pe.wait_ge(added, j + 1)
                    pe.wait_ge(h_lo_ready, FC * (j + 1))
                    for t in range(4):
                        rows = slice(P * t, P * t + P)
                        for f in range(FC):
                            cols = slice(W1 + D * f, W1 + D * f + D)
                            pe.matmul(o_ps[s % 2][:, t, :], h_hi[s % 2][:, f, rows], w_hi[i][:, cols], start=(f == 0), stop=False)
                            pe.matmul(o_ps[s % 2][:, t, :], h_hi[s % 2][:, f, rows], w_lo[i][:, cols], start=False, stop=False)
                            last = pe.matmul(o_ps[s % 2][:, t, :], h_lo[s % 2][:, f, rows], w_hi[i][:, cols],
                                             start=False, stop=(f == FC - 1))
                    last.then_inc(down_ready, 1)

                up(0, 0, 0)

                def body(ep):
                    for s in range(STEPS):
                        j = STEPS * ep + s
                        if not (s == STEPS - 1 and final(ep)):
                            up(j + 1, 2 * ep + (s + 1) // 4, s + 1)
                        down(j, s)
                experts(pe, body)


class Unit:

    def __init__(self, u):
        self.u = u
        self.head = u // (QT * B)
        self.row = u // B
        self.tile = QT - 1 - (u % (QT * B)) // B
        self.batch = u % B
        self.blocks = self.tile + 1
        self.chunks = [(c * 4, min(4, self.blocks - c * 4)) for c in range((self.blocks + 3) // 4)]


BODY = [Unit(u) for u in range(UNITS)]
FIRST_CHUNK = [sum(len(x.chunks) for x in BODY[:u]) for u in range(UNITS + 1)]
CHUNKS = FIRST_CHUNK[UNITS]
GROUPS = UNITS // 8


def apart(eng, marks):
    eng.sem_inc(marks, 1)


def wait(eng, sem, value):
    if isinstance(value, int) and value <= 0:
        return
    eng.wait_ge(sem, value)


def program(nc, x, bias, cond, mask, g_in, nab, Wq, Wkv, Wo, out, **aps):
    outer = ExitStack()
    with outer:
        def sbuf(stack, name, shape, dt=F32):
            return stack.enter_context(nc.sbuf_tensor(name, shape, dt))

        def psum(stack, name, shape, dt=F32):
            return stack.enter_context(nc.psum_tensor(name, shape, dt))

        def sem(name):
            return outer.enter_context(nc.semaphore(name))

        xs = sbuf(outer, "xs", [P, NT, D])
        ident = sbuf(outer, "ident", [P, P])
        yacc = sbuf(outer, "yacc", [P, NT, D])

        attn = ExitStack()
        xnT = sbuf(attn, "xnT", [P, DC, T])
        k_hi = sbuf(attn, "k_hi", [P, T + 2], F32R)
        k_lo = sbuf(attn, "k_lo", [P, T + 2], F32R)
        values = sbuf(attn, "values", [P, NT, DH])
        nv = sbuf(attn, "nv", [P, DH])
        nab_b = sbuf(attn, "nab_b", [P, H])

        with ExitStack() as st:
            xh = sbuf(st, "xh", [P, 4, 4, D])
            mv = sbuf(st, "mv", [P, NT, 2])
            stats = sbuf(st, "stats", [P, NT, 6])
            rstd = sbuf(st, "rstd", [P, NT])
            power = sbuf(st, "power", [P, 4])
            gcol = sbuf(st, "gcol", [P, DC])
            wk = sbuf(st, "wk", [P, DC, P])
            wv = sbuf(st, "wv", [P, DC, DH])
            nk = sbuf(st, "nk", [P, 1])
            mask8 = sbuf(st, "mask8", [P, T], U8)
            turn = [psum(st, f"turn{i}", [P, CW]) for i in range(2)]
            kps = [psum(st, f"kps{i}", [P, CW]) for i in range(2)]
            vps = [psum(st, f"vps{i}", [P, QT, DH]) for i in range(B)]
            x_in = [sem(f"x_in{g}") for g in range(4)]
            w_in, small_in = sem("w_in"), sem("small_in")
            const_ready, var_ready, rstd_ready = sem("const_ready"), sem("var_ready"), sem("rstd_ready")
            xh_ready, turned, xnT_ready = sem("xh_ready"), sem("turned"), sem("xnT_ready")
            k_ready, khi_ready, klo_ready, v_ready, v_out = (sem(n) for n in ("k_ready", "khi_ready", "klo_ready", "v_ready", "v_out"))
            step0 = sem("step0")
            zeroed = sem("zeroed")
            with nc.Block() as block:
                @block.sync
                def _(sp):
                    xt = x.rearrange("(t p) d -> p t d", p=P)
                    for g in range(4):
                        sp.dma_start(xs[:, 4 * g:4 * g + 4, :], xt[:, 4 * g:4 * g + 4, :]).then_inc(x_in[g], 16)
                    wkv = Wkv.rearrange("(c p) n -> p c n", p=P)
                    sp.dma_start(wk[:, :, 0:DH], wkv[:, :, 0:DH]).then_inc(w_in, 16)
                    sp.dma_start(wk[:, :, DH:P], wkv[:, :, 0:DH]).then_inc(w_in, 16)
                    sp.dma_start(wv[:], wkv[:, :, DH:2 * DH]).then_inc(w_in, 16)

                @block.scalar
                def _(act):
                    act.dma_start(gcol[:], g_in).then_inc(small_in, 16)
                    nkc = cond[0:1, :].rearrange("o d -> d o")
                    act.dma_start(nk[0:DH, :], nkc).then_inc(small_in, 16)
                    act.dma_start(nk[DH:P, :], nkc).then_inc(small_in, 16)
                    act.dma_start(nv[:], cond[1:2, :].broadcast_to([P, DH])).then_inc(small_in, 16)
                    act.dma_start(nab_b[:], nab.rearrange("(o h) -> o h", o=1).broadcast_to([P, H])).then_inc(small_in, 16)
                    act.dma_start(mask8[DH:DH + 1, :], mask).then_inc(small_in, 16)
                    act.wait_ge(small_in, 16 * 6)
                    for g in range(4):
                        for c in range(DC):
                            act.wait_ge(turned, DC * g + c + 1)
                            act.activation(xnT[:, c, CW * g:CW * g + CW], turn[c][:], ACT.Copy,
                                           scale=gcol[:, c:c + 1]).then_inc(xnT_ready, 1)
                        act.wait_ge(k_ready, g + 1)
                        act.activation(k_hi[:, CW * g:CW * g + CW], kps[g % 2][:], ACT.Copy).then_inc(khi_ready, 1)
                    for b in range(B):
                        act.wait_ge(v_ready, b + 1)
                        act.activation(values[:, QT * b:QT * b + QT, :], vps[b][:], ACT.Copy).then_inc(v_out, 1)

                @block.gpsimd
                def _(pool):
                    pool.memset(ident[:], 0.0).then_inc(zeroed, 1)
                    pool.memset(power[:], -0.5).then_inc(const_ready, 1)
                    pool.wait_ge(zeroed, 1)
                    pool.affine_select(out=ident[:], in_=ident[:], compare_op=ALU.not_equal, fill=1.0, base=0,
                                       pattern=[[-1, P]], channel_multiplier=1).then_inc(const_ready, 1)
                    pool.wait_ge(const_ready, 1)
                    for g in range(4):
                        pool.wait_ge(var_ready, g + 1)
                        pool.tensor_tensor(rstd[:, 4 * g:4 * g + 4], rstd[:, 4 * g:4 * g + 4], power[:],
                                           ALU.pow).then_inc(rstd_ready, 1)

                @block.vector
                def _(dve):
                    dve.memset(k_lo[DH:P, :].bitcast(F32), 0.0).then_inc(step0, 1)
                    for g in range(4):
                        dve.wait_ge(x_in[g], 16)
                        for t in range(4 * g, 4 * g + 4):
                            last = dve.bn_stats(stats[:, t, :], xs[:, t, :])
                        last.then_inc(step0, 1)
                        dve.wait_ge(step0, 2 + 2 * g)
                        for t in range(4 * g, 4 * g + 4):
                            last = dve.bn_aggr(mv[:, t, :], stats[:, t, :])
                        last.then_inc(step0, 1)
                        dve.wait_ge(step0, 3 + 2 * g)
                        dve.tensor_scalar(rstd[:, 4 * g:4 * g + 4], mv[:, 4 * g:4 * g + 4, 1], EPS, None,
                                          ALU.add).then_inc(var_ready, 1)
                    for g in range(4):
                        dve.wait_ge(rstd_ready, g + 1)
                        for t in range(4):
                            tt = 4 * g + t
                            last = dve.tensor_scalar(xh[:, g, t, :], xs[:, tt, :], mv[:, tt, 0:1], rstd[:, tt:tt + 1],
                                                     ALU.subtract, ALU.mult)
                        last.then_inc(xh_ready, 1)
                    dve.memset(yacc[:], 0.0).then_inc(step0, 1)
                    dve.wait_ge(small_in, 16 * 6)
                    dve.tensor_scalar(k_lo[DH:DH + 1, 0:T], mask8[DH:DH + 1, :], MASKED, -MASKED, ALU.mult, ALU.add)
                    for j in range(2):
                        last = dve.tensor_copy(k_hi[:, T + j:T + j + 1], nk[:])
                    last.then_inc(step0, 1)
                    dve.wait_ge(step0, 11)
                    for j in range(2):
                        dve.tensor_tensor(k_lo[0:DH, T + j:T + j + 1], nk[0:DH, :],
                                          k_hi[0:DH, T + j:T + j + 1].bitcast(F32), ALU.subtract)
                    for g in range(4):
                        dve.wait_ge(khi_ready, g + 1)
                        cols = slice(CW * g, CW * g + CW)
                        dve.tensor_tensor(k_lo[0:DH, cols], kps[g % 2][0:DH, :], k_hi[0:DH, cols].bitcast(F32),
                                          ALU.subtract).then_inc(klo_ready, 1)

                @block.tensor
                def _(pe):
                    pe.wait_ge(const_ready, 2)
                    pe.wait_ge(w_in, 48)
                    for g in range(4):
                        pe.wait_ge(xh_ready, g + 1)
                        for c in range(DC):
                            if g:
                                pe.wait_ge(xnT_ready, DC * (g - 1) + c + 1)
                            for t in range(4):
                                last = pe.transpose(turn[c][:, P * t:P * t + P], xh[:, g, t, P * c:P * c + P], ident[:])
                            last.then_inc(turned, 1)
                        pe.wait_ge(xnT_ready, DC * (g + 1))
                        if g >= 2:
                            pe.wait_ge(klo_ready, g - 1)
                        for c in range(DC):
                            last = pe.matmul(kps[g % 2][:], wk[:, c, :], xnT[:, c, CW * g:CW * g + CW],
                                             start=(c == 0), stop=(c == DC - 1))
                        last.then_inc(k_ready, 1)
                        for t in range(4 * g, 4 * g + 4):
                            for c in range(DC):
                                last = pe.matmul(vps[t // QT][:, t % QT, :], xnT[:, c, P * t:P * t + P], wv[:, c, :],
                                                 start=(c == 0), stop=(c == DC - 1))
                        if g % 2:
                            last.then_inc(v_ready, 1)

        with ExitStack() as st:
            wq = sbuf(st, "wq", [P, DC, P])
            wo = sbuf(st, "wo", [P, D])
            q_f32 = sbuf(st, "q_f32", [P, T])
            q_hi = sbuf(st, "q_hi", [P, T], F32R)
            q_lo = sbuf(st, "q_lo", [P, T], F32R)
            q_hilo = [sbuf(st, f"q_hilo{h}", [P, T], F32R) for h in range(2)]
            q_one = [sbuf(st, f"q_one{h}", [P, T], F32R) for h in range(2)]
            bias_row = [sbuf(st, f"bias_row{i}", [P, S]) for i in range(4)]
            probs = [sbuf(st, f"probs{i}", [P, S]) for i in range(4)]
            probsT = [sbuf(st, f"probsT{i}", [P, QT, P]) for i in range(2)]
            o_part = [sbuf(st, f"o_part{i}", [P, 8, DH]) for i in range(2)]
            o_null = [sbuf(st, f"o_null{i}", [P, 8, DH]) for i in range(2)]
            o_nat = sbuf(st, "o_nat", [P, QT, B, P])
            oT = sbuf(st, "oT", [P, QT, B, P])
            neg_null = sbuf(st, "neg_null", [P, 2, QT * B])
            neg_max = sbuf(st, "neg_max", [P, UNITS])
            part_max = sbuf(st, "part_max", [P, UNITS])
            null_arg = sbuf(st, "null_arg", [P, UNITS])
            null_exp = sbuf(st, "null_exp", [P, UNITS])
            row_sum = sbuf(st, "row_sum", [P, UNITS])
            full_sum = sbuf(st, "full_sum", [P, UNITS])
            inv_sum = sbuf(st, "inv_sum", [P, UNITS])
            null_w = sbuf(st, "null_w", [P, UNITS])
            s_ps = [psum(st, f"s_ps{i}", [P, CW]) for i in range(3)]
            t_ps = [psum(st, f"t_ps{i}", [P, CW]) for i in range(2)]
            o_ps = [psum(st, f"o_ps{i}", [P, 8, DH]) for i in range(2)]
            m_ps = psum(st, "m_ps", [P, CW])

            wq_in, wo_in = sem("wq_in"), sem("wo_in")
            bias_in = [sem(f"bias_in{i}") for i in range(4)]
            bias_ready = sem("bias_ready")
            scores_ready, scores_read = sem("scores_ready"), sem("scores_read")
            probs_ready = sem("probs_ready")
            turn_ready, turn_out_act, turn_out_dve = sem("turn_ready"), sem("turn_out_act"), sem("turn_out_dve")
            pv_done = sem("pv_done")
            misc_ready, misc_read = sem("misc_ready"), sem("misc_read")
            q_copied = sem("q_copied")
            q_split, q_in = sem("q_split"), [sem(f"q_in{h}") for h in range(2)]
            null_arg_ready, null_exp_ready, inv_ready = sem("null_arg_ready"), sem("null_exp_ready"), sem("inv_ready")
            o_part_ready, o_nat_ready, o_null_ready = sem("o_part_ready"), sem("o_nat_ready"), sem("o_null_ready")
            ones_ready, dve_sum, null_w_ready = sem("ones_ready"), sem("dve_sum"), sem("null_w_ready")

            marks_dve, marks_pool, marks_sp = sem("marks_dve"), sem("marks_pool"), sem("marks_sp")
            LAST = PAIRS - 1
            MISC = ([(3 + j, "turn", j) for j in range(4)] + [(7, "nullB", 0)] + [(8 + j, "query", j) for j in range(4)]
                    + [(12 + j, "project", j) for j in range(8)] + [(28, "nullA", 0)])
            PER_PAIR = len(MISC)
            PRO = 5

            def misc_of(p, step):
                for m, (s, kind, j) in enumerate(MISC):
                    if s == step:
                        if isinstance(p, int):
                            first, last = p == 0, p == LAST
                            if first and kind in ("turn", "project") or last and kind in ("query", "nullA"):
                                return None
                            skipped = 12 if p else sum(1 for _, k, _ in MISC[:m] if k in ("turn", "project"))
                            if last:
                                skipped += sum(1 for _, k, _ in MISC[:m] if k == "query")
                            return kind, j, PRO + PER_PAIR * p + m - skipped
                        return kind, j, PER_PAIR * p + (PRO + m - 12)
                return None

            TAIL = PRO + PER_PAIR * PAIRS - 12 - 5

            def pairs(eng, body):
                body(0)
                with eng.Fori(1, LAST) as p:
                    body(p)
                body(LAST)

            def unit_at(p, u):
                if u >= UNITS:
                    if isinstance(p, int) and p == LAST:
                        return None
                    return p + 1, BODY[u - UNITS]
                return p, BODY[u]

            def query_tile(x):
                t = QT * x.batch + x.tile
                return slice(P * t, P * t + P)

            with nc.Block() as block:
                @block.sync
                def _(sp):
                    wq_h = Wq.rearrange("(c p) (r n) -> r p c n", p=P, n=P)
                    wo_h = Wo.rearrange("(r p) n -> r p n", p=P)
                    sp.dma_start(wq[:], wq_h[0]).then_inc(wq_in, 16)

                    def body(p):
                        for r in range(UNITS // B):
                            x = BODY[r * B]
                            wait(sp, scores_read, CHUNKS * p + (FIRST_CHUNK[B * (r - 3)] if r >= 4 else FIRST_CHUNK[B * (r + 13)] - CHUNKS))
                            apart(sp, marks_sp)
                            width = P * x.blocks
                            rows = bias[2 * p + x.head]
                            sp.dma_start(bias_row[r % 4][:, 0:width],
                                         rows[P * x.tile:P * x.tile + P, 0:width]).then_inc(bias_in[r % 4], 16)
                            if r == 1 and not (isinstance(p, int) and p == LAST):
                                sp.wait_ge(q_split, 2 * p + 1)
                                sp.dma_start(wq[:], wq_h[p + 1]).then_inc(wq_in, 16)
                            if r == 15:
                                if not (isinstance(p, int) and p == 0):
                                    sp.wait_ge(misc_ready, misc_of(p, 19)[2] + 1)
                                sp.dma_start(wo[:], wo_h[p]).then_inc(wo_in, 16)
                    pairs(sp, body)

                @block.gpsimd
                def _(pool):
                    for h in range(2):
                        pool.memset(q_one[h][DH:P, :].bitcast(F32), 0.0).then_inc(ones_ready, 1)
                    pool.wait_ge(ones_ready, 2)
                    for h in range(2):
                        pool.memset(q_one[h][DH:DH + 1, :].bitcast(F32), 1.0).then_inc(ones_ready, 1)
                    pool.wait_ge(ones_ready, 4)

                    def split(p, queries):
                        pool.wait_ge(misc_read, queries)
                        wait(pool, q_in[0], 16 * p)
                        wait(pool, q_in[1], 48 * p)
                        apart(pool, marks_pool)
                        pool.tensor_copy(q_hi[:], q_f32[:]).then_inc(q_split, 1)
                        pool.wait_ge(q_split, 2 * p + 1)
                        pool.tensor_tensor(q_lo[:], q_f32[:], q_hi[:].bitcast(F32), ALU.subtract).then_inc(q_split, 1)

                    def fill_a(p):
                        wait(pool, scores_ready, CHUNKS * p - CHUNKS // 2)
                        pool.wait_ge(q_split, 2 * p + 2)
                        apart(pool, marks_pool)
                        pool.dma_start(q_hilo[0][DH:P, :], q_lo[0:DH, :]).then_inc(q_in[0], 16)
                        pool.tensor_copy(q_hilo[0][0:DH, :], q_hi[0:DH, :].bitcast(F32)).then_inc(q_copied, 1)
                        pool.tensor_copy(q_one[0][0:DH, :], q_hi[0:DH, :].bitcast(F32)).then_inc(q_copied, 1)

                    def fill_b(p):
                        wait(pool, scores_ready, CHUNKS * p)
                        pool.wait_ge(q_split, 2 * p + 2)
                        apart(pool, marks_pool)
                        pool.dma_start(q_hilo[1][0:DH, :], q_hi[DH:P, :]).then_inc(q_in[1], 16)
                        pool.dma_start(q_hilo[1][DH:P, :], q_lo[DH:P, :]).then_inc(q_in[1], 16)
                        pool.dma_start(q_one[1][0:DH, :], q_hi[DH:P, :]).then_inc(q_in[1], 16)

                    def diagonal(p, r):
                        x = BODY[r * B]
                        pool.wait_ge(bias_in[r % 4], 16 * (4 * p + r // 4 + 1))
                        d = bias_row[r % 4][:, P * x.tile:P * x.tile + P]
                        apart(pool, marks_pool)
                        pool.affine_select(out=d, in_=d, compare_op=ALU.is_ge, fill=-MASKED, base=0,
                                           pattern=[[-1, P]], channel_multiplier=1).then_inc(bias_ready, 1)

                    def finish(p, g):
                        cols = slice(8 * g, 8 * g + 8)
                        pool.wait_ge(inv_ready, GROUPS * p + g + 1)
                        pool.tensor_tensor(null_w[:, cols], null_exp[:, cols], inv_sum[:, cols],
                                           ALU.mult).then_inc(null_w_ready, 1)
                        pool.wait_ge(null_w_ready, GROUPS * p + g + 1)
                        pool.tensor_tensor(o_null[g % 2][:], nv[:].unsqueeze(1).broadcast_to([P, 8, DH]),
                                           null_w[:, cols].unsqueeze(2).broadcast_to([P, 8, DH]),
                                           ALU.mult).then_inc(o_null_ready, 1)
                        pool.wait_ge(o_null_ready, GROUPS * p + g + 1)
                        pool.wait_ge(o_part_ready, GROUPS * p + g + 1)
                        if g == 0 and not (isinstance(p, int) and p == 0):
                            pool.wait_ge(misc_ready, misc_of(p, 6)[2] + 1)
                        rows, head = slice(4 * (g % 2), 4 * (g % 2) + 4), g // 2
                        pool.tensor_tensor(o_nat[:, rows, :, DH * head:DH * head + DH],
                                           o_part[g % 2][:], o_null[g % 2][:], ALU.add).then_inc(o_nat_ready, 1)

                    def body(p):
                        first, last = isinstance(p, int) and p == 0, isinstance(p, int) and p == LAST
                        for r in range(16):
                            diagonal(p, r)
                            if r == 3:
                                fill_b(p)
                                if not first:
                                    finish(p - 1, 3)
                            if r == 6:
                                finish(p, 0)
                            if r == 9 and not last:
                                split(p + 1, misc_of(p, 11)[2] + 1)
                            if r == 10:
                                finish(p, 1)
                            if r == 11 and not last:
                                fill_a(p + 1)
                            if r == 14:
                                finish(p, 2)
                    split(0, 4)
                    fill_a(0)
                    pairs(pool, body)
                    finish(LAST, 3)

                @block.scalar
                def _(act):
                    def exps(p, u):
                        at = unit_at(p, u)
                        if at is None:
                            return
                        p, x = at
                        w = P * x.blocks
                        act.wait_ge(scores_read, CHUNKS * p + FIRST_CHUNK[x.u + 1])
                        act.activation(probs[x.u % 4][:, 0:w], probs[x.u % 4][:, 0:w], ACT.Exp, scale=-1.0,
                                       bias=neg_max[:, x.u:x.u + 1], accum_out=row_sum[:, x.u:x.u + 1]).then_inc(probs_ready, 1)

                    def turned_out(p, u):
                        at = unit_at(p, u)
                        if at is None:
                            return
                        p, x = at
                        for n, (first, k) in enumerate(x.chunks):
                            c = FIRST_CHUNK[x.u] + n
                            if c % 2 == 0:
                                continue
                            act.wait_ge(turn_ready, CHUNKS * p + c + 1)
                            wait(act, pv_done, UNITS * p + x.u - 1)
                            act.activation(probsT[x.u % 2][:, first:first + k, :], t_ps[1][:, 0:P * k],
                                           ACT.Copy).then_inc(turn_out_act, 1)

                    def misc(kind, j, use):
                        act.wait_ge(misc_ready, use + 1)
                        if kind == "turn":
                            act.activation(oT[:, 2 * j:2 * j + 2, :, :], m_ps[:], ACT.Copy).then_inc(misc_read, 1)
                        else:
                            act.activation(q_f32[:, CW * j:CW * j + CW], m_ps[:], ACT.Copy,
                                           scale=DH ** -0.5).then_inc(misc_read, 1)

                    def step(p, s):
                        if s + 2 >= 0:
                            exps(p, s + 2)
                        use = misc_of(p, s - 1)
                        if use and use[0] in ("turn", "query"):
                            if use[0] == "query" and use[1] == 0:
                                act.wait_ge(q_split, 2 * p + 2)
                            misc(*use)
                        if s + 1 >= 0:
                            turned_out(p, s + 1)
                        if s >= 0 and s % 8 == 6:
                            g = s // 8
                            cols = slice(8 * g, 8 * g + 8)
                            act.wait_ge(null_arg_ready, GROUPS * p + g + 1)
                            act.activation(null_exp[:, cols], null_arg[:, cols], ACT.Exp).then_inc(null_exp_ready, 1)

                    for j in range(4):
                        misc("query", j, j)
                    for s in range(-3, 0):
                        step(0, s)

                    def body(p):
                        for s in range(UNITS):
                            step(p, s)
                    pairs(act, body)
                    for j in range(4):
                        misc("turn", j, TAIL + j)

                @block.vector
                def _(dve):
                    def scores(p, u):
                        at = unit_at(p, u)
                        if at is None:
                            return
                        p, x = at
                        u = x.u
                        dve.wait_ge(bias_ready, 16 * p + x.row + 1)
                        wait(dve, turn_ready, CHUNKS * p + (FIRST_CHUNK[u - 3] if u >= 4 else FIRST_CHUNK[UNITS + u - 3] - CHUNKS))
                        for n, (first, k) in enumerate(x.chunks):
                            c = FIRST_CHUNK[u] + n
                            cols = slice(P * first, P * (first + k))
                            start = part_max[:, u:u + 1] if n else neg_null[:, x.head, u % 16:u % 16 + 1]
                            to = neg_max if n == len(x.chunks) - 1 else part_max
                            dve.wait_ge(scores_ready, CHUNKS * p + c + 1)
                            if n:
                                dve.wait_ge(scores_read, CHUNKS * p + c)
                            apart(dve, marks_dve)
                            dve.tensor_tensor_reduce(probs[u % 4][:, cols], s_ps[c % 3][:, 0:P * k],
                                                     bias_row[x.row % 4][:, cols], -1.0, start, ALU.add, ALU.min,
                                                     to[:, u:u + 1]).then_inc(scores_read, 1)

                    def turned_out(p, u):
                        at = unit_at(p, u)
                        if at is None:
                            return
                        p, x = at
                        for n, (first, k) in enumerate(x.chunks):
                            c = FIRST_CHUNK[x.u] + n
                            if c % 2:
                                continue
                            dve.wait_ge(turn_ready, CHUNKS * p + c + 1)
                            wait(dve, pv_done, UNITS * p + x.u - 1)
                            dve.tensor_copy(probsT[x.u % 2][:, first:first + k, :], t_ps[0][:, 0:P * k]).then_inc(turn_out_dve, 1)

                    def null_scores(p, h, use):
                        dve.wait_ge(misc_ready, use + 1)
                        dve.tensor_scalar(neg_null[:, h, :], m_ps[:, 0:4 * QT:2], -1.0, nab_b[:, bass.ds(2 * p + h, 1)],
                                          ALU.mult, ALU.subtract).then_inc(misc_read, 1)
                        dve.wait_ge(misc_read, use + 1)

                    def project(j, use):
                        dve.wait_ge(misc_ready, use + 1)
                        tiles = yacc[:].rearrange("p (b i) d -> p i b d", b=B)[:, QT - 1 - j]
                        dve.tensor_tensor(tiles, m_ps[:].rearrange("p (b d) -> p b d", b=B), tiles, ALU.add).then_inc(misc_read, 1)

                    def outputs(p, g):
                        cols = slice(8 * g, 8 * g + 8)
                        dve.wait_ge(pv_done, UNITS * p + 8 * g + 8)
                        dve.wait_ge(inv_ready, GROUPS * p + g + 1)
                        wait(dve, o_nat_ready, GROUPS * p + g - 1)
                        dve.tensor_tensor(o_part[g % 2][:], o_ps[g % 2][:], inv_sum[:, cols].unsqueeze(2).broadcast_to([P, 8, DH]),
                                          ALU.mult).then_inc(o_part_ready, 1)

                    def step(p, s):
                        use = misc_of(p, s - 1)
                        if use and use[0] == "nullB":
                            null_scores(p, 1, use[2])
                        if use and use[0] == "nullA":
                            null_scores(p + 1, 0, use[2])
                        scores(p, s + 3)
                        if use and use[0] == "project":
                            project(use[1], use[2])
                        if s + 1 >= 0:
                            turned_out(p, s + 1)
                        if s >= 0 and s % 8 == 5:
                            g = s // 8
                            cols = slice(8 * g, 8 * g + 8)
                            dve.wait_ge(scores_read, CHUNKS * p + FIRST_CHUNK[8 * g + 8])
                            dve.tensor_tensor(null_arg[:, cols], neg_max[:, cols], neg_null[:, g // 2, 8 * (g % 2):8 * (g % 2) + 8],
                                              ALU.subtract).then_inc(null_arg_ready, 1)
                        if s >= 0 and s % 8 == 7:
                            g = s // 8
                            cols = slice(8 * g, 8 * g + 8)
                            dve.wait_ge(null_exp_ready, GROUPS * p + g + 1)
                            dve.wait_ge(probs_ready, UNITS * p + 8 * g + 8)
                            dve.tensor_tensor(full_sum[:, cols], row_sum[:, cols], null_exp[:, cols], ALU.add).then_inc(dve_sum, 1)
                            dve.wait_ge(dve_sum, GROUPS * p + g + 1)
                            dve.reciprocal(inv_sum[:, cols], full_sum[:, cols]).then_inc(inv_ready, 1)
                        if s >= 9 and s % 8 == 1:
                            outputs(p, s // 8 - 1)
                        if s == 1 and not (isinstance(p, int) and p == 0):
                            outputs(p - 1, GROUPS - 1)

                    null_scores(0, 0, 4)
                    for s in range(-3, 0):
                        step(0, s)

                    def body(p):
                        for s in range(UNITS):
                            step(p, s)
                    pairs(dve, body)
                    outputs(LAST, GROUPS - 1)
                    for j in range(8):
                        project(j, TAIL + 4 + j)

                @block.tensor
                def _(pe):
                    def scores(p, u):
                        at = unit_at(p, u)
                        if at is None:
                            return
                        p, x = at
                        h, keys = x.head, S * x.batch
                        for n, (first, k) in enumerate(x.chunks):
                            c = FIRST_CHUNK[x.u] + n
                            cols = slice(keys + P * first, keys + P * (first + k))
                            wait(pe, scores_read, CHUNKS * p + c - 2)
                            pe.matmul(s_ps[c % 3][:, 0:P * k], q_hilo[h][:, query_tile(x)], k_hi[:, cols], start=True, stop=False)
                            pe.matmul(s_ps[c % 3][:, 0:P * k], q_one[h][:, query_tile(x)], k_lo[:, cols],
                                      start=False, stop=True).then_inc(scores_ready, 1)

                    def turn(p, u):
                        at = unit_at(p, u)
                        if at is None:
                            return
                        p, x = at
                        pe.wait_ge(probs_ready, UNITS * p + x.u + 1)
                        for n, (first, k) in enumerate(x.chunks):
                            c = FIRST_CHUNK[x.u] + n
                            wait(pe, (turn_out_dve, turn_out_act)[c % 2], CHUNKS // 2 * p + c // 2)
                            for j in range(k):
                                last = pe.transpose(t_ps[c % 2][:, P * j:P * j + P],
                                                    probs[x.u % 4][:, P * (first + j):P * (first + j) + P], ident[:])
                            last.then_inc(turn_ready, 1)

                    def weigh(p, u):
                        x = BODY[u]
                        g = u // 8
                        for n in range(len(x.chunks)):
                            c = FIRST_CHUNK[u] + n
                            pe.wait_ge((turn_out_dve, turn_out_act)[c % 2], CHUNKS // 2 * p + c // 2 + 1)
                        if u % 8 == 0:
                            wait(pe, o_part_ready, GROUPS * p + g - 1)
                        for k in range(x.blocks):
                            last = pe.matmul(o_ps[g % 2][:, u % 8, :], probsT[u % 2][:, k, :], values[:, QT * x.batch + k, :],
                                             start=(k == 0), stop=(k == x.blocks - 1))
                        last.then_inc(pv_done, 1)

                    def misc(p, kind, j, use):
                        wait(pe, misc_read, use)
                        if kind == "turn":
                            pe.wait_ge(o_nat_ready, GROUPS * p)
                            for t in range(4):
                                last = pe.transpose(m_ps[:, P * t:P * t + P], o_nat[:, 2 * j + t // 2, t % 2, :], ident[:])
                        elif kind == "project":
                            pe.wait_ge(wo_in, 16 * p)
                            for b in range(B):
                                last = pe.matmul(m_ps[:, D * b:D * b + D], oT[:, j, b, :], wo[:], start=True, stop=True)
                        elif kind == "query":
                            pe.wait_ge(wq_in, 16 * (p + 2))
                            for c in range(DC):
                                last = pe.matmul(m_ps[:], wq[:, c, :], xnT[:, c, CW * j:CW * j + CW], start=(c == 0), stop=(c == DC - 1))
                        else:
                            h = 1 if kind == "nullB" else 0
                            pp = p if h else p + 1
                            if h == 0:
                                pe.wait_ge(q_copied, 2 * pp + 2)
                            pe.wait_ge(q_in[h], (16, 48)[h] * (pp + 1))
                            for u in range(QT * B):
                                x = BODY[u]
                                pe.matmul(m_ps[:, 2 * u:2 * u + 2], q_hilo[h][:, query_tile(x)], k_hi[:, T:T + 2], start=True, stop=False)
                                last = pe.matmul(m_ps[:, 2 * u:2 * u + 2], q_one[h][:, query_tile(x)], k_lo[:, T:T + 2],
                                                 start=False, stop=True)
                        last.then_inc(misc_ready, 1)

                    def step(p, s):
                        scores(p, s + 3)
                        if s + 1 >= 0:
                            turn(p, s + 1)
                        if s >= 0:
                            weigh(p, s)
                        use = misc_of(p, s)
                        if use:
                            misc(p, *use)

                    pe.wait_ge(ones_ready, 4)
                    for j in range(4):
                        misc(-1, "query", j, j)
                    misc(-1, "nullA", 0, 4)
                    for s in range(-3, 0):
                        step(0, s)

                    def body(p):
                        for s in range(UNITS):
                            step(p, s)
                    pairs(pe, body)
                    for j in range(4):
                        misc(PAIRS, "turn", j, TAIL + j)
                    for j in range(8):
                        misc(PAIRS, "project", j, TAIL + 4 + j)

        attn.close()

        with ExitStack() as later:
            xT_hi = sbuf(later, "xT_hi", [P, DC, T], F32R)
            xT_lo = sbuf(later, "xT_lo", [P, DC, T], F32R)
            gates = sbuf(later, "gates", [P, NT, EXPERTS])
            gates2 = sbuf(later, "gates2", [P, NT, E])
            ident_bf = sbuf(later, "ident_bf", [P, P], BF16)
            power4 = sbuf(later, "power4", [P, 4])
            set_up = sem("set_up")
            with nc.Block() as block:
                @block.vector
                def _(dve):
                    dve.memset(power4[:], -0.5).then_inc(set_up, 1)
                    dve.tensor_copy(ident_bf[:], ident[:]).then_inc(set_up, 1)
            feed_forward_stage(nc, sbuf, psum, sem, aps, (xs, yacc, ident[:], ident_bf[:], xT_hi, xT_lo, gates, power4[:]))
            first_mixture_stage(nc, sbuf, psum, sem, aps, (yacc, xT_hi, xT_lo, gates))
            pair_attention_stage(nc, sbuf, psum, sem, aps, (xs, yacc, ident[:], xT_hi, xT_lo, gates2, power4[:]))
            second_mixture_stage(nc, sbuf, psum, sem, aps, (xs, xT_hi, xT_lo, gates2, out))


def kernel(**inputs):
    import numpy as np
    import concourse.bacc as bacc
    from concourse.bass_utils import run_bass_kernel_spmd

    def by_partition(w):
        e, k, n = w.shape
        return w.reshape(e, k // P, P, n).transpose(0, 2, 1, 3).reshape(e, P, k // P * n)

    def halves(w, axis):
        return np.stack(np.split(w, 2, axis=axis))

    gate = np.concatenate([inputs["L1_cond_w_gate"], halves(inputs["L1_cond_sw_gate"], 1)])
    up = np.concatenate([inputs["L1_cond_w_up"], halves(inputs["L1_cond_sw_up"], 1)])
    down = np.concatenate([inputs["L1_cond_w_down"], halves(inputs["L1_cond_sw_down"], 0)])
    first_weights = np.concatenate([by_partition(np.concatenate([gate, up], 2)), by_partition(down)], 2)
    second_weights = np.concatenate([by_partition(inputs["L1_ffn_moe_w1"]), by_partition(inputs["L1_ffn_moe_w2"])], 2)
    nc = bacc.Bacc("TRN2", target_bir_lowering=False, num_devices=1)
    laid = {
        "x": inputs["x"].reshape(T, D),
        "bias": inputs["fside_16xSxS_0"],
        "cond": inputs["cond_64"],
        "mask": inputs["mask_BxS_bk0"].reshape(1, T),
        "g_in": inputs["L0_cond_g_in"].reshape(DC, P).T,
        "nab": inputs["L0_cond_null_attn_bias"],
        "Wq": inputs["L0_cond_Wq"],
        "Wkv": inputs["L0_cond_Wkv"],
        "Wo": inputs["L0_cond_Wo"],
        "g_out": inputs["L0_cond_g_out"].reshape(1, D),
        "ffT": inputs["L0_ffn_weight"].T,
        "wtT": inputs["L1_cond_wt"].T,
        "wgT": inputs["L1_cond_wg"].T,
        "condT": inputs["cond_64"].T,
        "order": np.tril(np.ones((E, E), np.float32), -1).reshape(1, E * E),
        "m1_w": first_weights,
        "ln1_w": inputs["L1_ffn_ln1_weight"].reshape(DC, P).T,
        "ln1_b": inputs["L1_ffn_ln1_bias"].reshape(DC, P).T,
        "ln2_w": inputs["L1_ffn_ln2_weight"].reshape(DC, P).T,
        "ln2_b": inputs["L1_ffn_ln2_bias"].reshape(DC, P).T,
        "qkvT": inputs["L1_ffn_qkv_weight"].T,
        "projT": inputs["L1_ffn_proj_weight"].T,
        "routerT": inputs["L1_ffn_router_weight"].T,
        "m2_w": second_weights,
    }
    laid = {n: np.ascontiguousarray(a) for n, a in laid.items()}
    aps = {n: nc.dram_tensor(n + "_dram", a.shape, mybir.dt.from_np(a.dtype), kind="ExternalInput").ap() for n, a in laid.items()}
    out = nc.dram_tensor("out_dram", (T, D), F32, kind="ExternalOutput").ap()
    program(nc, **aps, out=out)
    r = run_bass_kernel_spmd(nc, [{n + "_dram": a for n, a in laid.items()}], core_ids=[0])
    return r.results[0]["out_dram"].reshape(B, S, D)
```

```python
import concourse.bass as bass
from concourse import mybir
from contextlib import ExitStack

F32 = mybir.dt.float32
F32R = mybir.dt.float32r
BF16 = mybir.dt.bfloat16
U8 = mybir.dt.uint8
ALU = mybir.AluOpType
ACT = mybir.ActivationFunctionType
AX = mybir.AxisListType

P = 128
B, S, D = 2, 1024, 256
T = B * S
NT = T // P
DC = D // P
H, DH = 16, 64
QT = S // P
PAIRS = H // 2
CW = 512
MASKED = 1.0e30
EPS = 1e-5
ROUND = 1.5 * 2 ** 23
E = 8
M1 = 128
EXPERTS = E + 2
LEAKY = 0.01
COND = 64
KV, HD = 4, 16
QKV = (H + 2 * KV) * HD
F2 = 512


class Steps:

    def __init__(self, per_body):
        self.per_body = per_body
        self.n = 0

    def up(self):
        self.n += 1
        return 1

    def here(self, it):
        return self.per_body * it + self.n


def flat(tiles):
    return tiles[:].rearrange("p t d -> p (t d)")


def gate_top_two(dve, step, steps, it, gate, scratch, weights):
    above, same, order, rank = scratch
    this = gate.unsqueeze(3).broadcast_to([P, 4, E, E])
    other = gate.unsqueeze(2).broadcast_to([P, 4, E, E])
    dve.tensor_tensor(above, other, this, ALU.is_gt)
    dve.tensor_tensor(same, other, this, ALU.is_equal).then_inc(step, steps.up())
    dve.wait_ge(step, steps.here(it))
    dve.tensor_tensor(same, same, order.unsqueeze(1).broadcast_to([P, 4, E, E]), ALU.mult).then_inc(step, steps.up())
    dve.wait_ge(step, steps.here(it))
    dve.tensor_tensor(above, above, same, ALU.add).then_inc(step, steps.up())
    dve.wait_ge(step, steps.here(it))
    dve.tensor_reduce(rank, above, AX.X, ALU.add).then_inc(step, steps.up())
    dve.wait_ge(step, steps.here(it))
    return dve.scalar_tensor_tensor(weights, rank, 1.5, gate, ALU.is_lt, ALU.mult)


def feed_forward_stage(nc, sbuf, psum, sem, aps, keep):
    xs, yacc, ident, ident_bf, xT_hi, xT_lo, gates, power4 = keep
    with ExitStack() as st:
        g_out = sbuf(st, "g_out", [P, D])
        w_raw = sbuf(st, "ff_w_raw", [P, DC, D])
        w_u = sbuf(st, "ff_w_u", [P, DC, D])
        w_ter = sbuf(st, "ff_w_ter", [P, DC, D], BF16)
        w_abs = sbuf(st, "ff_w_abs", [P, 1])
        w_scale = sbuf(st, "ff_w_scale", [P, 1])
        w_inv = sbuf(st, "ff_w_inv", [P, 1])
        w_scale127 = sbuf(st, "ff_w_scale127", [P, 1])
        ones = sbuf(st, "ff_ones", [P, P])
        cond_c = sbuf(st, "cond_c", [COND, B])
        cond_b = sbuf(st, "cond_b", [COND, B, P])
        wg = sbuf(st, "wg", [COND, E])
        wt = sbuf(st, "wt", [P, DC, E])
        order = sbuf(st, "ff_order", [P, E, E])
        half_cond = sbuf(st, "half_cond", [P, B, E])
        stats = [sbuf(st, f"ff_stats{r}", [P, 4, 6]) for r in range(2)]
        mv = [sbuf(st, f"ff_mv{r}", [P, 4, 2]) for r in range(2)]
        rstd = [sbuf(st, f"ff_rstd{r}", [P, 4]) for r in range(2)]
        yl = [sbuf(st, f"ff_yl{r}", [P, 4, D]) for r in range(2)]
        a_scale = [sbuf(st, f"a_scale{r}", [P, 4]) for r in range(2)]
        a_inv = [sbuf(st, f"a_inv{r}", [P, 4]) for r in range(2)]
        out_scale = [sbuf(st, f"out_scale{r}", [P, 4]) for r in range(2)]
        z = [sbuf(st, f"z{r}", [P, 4, D], BF16) for r in range(2)]
        zT = [sbuf(st, f"zT{r}", [P, DC, CW], BF16) for r in range(2)]
        x1 = [sbuf(st, f"x1_{r}", [P, 4, D]) for r in range(2)]
        x1T = [sbuf(st, f"x1T{r}", [P, DC, CW]) for r in range(2)]
        gate = [sbuf(st, f"ff_gate{r}", [P, 4, E]) for r in range(2)]
        top = [sbuf(st, f"ff_top{r}", [P, 4, E]) for r in range(2)]
        row = [sbuf(st, f"ff_row{r}", [P, 4]) for r in range(2)]
        above = sbuf(st, "ff_above", [P, 4, E, E])
        same = sbuf(st, "ff_same", [P, 4, E, E])
        rank = sbuf(st, "ff_rank", [P, 4, E])
        zT_ps = psum(st, "zT_ps", [P, DC, CW], BF16)
        f_ps = [psum(st, f"f_ps{r}", [P, 4, D]) for r in range(2)]
        x_ps = [psum(st, f"x_ps{c}", [P, CW]) for c in range(DC)]
        logits = [f_ps[r][:, 0, 0:4 * E].rearrange("p (t e) -> p t e", e=E) for r in range(2)]
        w_total = x_ps[0][:, 0:1]
        cond_ps = x_ps[1][:, 0:B * E].rearrange("p (b e) -> p b e", e=E)

        loaded, step, ones_set = sem("ff_loaded"), sem("ff_step"), sem("ff_ones_set")
        w_abs_ready, totals_ready, w_ready, cond_ready = (sem(f"ff_{n}") for n in ("w_abs_ready", "totals_ready", "w_ready", "cond_ready"))
        var_ready, rstd_ready, z_ready, z_turned, zT_ready, f_ready = (
            sem(f"ff_{n}") for n in ("var_ready", "rstd_ready", "z_ready", "z_turned", "zT_ready", "f_ready"))
        x1_ready, x1_turned, x1T_ready, xs_ready, hi_ready, lo_ready = (
            sem(f"ff_{n}") for n in ("x1_ready", "x1_turned", "x1T_ready", "xs_ready", "hi_ready", "lo_ready"))
        logits_ready, logits_read, exp_ready = (sem(f"ff_{n}") for n in ("logits_ready", "logits_read", "exp_ready"))
        marks = sem("ff_marks")
        LOADS = 16 * 6
        SETUP, PER_BODY = 5, 46
        xs_f, yacc_f = flat(xs), flat(yacc)

        def tile(it, r, t):
            return bass.ds(D * (QT * it + 4 * r + t), D)

        with nc.Block() as block:
            @block.sync
            def _(sp):
                sp.dma_start(w_raw[:], aps["ffT"].rearrange("(c p) o -> p c o", p=P)).then_inc(loaded, 16)
                sp.dma_start(g_out[:], aps["g_out"].broadcast_to([P, D])).then_inc(loaded, 16)
                sp.dma_start(wt[:], aps["wtT"].rearrange("(c p) e -> p c e", p=P)).then_inc(loaded, 16)
                sp.dma_start(wg[:], aps["wgT"]).then_inc(loaded, 16)
                sp.dma_start(cond_c[:], aps["condT"]).then_inc(loaded, 16)
                sp.dma_start(order[:], aps["order"].broadcast_to([P, E * E])).then_inc(loaded, 16)

            @block.gpsimd
            def _(pool):
                pool.memset(ones[:], 1.0).then_inc(ones_set, 1)
                with pool.Fori(0, B) as it:
                    for r in range(2):
                        pool.wait_ge(var_ready, 2 * it + r + 1)
                        pool.tensor_tensor(rstd[r][:], rstd[r][:], power4, ALU.pow).then_inc(rstd_ready, 1)

            @block.vector
            def _(dve):
                dve.wait_ge(loaded, LOADS)
                dve.tensor_reduce(w_abs[:], w_raw[:].rearrange("p c o -> p (c o)"), AX.X, ALU.add,
                                  apply_absolute_value=True).then_inc(w_abs_ready, 1)
                for b in range(B):
                    last = dve.tensor_copy(cond_b[:, b, :], cond_c[:, b:b + 1].broadcast_to([COND, P]))
                last.then_inc(cond_ready, 1)
                dve.wait_ge(totals_ready, 1)
                dve.tensor_scalar(w_scale[:], w_total, 1.0 / (D * D), 1e-8, ALU.mult, ALU.add).then_inc(step, 1)
                dve.wait_ge(step, 1)
                dve.reciprocal(w_inv[:], w_scale[:]).then_inc(step, 1)
                dve.wait_ge(step, 2)
                dve.tensor_scalar(w_u[:], w_raw[:], w_inv[:, 0:1], None, ALU.mult)
                dve.tensor_scalar(w_scale127[:], w_scale[:], 1.0 / 127.0, None, ALU.mult).then_inc(step, 1)
                dve.wait_ge(step, 3)
                dve.tensor_scalar(w_u[:], w_u[:], ROUND, ROUND, ALU.add, ALU.subtract).then_inc(step, 1)
                dve.wait_ge(step, 4)
                dve.tensor_scalar(w_ter[:], w_u[:], 1.0, -1.0, ALU.min, ALU.max).then_inc(w_ready, 1)
                dve.wait_ge(totals_ready, 2)
                dve.tensor_scalar(half_cond[:], cond_ps, 0.5, None, ALU.mult).then_inc(step, 1)
                dve.wait_ge(step, 5)

                with dve.Fori(0, B) as it:
                    steps = Steps(PER_BODY)
                    steps.n = SETUP
                    dve.wait_ge(exp_ready, 2 * it + 1)
                    for r in range(2):
                        for t in range(4):
                            last = dve.bn_stats(stats[r][:, t, :], yacc_f[:, tile(it, r, t)])
                        last.then_inc(step, steps.up())
                        dve.wait_ge(step, steps.here(it))
                        apart(dve, marks)
                        for t in range(4):
                            last = dve.bn_aggr(mv[r][:, t, :], stats[r][:, t, :])
                        last.then_inc(step, steps.up())
                        dve.wait_ge(step, steps.here(it))
                        dve.tensor_scalar(rstd[r][:], mv[r][:, :, 1], EPS, None, ALU.add).then_inc(var_ready, 1)
                    for r in range(2):
                        dve.wait_ge(rstd_ready, 2 * it + r + 1)
                        for t in range(4):
                            last = dve.tensor_scalar(yl[r][:, t, :], yacc_f[:, tile(it, r, t)], mv[r][:, t, 0:1],
                                                     rstd[r][:, t:t + 1], ALU.subtract, ALU.mult)
                        last.then_inc(step, steps.up())
                        dve.wait_ge(step, steps.here(it))
                        dve.tensor_tensor(yl[r][:], yl[r][:], g_out[:].unsqueeze(1).broadcast_to([P, 4, D]),
                                          ALU.mult).then_inc(step, steps.up())
                        dve.wait_ge(step, steps.here(it))
                        dve.tensor_reduce(a_scale[r][:], yl[r][:], AX.X, ALU.max, apply_absolute_value=True).then_inc(step, steps.up())
                        dve.wait_ge(step, steps.here(it))
                        dve.tensor_scalar(a_scale[r][:], a_scale[r][:], 1e-8, None, ALU.add).then_inc(step, steps.up())
                        dve.wait_ge(step, steps.here(it))
                        dve.tensor_scalar(out_scale[r][:], a_scale[r][:], w_scale127[:, 0:1], None, ALU.mult)
                        dve.reciprocal(a_inv[r][:], a_scale[r][:]).then_inc(step, steps.up())
                        dve.wait_ge(step, steps.here(it))
                        for t in range(4):
                            last = dve.tensor_scalar(yl[r][:, t, :], yl[r][:, t, :], a_inv[r][:, t:t + 1], 127.0,
                                                     ALU.mult, ALU.mult)
                        last.then_inc(step, steps.up())
                        dve.wait_ge(step, steps.here(it))
                        dve.tensor_scalar(yl[r][:], yl[r][:], 127.0, -128.0, ALU.min, ALU.max).then_inc(step, steps.up())
                        dve.wait_ge(step, steps.here(it))
                        dve.tensor_scalar(z[r][:], yl[r][:], ROUND, ROUND, ALU.add, ALU.subtract).then_inc(z_ready, 1)
                    for r in range(2):
                        dve.wait_ge(f_ready, 2 * it + r + 1)
                        for t in range(4):
                            last = dve.scalar_tensor_tensor(x1[r][:, t, :], f_ps[r][:, t, :], out_scale[r][:, t:t + 1],
                                                            xs_f[:, tile(it, r, t)], ALU.mult, ALU.add)
                        last.then_inc(x1_ready, 1)
                    for r in range(2):
                        for c in range(DC):
                            dve.wait_ge(hi_ready, 2 * DC * it + DC * r + c + 1)
                            cols = bass.ds(2 * CW * it + CW * r, CW)
                            last = dve.tensor_tensor(xT_lo[:, c, cols], x1T[r][:, c, :], xT_hi[:, c, cols].bitcast(F32), ALU.subtract)
                        last.then_inc(lo_ready, 1)
                    for r in range(2):
                        dve.wait_ge(logits_ready, 2 * it + r + 1)
                        dve.scalar_tensor_tensor(gate[r][:], logits[r], 0.5,
                                                 half_cond[:, bass.ds(it, 1), :].broadcast_to([P, 4, E]),
                                                 ALU.mult, ALU.add).then_inc(step, steps.up())
                        dve.wait_ge(step, steps.here(it))
                        dve.tensor_reduce(row[r][:], gate[r][:], AX.X, ALU.max).then_inc(step, steps.up())
                        dve.wait_ge(step, steps.here(it))
                        dve.tensor_tensor(gate[r][:], gate[r][:], row[r][:].unsqueeze(2).broadcast_to([P, 4, E]),
                                          ALU.subtract).then_inc(logits_read, 1)
                    for r in range(2):
                        dve.wait_ge(exp_ready, 2 * it + r + 2)
                        dve.tensor_reduce(row[r][:], gate[r][:], AX.X, ALU.add).then_inc(step, steps.up())
                        dve.wait_ge(step, steps.here(it))
                        dve.reciprocal(row[r][:], row[r][:]).then_inc(step, steps.up())
                        dve.wait_ge(step, steps.here(it))
                        dve.tensor_tensor(gate[r][:], gate[r][:], row[r][:].unsqueeze(2).broadcast_to([P, 4, E]),
                                          ALU.mult).then_inc(step, steps.up())
                        dve.wait_ge(step, steps.here(it))
                        gate_top_two(dve, step, steps, it, gate[r][:], (above[:], same[:], order[:], rank[:]), top[r][:]
                                     ).then_inc(step, steps.up())
                        dve.wait_ge(step, steps.here(it))
                        dve.tensor_reduce(row[r][:], top[r][:], AX.X, ALU.add).then_inc(step, steps.up())
                        dve.wait_ge(step, steps.here(it))
                        dve.tensor_scalar(row[r][:], row[r][:], 1e-20, None, ALU.add).then_inc(step, steps.up())
                        dve.wait_ge(step, steps.here(it))
                        dve.reciprocal(row[r][:], row[r][:]).then_inc(step, steps.up())
                        dve.wait_ge(step, steps.here(it))
                        dve.tensor_tensor(gates[:, bass.ds(QT * it + 4 * r, 4), 0:E], top[r][:],
                                          row[r][:].unsqueeze(2).broadcast_to([P, 4, E]), ALU.mult).then_inc(step, steps.up())
                    assert steps.n == SETUP + PER_BODY, steps.n - SETUP
                dve.memset(gates[:, :, E:EXPERTS], 1.0)

            @block.scalar
            def _(act):
                act.wait_ge(loaded, LOADS)
                act.sem_inc(exp_ready, 1)
                with act.Fori(0, B) as it:
                    for r in range(2):
                        act.wait_ge(z_turned, 2 * it + r + 1)
                        act.activation(zT[r][:], zT_ps[:], ACT.Copy).then_inc(zT_ready, 1)
                    for r in range(2):
                        for c in range(DC):
                            act.wait_ge(x1_turned, 2 * DC * it + DC * r + c + 1)
                            act.activation(x1T[r][:, c, :], x_ps[c][:], ACT.Copy).then_inc(x1T_ready, 1)
                        for c in range(DC):
                            act.wait_ge(x1T_ready, 2 * DC * it + DC * r + c + 1)
                            act.activation(xT_hi[:, c, bass.ds(2 * CW * it + CW * r, CW)], x1T[r][:, c, :],
                                           ACT.Copy).then_inc(hi_ready, 1)
                        act.wait_ge(x1_ready, 2 * it + r + 1)
                        act.activation(xs_f[:, bass.ds(D * (QT * it + 4 * r), 4 * D)], flat(x1[r]), ACT.Copy).then_inc(xs_ready, 1)
                    for r in range(2):
                        act.wait_ge(logits_read, 2 * it + r + 1)
                        act.activation(gate[r][:], gate[r][:], ACT.Exp).then_inc(exp_ready, 1)

            @block.tensor
            def _(pe):
                pe.wait_ge(ones_set, 1)
                pe.wait_ge(w_abs_ready, 1)
                pe.matmul(w_total, ones[:], w_abs[:], start=True, stop=True).then_inc(totals_ready, 1)
                pe.wait_ge(cond_ready, 1)
                for b in range(B):
                    last = pe.matmul(cond_ps[:, b, :], cond_b[:, b, :], wg[:], start=True, stop=True)
                last.then_inc(totals_ready, 1)
                pe.wait_ge(w_ready, 1)
                with pe.Fori(0, B) as it:
                    for r in range(2):
                        pe.wait_ge(z_ready, 2 * it + r + 1)
                        if r:
                            pe.wait_ge(zT_ready, 2 * it + r)
                        for c in range(DC):
                            for t in range(4):
                                last = pe.transpose(zT_ps[:, c, P * t:P * t + P], z[r][:, t, P * c:P * c + P], ident_bf)
                        last.then_inc(z_turned, 1)
                    for r in range(2):
                        pe.wait_ge(zT_ready, 2 * it + r + 1)
                        for t in range(4):
                            for c in range(DC):
                                last = pe.matmul(f_ps[r][:, t, :], zT[r][:, c, P * t:P * t + P], w_ter[:, c, :],
                                                 start=(c == 0), stop=(c == DC - 1))
                        last.then_inc(f_ready, 1)
                    for r in range(2):
                        pe.wait_ge(x1_ready, 2 * it + r + 1)
                        for c in range(DC):
                            if r:
                                pe.wait_ge(x1T_ready, 2 * DC * it + c + 1)
                            for t in range(4):
                                last = pe.transpose(x_ps[c][:, P * t:P * t + P], x1[r][:, t, P * c:P * c + P], ident)
                            last.then_inc(x1_turned, 1)
                    for r in range(2):
                        pe.wait_ge(x1T_ready, 2 * DC * it + DC * (r + 1))
                        for t in range(4):
                            for c in range(DC):
                                last = pe.matmul(logits[r][:, t, :], x1T[r][:, c, P * t:P * t + P], wt[:, c, :],
                                                 start=(c == 0), stop=(c == DC - 1))
                        last.then_inc(logits_ready, 1)


def first_mixture_stage(nc, sbuf, psum, sem, aps, keep):
    yacc, xT_hi, xT_lo, gates = keep
    GU = 2 * M1
    WCOLS = DC * GU + D
    LAST = EXPERTS // 2 - 1
    with ExitStack() as st:
        w_raw = [sbuf(st, f"m1_raw{i}", [P, WCOLS]) for i in range(2)]
        w_hi = [sbuf(st, f"m1_hi{i}", [P, WCOLS], F32R) for i in range(2)]
        w_lo = [sbuf(st, f"m1_lo{i}", [P, WCOLS], F32R) for i in range(2)]
        slope = sbuf(st, "m1_slope", [P, CW])
        leaky = sbuf(st, "m1_leaky", [P, CW])
        h = [sbuf(st, f"m1_h{i}", [P, CW]) for i in range(2)]
        h_hi = [sbuf(st, f"m1_h_hi{i}", [P, CW], F32R) for i in range(2)]
        h_lo = [sbuf(st, f"m1_h_lo{i}", [P, CW], F32R) for i in range(2)]
        g_ps = [psum(st, f"m1_g_ps{i}", [P, CW]) for i in range(2)]
        u_ps = [psum(st, f"m1_u_ps{i}", [P, CW]) for i in range(2)]
        o_ps = [psum(st, f"m1_o_ps{i}", [P, 4, D]) for i in range(2)]
        w_in = [sem(f"m1_w_in{i}") for i in range(2)]
        w_hi_ready, w_lo_ready = sem("m1_w_hi_ready"), sem("m1_w_lo_ready")
        up_ready, slope_ready, leaky_ready, h_ready, h_hi_ready, h_lo_ready = (
            sem(f"m1_{n}") for n in ("up_ready", "slope_ready", "leaky_ready", "h_ready", "h_hi_ready", "h_lo_ready"))
        down_ready, added = sem("m1_down_ready"), sem("m1_added")
        STEPS = 8

        def experts(eng, body):
            with eng.Fori(0, LAST) as ep:
                body(ep)
            body(LAST)

        def final(ep):
            return isinstance(ep, int) and ep == LAST

        with nc.Block() as block:
            @block.sync
            def _(sp):
                sp.dma_start(w_raw[0][:], aps["m1_w"][0]).then_inc(w_in[0], 16)

                def body(ep):
                    for i in range(2):
                        if i and final(ep):
                            continue
                        e = 2 * ep + 1 + i
                        sp.wait_ge(w_lo_ready, 2 * ep + 1)
                        sp.dma_start(w_raw[1 - i][:], aps["m1_w"][e]).then_inc(w_in[1 - i], 16)
                experts(sp, body)

            @block.scalar
            def _(act):
                def split(i, loads, steps_done):
                    act.wait_ge(w_in[i], 16 * loads)
                    wait(act, down_ready, steps_done)
                    act.activation(w_hi[i][:], w_raw[i][:], ACT.Copy).then_inc(w_hi_ready, 1)

                def slopes(j, i):
                    act.wait_ge(up_ready, j + 1)
                    wait(act, leaky_ready, j)
                    act.activation(slope[:], g_ps[i][:], ACT.Copy, scale=LEAKY).then_inc(slope_ready, 1)

                split(0, 1, 0)
                slopes(0, 0)
                act.wait_ge(h_ready, 1)
                act.activation(h_hi[0][:], h[0][:], ACT.Copy).then_inc(h_hi_ready, 1)

                def body(ep):
                    for s in range(STEPS):
                        if s == 1:
                            split(1, ep + 1, STEPS * ep + 1)
                        if s == 5 and not final(ep):
                            split(0, ep + 2, STEPS * ep + 4)
                        if s == STEPS - 1 and final(ep):
                            continue
                        j = STEPS * ep + s + 1
                        slopes(j, (s + 1) % 2)
                        act.wait_ge(down_ready, STEPS * ep + max(s, 1))
                        act.wait_ge(h_ready, j + 1)
                        act.activation(h_hi[(s + 1) % 2][:], h[(s + 1) % 2][:], ACT.Copy).then_inc(h_hi_ready, 1)
                experts(act, body)

            @block.vector
            def _(dve):
                def split(i, n):
                    dve.wait_ge(w_hi_ready, n)
                    dve.tensor_tensor(w_lo[i][:], w_raw[i][:], w_hi[i][:].bitcast(F32), ALU.subtract).then_inc(w_lo_ready, 1)

                def hidden(j, i):
                    dve.wait_ge(slope_ready, j + 1)
                    dve.tensor_tensor(leaky[:], slope[:], g_ps[i][:], ALU.max).then_inc(leaky_ready, 1)
                    dve.wait_ge(leaky_ready, j + 1)
                    dve.tensor_tensor(h[i][:], leaky[:], u_ps[i][:], ALU.mult).then_inc(h_ready, 1)

                def low(j, i):
                    dve.wait_ge(h_hi_ready, j + 1)
                    dve.tensor_tensor(h_lo[i][:], h[i][:], h_hi[i][:].bitcast(F32), ALU.subtract).then_inc(h_lo_ready, 1)

                dve.memset(yacc[:], 0.0).then_inc(added, 2)
                split(0, 1)
                hidden(0, 0)
                low(0, 0)

                def body(ep):
                    for s in range(STEPS):
                        if s == 1:
                            split(1, 2 * ep + 2)
                        if s == 5 and not final(ep):
                            split(0, 2 * ep + 3)
                        more = not (s == STEPS - 1 and final(ep))
                        if more:
                            hidden(STEPS * ep + s + 1, (s + 1) % 2)
                        dve.wait_ge(added, STEPS * ep + max(s - 1, 2))
                        dve.wait_ge(down_ready, STEPS * ep + s + 1)
                        for t in range(4):
                            n = 4 * (s % 4) + t
                            last = dve.scalar_tensor_tensor(yacc[:, n, :], o_ps[s % 2][:, t, :], gates[:, n, bass.ds(2 * ep + s // 4, 1)],
                                                            yacc[:, n, :], ALU.mult, ALU.add)
                        last.then_inc(added, 1)
                        if more:
                            low(STEPS * ep + s + 1, (s + 1) % 2)
                experts(dve, body)

            @block.tensor
            def _(pe):
                def up(j, e, s):
                    i, x = (s // 4) % 2, slice(CW * (s % 4), CW * (s % 4) + CW)
                    pe.wait_ge(w_lo_ready, e + 1)
                    for ps, first in ((g_ps[s % 2], 0), (u_ps[s % 2], M1)):
                        for c in range(DC):
                            cols = slice(GU * c + first, GU * c + first + M1)
                            pe.matmul(ps[:], w_hi[i][:, cols], xT_hi[:, c, x], start=(c == 0), stop=False)
                            pe.matmul(ps[:], w_hi[i][:, cols], xT_lo[:, c, x], start=False, stop=False)
                            last = pe.matmul(ps[:], w_lo[i][:, cols], xT_hi[:, c, x], start=False, stop=(c == DC - 1))
                    last.then_inc(up_ready, 1)

                def down(j, s):
                    i = s // 4
                    cols = slice(DC * GU, WCOLS)
                    pe.wait_ge(added, j + 1)
                    pe.wait_ge(h_lo_ready, j + 1)
                    for t in range(4):
                        rows = slice(P * t, P * t + P)
                        pe.matmul(o_ps[s % 2][:, t, :], h_hi[s % 2][:, rows], w_hi[i][:, cols], start=True, stop=False)
                        pe.matmul(o_ps[s % 2][:, t, :], h_hi[s % 2][:, rows], w_lo[i][:, cols], start=False, stop=False)
                        last = pe.matmul(o_ps[s % 2][:, t, :], h_lo[s % 2][:, rows], w_hi[i][:, cols], start=False, stop=True)
                    last.then_inc(down_ready, 1)

                up(0, 0, 0)

                def body(ep):
                    for s in range(STEPS):
                        j = STEPS * ep + s
                        if not (s == STEPS - 1 and final(ep)):
                            up(j + 1, 2 * ep + (s + 1) // 4, s + 1)
                        down(j, s)
                experts(pe, body)


def pair_attention_stage(nc, sbuf, psum, sem, aps, keep):
    xs, yacc, ident, xT_hi, xT_lo, gates, power4 = keep
    with ExitStack() as st:
        ln_w = [sbuf(st, f"ln{i}_w", [P, DC]) for i in (1, 2)]
        ln_b = [sbuf(st, f"ln{i}_b", [P, DC]) for i in (1, 2)]
        w_qkv = sbuf(st, "w_qkv", [P, DC, QKV])
        w_proj = sbuf(st, "w_proj", [P, DC, D])
        w_router = sbuf(st, "w_router", [P, DC, E])
        order = sbuf(st, "pa_order", [P, E, E])
        stats = [sbuf(st, f"pa_stats{r}", [P, 4, 6]) for r in range(2)]
        mv = [sbuf(st, f"pa_mv{r}", [P, 4, 2]) for r in range(2)]
        rstd = [sbuf(st, f"pa_rstd{r}", [P, 4]) for r in range(2)]
        xh = [sbuf(st, f"pa_xh{r}", [P, 4, D]) for r in range(2)]
        lT = [sbuf(st, f"pa_lT{r}", [P, DC, CW]) for r in range(2)]
        qkv_sb = [sbuf(st, f"pa_qkv{r}", [P, 4, QKV]) for r in range(2)]
        prod = sbuf(st, "pa_prod", [P, 2, 2, H, HD])
        score = [sbuf(st, f"pa_score{r}", [P, 2, 2, H]) for r in range(2)]
        peak = [sbuf(st, f"pa_peak{r}", [P, 2, H]) for r in range(2)]
        attn = [sbuf(st, f"pa_attn{r}", [P, 4, D]) for r in range(2)]
        attnT = [sbuf(st, f"pa_attnT{r}", [P, DC, CW]) for r in range(2)]
        ha = [sbuf(st, f"pa_ha{r}", [P, 4, D]) for r in range(2)]
        gate = [sbuf(st, f"pa_gate{r}", [P, 4, E]) for r in range(2)]
        row = [sbuf(st, f"pa_row{r}", [P, 4]) for r in range(2)]
        above = sbuf(st, "pa_above", [P, 4, E, E])
        same = sbuf(st, "pa_same", [P, 4, E, E])
        rank = sbuf(st, "pa_rank", [P, 4, E])
        x_ps = [psum(st, f"pa_x_ps{c}", [P, CW]) for c in range(DC)]
        q_ps = [psum(st, f"pa_q_ps{j}", [P, CW]) for j in range(4)]
        p_ps = psum(st, "pa_p_ps", [P, 4, D])
        logits = [p_ps[:, 2 * r, 0:4 * E].rearrange("p (j e) -> p j e", e=E) for r in range(2)]
        names = ("loaded step var_ready rstd_ready xh_ready turned lT_ready qkv_ready qkv_read prod_ready first_ready scores_ready "
                 "exp_ready attn_ready attnT_ready proj_ready ha_ready summed hi_ready lo_ready logits_ready logits_read gate_exp_ready").split()
        (loaded, step, var_ready, rstd_ready, xh_ready, turned, lT_ready, qkv_ready, qkv_read, prod_ready, first_ready, scores_ready,
         exp_ready, attn_ready, attnT_ready, proj_ready, ha_ready, summed, hi_ready, lo_ready, logits_ready, logits_read,
         gate_exp_ready) = (sem("pa_" + n) for n in names)
        marks = sem("pa_marks")
        LOADS = 16 * 8
        PER_BODY = 38
        POS = QT // 4

        def group_tiles(tiles, it, r):
            return tiles[:].rearrange("p (b i) d -> p b i d", b=B)[:, :, bass.ds(4 * it + 2 * r, 2), :]

        def tile(it, r, j):
            return bass.ds(D * (4 * it + QT * (j // 2) + 2 * r + j % 2), D)

        def heads(ap):
            return ap.rearrange("p (k d) -> p k d", d=HD).unsqueeze(2).broadcast_to([P, KV, H // KV, HD])

        def by_kv(ap):
            return ap.rearrange("p (k r d) -> p k r d", k=KV, d=HD)

        def per_head(ap):
            return ap.rearrange("p (k r) -> p k r", k=KV).unsqueeze(3).broadcast_to([P, KV, H // KV, HD])

        def qkv(r, b, i, part):
            first, last = ((0, D), (D, D + KV * HD), (D + KV * HD, QKV))[part]
            return qkv_sb[r][:, 2 * b + i, first:last]

        with nc.Block() as block:
            @block.sync
            def _(sp):
                for i in range(2):
                    sp.dma_start(ln_w[i][:], aps[f"ln{i + 1}_w"]).then_inc(loaded, 16)
                    sp.dma_start(ln_b[i][:], aps[f"ln{i + 1}_b"]).then_inc(loaded, 16)
                sp.dma_start(w_qkv[:], aps["qkvT"].rearrange("(c p) o -> p c o", p=P)).then_inc(loaded, 16)
                sp.dma_start(w_proj[:], aps["projT"].rearrange("(c p) o -> p c o", p=P)).then_inc(loaded, 16)
                sp.dma_start(w_router[:], aps["routerT"].rearrange("(c p) e -> p c e", p=P)).then_inc(loaded, 16)
                sp.dma_start(order[:], aps["order"].broadcast_to([P, E * E])).then_inc(loaded, 16)

            @block.gpsimd
            def _(pool):
                pool.sem_inc(summed, 1)
                with pool.Fori(0, POS) as it:
                    for norm in range(2):
                        for r in range(2):
                            pool.wait_ge(var_ready, 4 * it + 2 * norm + r + 1)
                            pool.tensor_tensor(rstd[r][:], rstd[r][:], power4, ALU.pow).then_inc(rstd_ready, 1)
                    for r in range(2):
                        pool.wait_ge(ha_ready, 2 * it + r + 1)
                        pool.tensor_tensor(group_tiles(xs, it, r), group_tiles(xs, it, r),
                                           ha[r][:].rearrange("p (b i) d -> p b i d", b=B), ALU.add).then_inc(summed, 1)

            @block.vector
            def _(dve):
                yacc_f = flat(yacc)
                dve.wait_ge(loaded, LOADS)
                with dve.Fori(0, POS) as it:
                    steps = Steps(PER_BODY)
                    dve.wait_ge(gate_exp_ready, 2 * it + 1)
                    dve.wait_ge(summed, 2 * it + 1)

                    def moments(source, r):
                        for j in range(4):
                            last = dve.bn_stats(stats[r][:, j, :], source(j))
                        last.then_inc(step, steps.up())
                        dve.wait_ge(step, steps.here(it))
                        apart(dve, marks)
                        for j in range(4):
                            last = dve.bn_aggr(mv[r][:, j, :], stats[r][:, j, :])
                        last.then_inc(step, steps.up())
                        dve.wait_ge(step, steps.here(it))
                        dve.tensor_scalar(rstd[r][:], mv[r][:, :, 1], EPS, None, ALU.add).then_inc(var_ready, 1)

                    def normalise(source, r, norm):
                        dve.wait_ge(rstd_ready, 4 * it + 2 * norm + r + 1)
                        for j in range(4):
                            last = dve.tensor_scalar(xh[r][:, j, :], source(j), mv[r][:, j, 0:1], rstd[r][:, j:j + 1],
                                                     ALU.subtract, ALU.mult)
                        last.then_inc(xh_ready, 1)

                    for r in range(2):
                        moments(lambda j: yacc_f[:, tile(it, r, j)], r)
                    for r in range(2):
                        normalise(lambda j: yacc_f[:, tile(it, r, j)], r, 0)
                    for r in range(2):
                        if r:
                            dve.wait_ge(attn_ready, 2 * it + r)
                        dve.wait_ge(qkv_read, 2 * it + r + 1)
                        for i in range(2):
                            for b in range(B):
                                last = dve.tensor_tensor(prod[:, i, b].rearrange("p (k r) d -> p k r d", k=KV),
                                                         by_kv(qkv(r, 1, i, 0)), heads(qkv(r, b, i, 1)), ALU.mult)
                        last.then_inc(step, steps.up())
                        dve.wait_ge(step, steps.here(it))
                        dve.tensor_reduce(score[r][:], prod[:], AX.X, ALU.add).then_inc(step, steps.up())
                        dve.wait_ge(step, steps.here(it))
                        dve.tensor_tensor(peak[r][:], score[r][:, :, 0, :], score[r][:, :, 1, :], ALU.max).then_inc(step, steps.up())
                        dve.wait_ge(step, steps.here(it))
                        dve.tensor_tensor(score[r][:], score[r][:], peak[r][:].unsqueeze(2).broadcast_to([P, 2, 2, H]),
                                          ALU.subtract).then_inc(scores_ready, 1)
                        dve.wait_ge(exp_ready, 2 * it + r + 1)
                        dve.tensor_tensor(peak[r][:], score[r][:, :, 0, :], score[r][:, :, 1, :], ALU.add).then_inc(step, steps.up())
                        dve.wait_ge(step, steps.here(it))
                        dve.reciprocal(peak[r][:], peak[r][:]).then_inc(step, steps.up())
                        dve.wait_ge(step, steps.here(it))
                        dve.tensor_tensor(score[r][:], score[r][:], peak[r][:].unsqueeze(2).broadcast_to([P, 2, 2, H]),
                                          ALU.mult).then_inc(step, steps.up())
                        dve.wait_ge(step, steps.here(it))
                        for i in range(2):
                            for b in range(B):
                                last = dve.tensor_tensor(prod[:, i, b].rearrange("p (k r) d -> p k r d", k=KV),
                                                         heads(qkv(r, b, i, 2)), per_head(score[r][:, i, b]), ALU.mult)
                        last.then_inc(prod_ready, 1)
                        dve.wait_ge(prod_ready, 2 * it + r + 1)
                        dve.tensor_tensor(attn[r][:, 2:4, :], prod[:, :, 0].rearrange("p i h d -> p i (h d)"),
                                          prod[:, :, 1].rearrange("p i h d -> p i (h d)"), ALU.add).then_inc(attn_ready, 1)
                    for r in range(2):
                        dve.wait_ge(proj_ready, 2 * it + r + 1)
                        dve.tensor_tensor(ha[r][:].rearrange("p (b i) d -> p b i d", b=B),
                                          p_ps[:].rearrange("p (b i) d -> p b i d", b=B),
                                          group_tiles(yacc, it, r), ALU.add).then_inc(ha_ready, 1)
                        dve.wait_ge(ha_ready, 2 * it + r + 1)
                        moments(lambda j: ha[r][:, j, :], r)
                    for r in range(2):
                        normalise(lambda j: ha[r][:, j, :], r, 1)
                    for r in range(2):
                        for c in range(DC):
                            dve.wait_ge(hi_ready, 2 * DC * it + DC * r + c + 1)
                            cols = bass.ds(2 * CW * it + CW * r, CW)
                            last = dve.tensor_tensor(xT_lo[:, c, cols], lT[r][:, c, :], xT_hi[:, c, cols].bitcast(F32), ALU.subtract)
                        last.then_inc(lo_ready, 1)
                    for r in range(2):
                        dve.wait_ge(logits_ready, 2 * it + r + 1)
                        dve.tensor_reduce(row[r][:], logits[r], AX.X, ALU.max).then_inc(step, steps.up())
                        dve.wait_ge(step, steps.here(it))
                        dve.tensor_tensor(gate[r][:], logits[r], row[r][:].unsqueeze(2).broadcast_to([P, 4, E]),
                                          ALU.subtract).then_inc(logits_read, 1)
                    for r in range(2):
                        dve.wait_ge(gate_exp_ready, 2 * it + r + 2)
                        dve.tensor_reduce(row[r][:], gate[r][:], AX.X, ALU.add).then_inc(step, steps.up())
                        dve.wait_ge(step, steps.here(it))
                        dve.reciprocal(row[r][:], row[r][:]).then_inc(step, steps.up())
                        dve.wait_ge(step, steps.here(it))
                        dve.tensor_tensor(gate[r][:], gate[r][:], row[r][:].unsqueeze(2).broadcast_to([P, 4, E]),
                                          ALU.mult).then_inc(step, steps.up())
                        dve.wait_ge(step, steps.here(it))
                        gate_top_two(dve, step, steps, it, gate[r][:], (above[:], same[:], order[:], rank[:]),
                                     gates[:, bass.ds(8 * it + 4 * r, 4), :]).then_inc(step, steps.up())
                    assert steps.n == PER_BODY, steps.n

            @block.scalar
            def _(act):
                act.wait_ge(loaded, LOADS)
                act.sem_inc(gate_exp_ready, 1)
                with act.Fori(0, POS) as it:
                    def evacuate(r, norm, out, n):
                        for c in range(DC):
                            act.wait_ge(turned, 6 * DC * it + n + DC * r + c + 1)
                            if norm is None:
                                act.activation(out[r][:, c, :], x_ps[c][:], ACT.Copy).then_inc(attnT_ready, 1)
                            else:
                                act.activation(out[r][:, c, :], x_ps[c][:], ACT.Identity, scale=ln_w[norm][:, c:c + 1],
                                               bias=ln_b[norm][:, c:c + 1]).then_inc(lT_ready, 1)

                    for r in range(2):
                        evacuate(r, 0, lT, 0)
                    for r in range(2):
                        act.wait_ge(qkv_ready, 2 * it + r + 1)
                        for j in range(4):
                            last = act.activation(qkv_sb[r][:, j, :], q_ps[j][:, 0:QKV], ACT.Copy)
                        last.then_inc(qkv_read, 1)
                        act.wait_ge(qkv_read, 2 * it + r + 1)
                        for i in range(2):
                            last = act.activation(by_kv(attn[r][:, i, :]), heads(qkv(r, 0, i, 2)), ACT.Copy)
                        last.then_inc(first_ready, 1)
                        act.wait_ge(scores_ready, 2 * it + r + 1)
                        act.activation(score[r][:], score[r][:], ACT.Exp, scale=HD ** -0.5).then_inc(exp_ready, 1)
                    for r in range(2):
                        evacuate(r, None, attnT, 2 * DC)
                    for r in range(2):
                        act.wait_ge(qkv_ready, 2 * it + 2)
                        evacuate(r, 1, lT, 4 * DC)
                        for c in range(DC):
                            act.wait_ge(lT_ready, 4 * DC * it + 2 * DC + DC * r + c + 1)
                            act.activation(xT_hi[:, c, bass.ds(2 * CW * it + CW * r, CW)], lT[r][:, c, :],
                                           ACT.Copy).then_inc(hi_ready, 1)
                    for r in range(2):
                        act.wait_ge(logits_read, 2 * it + r + 1)
                        act.activation(gate[r][:], gate[r][:], ACT.Exp).then_inc(gate_exp_ready, 1)

            @block.tensor
            def _(pe):
                pe.wait_ge(loaded, LOADS)
                with pe.Fori(0, POS) as it:
                    def turn(source, r, read):
                        for c in range(DC):
                            if read(c):
                                pe.wait_ge(*read(c))
                            for j in range(4):
                                last = pe.transpose(x_ps[c][:, P * j:P * j + P], source[r][:, j, P * c:P * c + P], ident)
                            last.then_inc(turned, 1)

                    for r in range(2):
                        pe.wait_ge(xh_ready, 4 * it + r + 1)
                        turn(xh, r, lambda c: (lT_ready, 4 * DC * it + c + 1) if r else None)
                    for r in range(2):
                        if r:
                            pe.wait_ge(qkv_read, 2 * it + r)
                        pe.wait_ge(lT_ready, 4 * DC * it + DC * (r + 1))
                        for j in range(4):
                            for c in range(DC):
                                last = pe.matmul(q_ps[j][:, 0:QKV], lT[r][:, c, P * j:P * j + P], w_qkv[:, c, :],
                                                 start=(c == 0), stop=(c == DC - 1))
                        last.then_inc(qkv_ready, 1)
                    for r in range(2):
                        pe.wait_ge(first_ready, 2 * it + r + 1)
                        pe.wait_ge(attn_ready, 2 * it + r + 1)
                        turn(attn, r, lambda c: (attnT_ready, 2 * DC * it + DC * (r - 1) + c + 1) if r else
                             (lT_ready, 4 * DC * it + DC + c + 1))
                    for r in range(2):
                        if r:
                            pe.wait_ge(ha_ready, 2 * it + r)
                        pe.wait_ge(attnT_ready, 2 * DC * it + DC * (r + 1))
                        for j in range(4):
                            for c in range(DC):
                                last = pe.matmul(p_ps[:, j, :], attnT[r][:, c, P * j:P * j + P], w_proj[:, c, :],
                                                 start=(c == 0), stop=(c == DC - 1))
                        last.then_inc(proj_ready, 1)
                    for r in range(2):
                        pe.wait_ge(xh_ready, 4 * it + 2 + r + 1)
                        turn(xh, r, lambda c: (lT_ready, 4 * DC * it + 2 * DC + c + 1) if r else
                             (attnT_ready, 2 * DC * it + DC + c + 1))
                    for r in range(2):
                        pe.wait_ge(lT_ready, 4 * DC * it + 2 * DC + DC * (r + 1))
                        for j in range(4):
                            for c in range(DC):
                                last = pe.matmul(logits[r][:, j, :], lT[r][:, c, P * j:P * j + P],
                                                 w_router[:, c, :], start=(c == 0), stop=(c == DC - 1))
                        last.then_inc(logits_ready, 1)


def second_mixture_stage(nc, sbuf, psum, sem, aps, keep):
    xs, xT_hi, xT_lo, gates, out = keep
    FC = F2 // P
    W1 = DC * F2
    WCOLS = W1 + FC * D
    LAST = E // 2 - 1
    STEPS = 8
    with ExitStack() as st:
        w_raw = [sbuf(st, f"m2_raw{i}", [P, WCOLS]) for i in range(2)]
        w_hi = [sbuf(st, f"m2_hi{i}", [P, WCOLS], F32R) for i in range(2)]
        w_lo = [sbuf(st, f"m2_lo{i}", [P, WCOLS], F32R) for i in range(2)]
        h = sbuf(st, "m2_h", [P, FC, CW])
        h_hi = [sbuf(st, f"m2_h_hi{i}", [P, FC, CW], F32R) for i in range(2)]
        h_lo = [sbuf(st, f"m2_h_lo{i}", [P, FC, CW], F32R) for i in range(2)]
        u_ps = [psum(st, f"m2_u_ps{f}", [P, CW]) for f in range(FC)]
        o_ps = [psum(st, f"m2_o_ps{i}", [P, 4, D]) for i in range(2)]
        w_in = [sem(f"m2_w_in{i}") for i in range(2)]
        w_hi_ready, w_lo_ready = sem("m2_w_hi_ready"), sem("m2_w_lo_ready")
        up_ready, h_ready, h_hi_ready, h_lo_ready = (sem(f"m2_{n}") for n in ("up_ready", "h_ready", "h_hi_ready", "h_lo_ready"))
        down_ready, added, stored = sem("m2_down_ready"), sem("m2_added"), sem("stored")

        def experts(eng, body):
            with eng.Fori(0, LAST) as ep:
                body(ep)
            body(LAST)

        def final(ep):
            return isinstance(ep, int) and ep == LAST

        with nc.Block() as block:
            @block.sync
            def _(sp):
                sp.dma_start(w_raw[0][:], aps["m2_w"][0]).then_inc(w_in[0], 16)

                def body(ep):
                    for i in range(2):
                        if i and final(ep):
                            continue
                        e = 2 * ep + 1 + i
                        sp.wait_ge(w_lo_ready, 2 * ep + 1)
                        sp.dma_start(w_raw[1 - i][:], aps["m2_w"][e]).then_inc(w_in[1 - i], 16)
                experts(sp, body)
                rows = out.rearrange("(b i p) d -> p b i d", b=B, p=P)
                for g in range(4):
                    sp.wait_ge(added, STEPS * LAST + 4 + g + 3)
                    for b in range(B):
                        sp.dma_start(rows[:, b, 2 * g:2 * g + 2, :],
                                     xs[:, QT * b + 2 * g:QT * b + 2 * g + 2, :]).then_inc(stored, 16)
                sp.wait_ge(stored, 16 * 4 * B)

            @block.scalar
            def _(act):
                def split(i, loads, steps_done):
                    act.wait_ge(w_in[i], 16 * loads)
                    wait(act, down_ready, steps_done)
                    act.activation(w_hi[i][:], w_raw[i][:], ACT.Copy).then_inc(w_hi_ready, 1)

                def hidden(j, i, multiplied):
                    for f in range(FC):
                        act.wait_ge(up_ready, FC * j + f + 1)
                        wait(act, h_lo_ready, FC * (j - 1) + f + 1)
                        act.activation(h[:, f, :], u_ps[f][:], ACT.Gelu_apprx_tanh).then_inc(h_ready, 1)
                        if f == 0:
                            wait(act, down_ready, multiplied)
                        act.wait_ge(h_ready, FC * j + f + 1)
                        act.activation(h_hi[i][:, f, :], h[:, f, :], ACT.Copy).then_inc(h_hi_ready, 1)

                split(0, 1, 0)
                hidden(0, 0, 0)

                def body(ep):
                    for s in range(STEPS):
                        if s == 1:
                            split(1, ep + 1, STEPS * ep + 1)
                        if s == 5 and not final(ep):
                            split(0, ep + 2, STEPS * ep + 4)
                        if not (s == STEPS - 1 and final(ep)):
                            hidden(STEPS * ep + s + 1, (s + 1) % 2, STEPS * ep + max(s, 1))
                experts(act, body)

            @block.vector
            def _(dve):
                def split(i, n):
                    dve.wait_ge(w_hi_ready, n)
                    dve.tensor_tensor(w_lo[i][:], w_raw[i][:], w_hi[i][:].bitcast(F32), ALU.subtract).then_inc(w_lo_ready, 1)

                def low(j, i):
                    for f in range(FC):
                        dve.wait_ge(h_hi_ready, FC * j + f + 1)
                        dve.tensor_tensor(h_lo[i][:, f, :], h[:, f, :], h_hi[i][:, f, :].bitcast(F32),
                                          ALU.subtract).then_inc(h_lo_ready, 1)

                split(0, 1)
                dve.sem_inc(added, 2)
                low(0, 0)

                def body(ep):
                    for s in range(STEPS):
                        if s == 1:
                            split(1, 2 * ep + 2)
                        if s == 5 and not final(ep):
                            split(0, 2 * ep + 3)
                        if not (s == STEPS - 1 and final(ep)):
                            low(STEPS * ep + s + 1, (s + 1) % 2)
                        dve.wait_ge(added, STEPS * ep + max(s - 1, 2))
                        dve.wait_ge(down_ready, STEPS * ep + s + 1)
                        for j in range(4):
                            g = s % 4
                            n = QT * (j // 2) + 2 * g + j % 2
                            last = dve.scalar_tensor_tensor(xs[:, n, :], o_ps[s % 2][:, j, :], gates[:, 4 * g + j, bass.ds(2 * ep + s // 4, 1)],
                                                            xs[:, n, :], ALU.mult, ALU.add)
                        last.then_inc(added, 1)
                experts(dve, body)

            @block.tensor
            def _(pe):
                def up(j, e, s):
                    i, x = (s // 4) % 2, slice(CW * (s % 4), CW * (s % 4) + CW)
                    pe.wait_ge(w_lo_ready, e + 1)
                    for f in range(FC):
                        wait(pe, h_ready, FC * (j - 1) + f + 1)
                        for c in range(DC):
                            cols = slice(F2 * c + P * f, F2 * c + P * f + P)
                            pe.matmul(u_ps[f][:], w_hi[i][:, cols], xT_hi[:, c, x], start=(c == 0), stop=False)
                            pe.matmul(u_ps[f][:], w_hi[i][:, cols], xT_lo[:, c, x], start=False, stop=False)
                            last = pe.matmul(u_ps[f][:], w_lo[i][:, cols], xT_hi[:, c, x], start=False, stop=(c == DC - 1))
                        last.then_inc(up_ready, 1)

                def down(j, s):
                    i = s // 4
                    pe.wait_ge(added, j + 1)
                    pe.wait_ge(h_lo_ready, FC * (j + 1))
                    for t in range(4):
                        rows = slice(P * t, P * t + P)
                        for f in range(FC):
                            cols = slice(W1 + D * f, W1 + D * f + D)
                            pe.matmul(o_ps[s % 2][:, t, :], h_hi[s % 2][:, f, rows], w_hi[i][:, cols], start=(f == 0), stop=False)
                            pe.matmul(o_ps[s % 2][:, t, :], h_hi[s % 2][:, f, rows], w_lo[i][:, cols], start=False, stop=False)
                            last = pe.matmul(o_ps[s % 2][:, t, :], h_lo[s % 2][:, f, rows], w_hi[i][:, cols],
                                             start=False, stop=(f == FC - 1))
                    last.then_inc(down_ready, 1)

                up(0, 0, 0)

                def body(ep):
                    for s in range(STEPS):
                        j = STEPS * ep + s
                        if not (s == STEPS - 1 and final(ep)):
                            up(j + 1, 2 * ep + (s + 1) // 4, s + 1)
                        down(j, s)
                experts(pe, body)


TILES = [t for j in range(QT // 2) for _ in range(B) for t in (QT - 1 - j, j)]
LATE_TILES = range(QT // 4, 3 * QT // 4)


class Unit:

    def __init__(self, u):
        self.u = u
        self.tile = TILES[u]
        self.batch = u // 2 % B
        self.round = u // 4
        self.short = u % 2
        self.half = 0 if self.tile in LATE_TILES else 1
        place = self.tile - QT // 4 if self.half == 0 else self.tile if self.tile < QT // 4 else self.tile - QT // 2
        self.query = S * self.batch + CW * self.half + P * place
        self.blocks = self.tile + 1
        self.chunks = [(c * 4, min(4, self.blocks - c * 4)) for c in range((self.blocks + 3) // 4)]
        two = 2 if self.blocks != 2 else 1
        self.slots = [(k, min(two, self.blocks - k)) for k in range(0, self.blocks, two)]


class Slot:

    def __init__(self, u, first, n, start):
        self.u, self.first, self.n, self.start = u, first, n, start


UNITS = QT * B
BODY = [Unit(u) for u in range(UNITS)]
FIRST_CHUNK = [sum(2 * len(x.chunks) for x in BODY[:u]) for u in range(UNITS + 1)]
SCORES = FIRST_CHUNK[UNITS]
FIRST_SLOT = [sum(len(x.slots) for x in BODY[:u]) for u in range(UNITS + 1)]
FIRST_BLOCK = [sum(x.blocks for x in BODY[:u]) for u in range(UNITS + 1)]
SLOTS = [Slot(x.u, k, n, FIRST_BLOCK[x.u] + k) for x in BODY for k, n in x.slots]
NS = len(SLOTS)
ROW_BLOCKS = (QT, QT, QT // 2, QT // 2)
ROW_BUFFER = (0, 2, 1, 3) * (UNITS // 4)
LEAD = 14
CHUNKS_AT = [[] for _ in range(NS)]
EXPS_AT = [[] for _ in range(NS)]
for _x in BODY:
    _rows = len(_x.chunks)
    for _i in range(2 * _rows):
        _block = FIRST_BLOCK[_x.u] + _x.blocks * _i / (2 * _rows) - LEAD
        _unit = _x.u if _block >= 0 else _x.u + UNITS
        _slot = max(t for t in range(NS) if SLOTS[t].start <= _block % FIRST_BLOCK[UNITS])
        CHUNKS_AT[_slot].append((_unit, _i))
        if _i % _rows == _rows - 1:
            EXPS_AT[(_slot + 1) % NS].append((_unit - UNITS * ((_slot + 1) // NS), _i // _rows))

QUERIES_AT = {4: (0, 2), 14: (1, 1), 20: (2, 3), 40: (3, 0)}
PROJECT_AT = {}
_t = -3
for _u in range(-2, UNITS - 2):
    _t = max(_t + 2, FIRST_SLOT[_u % UNITS + 1] + 1 - (NS if _u < 0 else 0))
    _t += _t % 2
    while _t in QUERIES_AT:
        _t += 2
    PROJECT_AT[_t] = _u
assert max(PROJECT_AT) < NS and min(PROJECT_AT) >= 0


def apart(eng, marks):
    eng.sem_inc(marks, 1)


def wait(eng, sem, value):
    if isinstance(value, int) and value <= 0:
        return
    eng.wait_ge(sem, value)


def program(nc, x, bias, cond, mask, g_in, nab, Wq, Wkv, Wo, out, **aps):
    outer = ExitStack()
    with outer:
        def sbuf(stack, name, shape, dt=F32):
            return stack.enter_context(nc.sbuf_tensor(name, shape, dt))

        def psum(stack, name, shape, dt=F32):
            return stack.enter_context(nc.psum_tensor(name, shape, dt))

        def sem(name):
            return outer.enter_context(nc.semaphore(name))

        xs = sbuf(outer, "xs", [P, NT, D])
        ident = sbuf(outer, "ident", [P, P])
        yacc = sbuf(outer, "yacc", [P, NT, D])

        attn = ExitStack()
        xnT = sbuf(attn, "xnT", [P, DC, T])
        k_hi = sbuf(attn, "k_hi", [P, T], F32R)
        k_lo = sbuf(attn, "k_lo", [P, T], F32R)
        values = sbuf(attn, "values", [P, NT, P], F32R)
        wo = sbuf(attn, "wo", [P, H, D])
        null_wo = sbuf(attn, "null_wo", [H, D])
        neg_null = sbuf(attn, "neg_null", [P, UNITS, H])
        null_w = sbuf(attn, "null_w", [P, UNITS, H])

        with ExitStack() as st:
            xh = sbuf(st, "xh", [P, 4, 4, D])
            mv = sbuf(st, "mv", [P, NT, 2])
            stats = sbuf(st, "stats", [P, NT, 6])
            rstd = sbuf(st, "rstd", [P, NT])
            power = sbuf(st, "power", [P, 4])
            gcol = sbuf(st, "gcol", [P, DC])
            wk = sbuf(st, "wk", [P, DC, P])
            wv = sbuf(st, "wv", [P, DC, DH])
            wq_all = sbuf(st, "wq_all", [P, DC, H, DH])
            nk_b = sbuf(st, "nk_b", [P, DH])
            nab_b = sbuf(st, "nab_b", [P, H])
            nv = sbuf(st, "nv", [DH, 1])
            nv_at = sbuf(st, "nv_at", [DH, H, H])
            nk_prod = sbuf(st, "nk_prod", [P, DC, H, DH])
            w_null = sbuf(st, "w_null", [P, DC, H])
            mask8 = sbuf(st, "mask8", [P, T], U8)
            turn = [psum(st, f"turn{i}", [P, CW]) for i in range(2)]
            kps = [psum(st, f"kps{i}", [P, CW]) for i in range(2)]
            vps = [psum(st, f"vps{i}", [P, QT, DH]) for i in range(B)]
            nps = psum(st, "nps", [P, CW])
            null_ps = nps[:, 0:UNITS * H].rearrange("p (u h) -> p u h", h=H)
            nwps = psum(st, "nwps", [P, CW])
            x_in = [sem(f"x_in{g}") for g in range(4)]
            w_in, small_in = sem("w_in"), sem("small_in")
            const_ready, var_ready, rstd_ready = sem("const_ready"), sem("var_ready"), sem("rstd_ready")
            xh_ready, turned, xnT_ready = sem("xh_ready"), sem("turned"), sem("xnT_ready")
            k_ready, khi_ready, klo_ready, v_ready, v_out = (sem(n) for n in ("k_ready", "khi_ready", "klo_ready", "v_ready", "v_out"))
            wq_all_in, wo_in, nv_ready, w_null_ready, null_ready, null_wo_ready = (
                sem(n) for n in ("wq_all_in", "wo_in", "nv_ready", "w_null_ready", "null_ready", "null_wo_ready"))
            step0 = sem("step0")
            zeroed = sem("zeroed")
            with nc.Block() as block:
                @block.sync
                def _(sp):
                    xt = x.rearrange("(t p) d -> p t d", p=P)
                    for g in range(4):
                        sp.dma_start(xs[:, 4 * g:4 * g + 4, :], xt[:, 4 * g:4 * g + 4, :]).then_inc(x_in[g], 16)
                    wkv = Wkv.rearrange("(c p) n -> p c n", p=P)
                    sp.dma_start(wk[:, :, 0:DH], wkv[:, :, 0:DH]).then_inc(w_in, 16)
                    sp.dma_start(wk[:, :, DH:P], wkv[:, :, 0:DH]).then_inc(w_in, 16)
                    sp.dma_start(wv[:], wkv[:, :, DH:2 * DH]).then_inc(w_in, 16)
                    sp.dma_start(wq_all[:].rearrange("p c h d -> p c (h d)"), Wq.rearrange("(c p) n -> p c n", p=P)).then_inc(wq_all_in, 16)
                    wo_h = Wo.rearrange("(h d) n -> d h n", d=DH)
                    for half in range(2):
                        sp.dma_start(wo[DH * half:DH * half + DH, :, :], wo_h).then_inc(wo_in, 16)

                @block.scalar
                def _(act):
                    act.dma_start(gcol[:], g_in).then_inc(small_in, 16)
                    act.dma_start(nk_b[:], cond[0:1, :].broadcast_to([P, DH])).then_inc(small_in, 16)
                    act.dma_start(nv[:], cond[1:2, :].rearrange("o d -> d o")).then_inc(small_in, 16)
                    act.dma_start(nab_b[:], nab.rearrange("(o h) -> o h", o=1).broadcast_to([P, H])).then_inc(small_in, 16)
                    act.dma_start(mask8[DH:DH + 1, :], mask).then_inc(small_in, 16)
                    act.wait_ge(small_in, 16 * 5)
                    for g in range(4):
                        for c in range(DC):
                            act.wait_ge(turned, DC * g + c + 1)
                            act.activation(xnT[:, c, CW * g:CW * g + CW], turn[c][:], ACT.Copy,
                                           scale=gcol[:, c:c + 1]).then_inc(xnT_ready, 1)
                        act.wait_ge(k_ready, g + 1)
                        act.activation(k_hi[:, CW * g:CW * g + CW], kps[g % 2][:], ACT.Copy).then_inc(khi_ready, 1)
                    for b in range(B):
                        act.wait_ge(v_ready, b + 1)
                        act.activation(values[:, QT * b:QT * b + QT, 0:DH], vps[b][:], ACT.Copy).then_inc(v_out, 1)
                    act.wait_ge(null_wo_ready, 1)
                    act.activation(null_wo[:], nwps[0:H, 0:D], ACT.Copy)

                @block.gpsimd
                def _(pool):
                    pool.memset(ident[:], 0.0).then_inc(zeroed, 1)
                    pool.memset(power[:], -0.5).then_inc(const_ready, 1)
                    pool.wait_ge(zeroed, 1)
                    pool.affine_select(out=ident[:], in_=ident[:], compare_op=ALU.not_equal, fill=1.0, base=0,
                                       pattern=[[-1, P]], channel_multiplier=1).then_inc(const_ready, 1)
                    pool.wait_ge(const_ready, 1)
                    for g in range(4):
                        pool.wait_ge(var_ready, g + 1)
                        pool.tensor_tensor(rstd[:, 4 * g:4 * g + 4], rstd[:, 4 * g:4 * g + 4], power[:],
                                           ALU.pow).then_inc(rstd_ready, 1)

                @block.vector
                def _(dve):
                    dve.memset(k_lo[DH:P, :].bitcast(F32), 0.0).then_inc(step0, 1)
                    for g in range(4):
                        dve.wait_ge(x_in[g], 16)
                        for t in range(4 * g, 4 * g + 4):
                            last = dve.bn_stats(stats[:, t, :], xs[:, t, :])
                        last.then_inc(step0, 1)
                        dve.wait_ge(step0, 2 + 2 * g)
                        for t in range(4 * g, 4 * g + 4):
                            last = dve.bn_aggr(mv[:, t, :], stats[:, t, :])
                        last.then_inc(step0, 1)
                        dve.wait_ge(step0, 3 + 2 * g)
                        dve.tensor_scalar(rstd[:, 4 * g:4 * g + 4], mv[:, 4 * g:4 * g + 4, 1], EPS, None,
                                          ALU.add).then_inc(var_ready, 1)
                    for g in range(4):
                        dve.wait_ge(rstd_ready, g + 1)
                        for t in range(4):
                            tt = 4 * g + t
                            last = dve.tensor_scalar(xh[:, g, t, :], xs[:, tt, :], mv[:, tt, 0:1], rstd[:, tt:tt + 1],
                                                     ALU.subtract, ALU.mult)
                        last.then_inc(xh_ready, 1)
                    dve.memset(yacc[:], 0.0).then_inc(step0, 1)
                    dve.wait_ge(small_in, 16 * 5)
                    dve.tensor_scalar(k_lo[DH:DH + 1, 0:T], mask8[DH:DH + 1, :], MASKED, -MASKED, ALU.mult, ALU.add)
                    dve.memset(nv_at[:], 0.0).then_inc(step0, 1)
                    dve.wait_ge(step0, 11)
                    dve.tensor_copy(nv_at[:].rearrange("d a b -> d (a b)")[:, 0:H * H:H + 1],
                                    nv[:].broadcast_to([DH, H])).then_inc(nv_ready, 1)
                    dve.wait_ge(wq_all_in, 16)
                    for c in range(DC):
                        last = dve.tensor_tensor(nk_prod[:, c], wq_all[:, c], nk_b[:].unsqueeze(1).broadcast_to([P, H, DH]), ALU.mult)
                    last.then_inc(step0, 1)
                    dve.wait_ge(step0, 12)
                    dve.tensor_reduce(w_null[:], nk_prod[:], AX.X, ALU.add).then_inc(w_null_ready, 1)
                    for g in range(4):
                        dve.wait_ge(khi_ready, g + 1)
                        cols = slice(CW * g, CW * g + CW)
                        dve.tensor_tensor(k_lo[0:DH, cols], kps[g % 2][0:DH, :], k_hi[0:DH, cols].bitcast(F32),
                                          ALU.subtract).then_inc(klo_ready, 1)
                    for b in range(B):
                        dve.wait_ge(v_out, b + 1)
                        rows = slice(QT * b, QT * b + QT)
                        dve.tensor_tensor(values[:, rows, DH:P], vps[b][:], values[:, rows, 0:DH].bitcast(F32), ALU.subtract)
                    dve.wait_ge(null_ready, 1)
                    dve.scalar_tensor_tensor(neg_null[:], null_ps, -DH ** -0.5, nab_b[:].unsqueeze(1).broadcast_to([P, UNITS, H]),
                                             ALU.mult, ALU.subtract)

                @block.tensor
                def _(pe):
                    pe.wait_ge(const_ready, 2)
                    pe.wait_ge(w_in, 48)
                    for g in range(4):
                        pe.wait_ge(xh_ready, g + 1)
                        for c in range(DC):
                            if g:
                                pe.wait_ge(xnT_ready, DC * (g - 1) + c + 1)
                            for t in range(4):
                                last = pe.transpose(turn[c][:, P * t:P * t + P], xh[:, g, t, P * c:P * c + P], ident[:])
                            last.then_inc(turned, 1)
                        pe.wait_ge(xnT_ready, DC * (g + 1))
                        if g >= 2:
                            pe.wait_ge(klo_ready, g - 1)
                        for c in range(DC):
                            last = pe.matmul(kps[g % 2][:], wk[:, c, :], xnT[:, c, CW * g:CW * g + CW],
                                             start=(c == 0), stop=(c == DC - 1))
                        last.then_inc(k_ready, 1)
                        for t in range(4 * g, 4 * g + 4):
                            for c in range(DC):
                                last = pe.matmul(vps[t // QT][:, t % QT, :], xnT[:, c, P * t:P * t + P], wv[:, c, :],
                                                 start=(c == 0), stop=(c == DC - 1))
                        if g % 2:
                            last.then_inc(v_ready, 1)
                    pe.wait_ge(nv_ready, 1)
                    pe.wait_ge(wo_in, 32)
                    for h in range(H):
                        last = pe.matmul(nwps[0:H, 0:D], nv_at[:, h, :], wo[0:DH, h, :], start=(h == 0), stop=(h == H - 1))
                    last.then_inc(null_wo_ready, 1)
                    pe.wait_ge(w_null_ready, 1)
                    for x in BODY:
                        t = QT * x.batch + x.tile
                        for c in range(DC):
                            last = pe.matmul(null_ps[:, x.u, :], xnT[:, c, P * t:P * t + P], w_null[:, c, :],
                                             start=(c == 0), stop=(c == DC - 1))
                    last.then_inc(null_ready, 1)

        with ExitStack() as st:
            wq = sbuf(st, "wq", [P, DC, P])
            q_hi = sbuf(st, "q_hi", [P, B, CW], F32R)
            q_lo = sbuf(st, "q_lo", [P, B, CW], F32R)
            q_hilo = [sbuf(st, f"q_hilo{h}", [P, T], F32R) for h in range(2)]
            q_one = [sbuf(st, f"q_one{h}", [P, T], F32R) for h in range(2)]
            bias_row = [[[sbuf(st, f"bias_row{i}_{s}_{h}", [P, P * ((QT - i), (QT // 2 - 1 + i))[s]]) for h in range(2)]
                         for s in range(2)] for i in range(2)]
            probs = [[sbuf(st, f"probs{i}_{h}", [P, P * n]) for h in range(2)] for i, n in enumerate(ROW_BLOCKS)]
            pT_hi = [sbuf(st, f"pT_hi{i}", [P, 2, 2 * P], F32R) for i in range(3)]
            pT_lo = [sbuf(st, f"pT_lo{i}", [P, 2, 2 * P], F32R) for i in range(3)]
            oT = [sbuf(st, f"oT{i}", [P, 2 * P]) for i in range(2)]
            neg_pair = sbuf(st, "neg_pair", [P, UNITS, 2])
            neg_max = sbuf(st, "neg_max", [P, UNITS, 2])
            part_max = sbuf(st, "part_max", [P, UNITS, 2])
            null_arg = sbuf(st, "null_arg", [P, UNITS, 2])
            null_exp = sbuf(st, "null_exp", [P, UNITS, 2])
            row_sum = sbuf(st, "row_sum", [P, UNITS, 2])
            full_sum = sbuf(st, "full_sum", [P, UNITS, 2])
            inv_sum = sbuf(st, "inv_sum", [P, UNITS, 2])
            y_head = [sbuf(st, f"y_head{i}", [P, 2, D]) for i in range(2)]
            s_ps = [psum(st, f"s_ps{i}", [P, CW]) for i in range(2)]
            t_ps = [psum(st, f"t_ps{i}", [P, CW]) for i in range(3)]
            o_ps = [psum(st, f"o_ps{i}", [P, CW])[:, 0:2 * P] for i in range(2)]
            m_ps = psum(st, "m_ps", [P, CW])

            wq_in = sem("wq_in")
            bias_in = [sem(f"bias_in{i}") for i in range(2)]
            bias_ready = sem("bias_ready")
            scores_ready, scores_read, probs_ready = sem("scores_ready"), sem("scores_read"), sem("probs_ready")
            turn_ready, hi_out, lo_out, pv_done = sem("turn_ready"), sem("hi_out"), sem("lo_out"), sem("pv_done")
            oT_ready, projected, scaled, added = sem("oT_ready"), sem("projected"), sem("scaled"), sem("added")
            q_ready, q_hi_ready, q_lo_ready, q_in = sem("q_ready"), sem("q_hi_ready"), sem("q_lo_ready"), sem("q_in")
            neg_ready, null_arg_ready, null_exp_ready = sem("neg_ready"), sem("null_arg_ready"), sem("null_exp_ready")
            sum_ready, inv_ready, null_w_ready = sem("sum_ready"), sem("inv_ready"), sem("null_w_ready")
            ones_ready = sem("ones_ready")
            marks_dve, marks_pool, marks_sp = sem("marks_dve"), sem("marks_pool"), sem("marks_sp")
            LAST = PAIRS - 1
            MOVES = 16 * 6

            def pairs(eng, body):
                body(0)
                with eng.Fori(1, LAST) as p:
                    body(p)
                body(LAST)

            def is_first(p):
                return isinstance(p, int) and p == 0

            def is_last(p):
                return isinstance(p, int) and p == LAST

            def unit_at(p, u):
                if u >= UNITS:
                    return None if is_last(p) else (p + 1, BODY[u - UNITS])
                if u < 0:
                    return None if is_first(p) else (p - 1, BODY[u + UNITS])
                return p, BODY[u]

            def slot_at(p, t):
                if t >= NS:
                    return None if is_last(p) else (p + 1, t - NS)
                return p, t

            def query_step(p, t):
                if t not in QUERIES_AT or (QUERIES_AT[t][0] and is_last(p)):
                    return None
                k, j = QUERIES_AT[t]
                return 4 * p + 3 + k, j, 2 * p + (1, 2, 2, 3)[k]

            AHEAD = ((0, 1, 0), (1, 3, 0), (2, 0, 1))

            with nc.Block() as block:
                @block.sync
                def _(sp):
                    wq_h = Wq.rearrange("(c p) (r n) -> r p c n", p=P, n=P)
                    sp.dma_start(wq[:], wq_h[0]).then_inc(wq_in, 16)

                    def move(half, chunks, scores):
                        wait(sp, scores_ready, scores)
                        apart(sp, marks_sp)
                        sp.wait_ge(q_lo_ready, chunks)
                        apart(sp, marks_sp)
                        for h in range(2):
                            mine = slice(DH * h, DH * h + DH)
                            for to, part in ((q_hilo[h][0:DH], q_hi), (q_hilo[h][DH:P], q_lo), (q_one[h][0:DH], q_hi)):
                                to = to.rearrange("p (b n) -> p b n", b=B)[:, :, CW * half:CW * half + CW]
                                sp.dma_start(to.bitcast(F32), part[mine].bitcast(F32)).then_inc(q_in, 16)

                    def bias_round(p, j):
                        if j >= QT // 2:
                            if is_last(p):
                                return
                            p, j = p + 1, j - QT // 2
                        wait(sp, scores_read, SCORES * p + (FIRST_CHUNK[4 * (j - 1)] if j >= 2 else FIRST_CHUNK[4 * (j + 3)] - SCORES))
                        apart(sp, marks_sp)
                        for s, tile in enumerate((QT - 1 - j, j)):
                            width = P * (tile + 1)
                            for h in range(2):
                                rows = bias[2 * p + h]
                                sp.dma_start(bias_row[j % 2][s][h][:, 0:width],
                                             rows[P * tile:P * tile + P, 0:width]).then_inc(bias_in[j % 2], 16)

                    def body(p):
                        bias_round(p, 2)
                        move(0, 4 * p + 4, SCORES * p)
                        if not is_last(p):
                            sp.dma_start(wq[:], wq_h[p + 1]).then_inc(wq_in, 16)
                        bias_round(p, 3)
                        if not is_last(p):
                            move(1, 4 * p + 6, SCORES * p + FIRST_CHUNK[8])
                        bias_round(p, 4)
                        bias_round(p, 5)
                    for j in range(2):
                        bias_round(0, j)
                    move(1, 2, 0)
                    pairs(sp, body)

                @block.gpsimd
                def _(pool):
                    for h in range(2):
                        pool.memset(q_one[h][DH:P, :].bitcast(F32), 0.0).then_inc(ones_ready, 1)
                    pool.wait_ge(ones_ready, 2)
                    for h in range(2):
                        pool.memset(q_one[h][DH:DH + 1, :].bitcast(F32), 1.0).then_inc(ones_ready, 1)

                    def diagonal(p, j):
                        if j >= QT // 2:
                            if is_last(p):
                                return
                            p, j = p + 1, j - QT // 2
                        pool.wait_ge(bias_in[j % 2], 64 * (2 * p + j // 2 + 1))
                        for s, tile in enumerate((QT - 1 - j, j)):
                            for h in range(2):
                                d = bias_row[j % 2][s][h][:, P * tile:P * tile + P]
                                apart(pool, marks_pool)
                                pool.affine_select(out=d, in_=d, compare_op=ALU.is_ge, fill=-MASKED, base=0,
                                                   pattern=[[-1, P]], channel_multiplier=1).then_inc(bias_ready, 1)

                    def add(p, u):
                        at = unit_at(p, u)
                        if at is None:
                            return
                        p, x = at
                        y = yacc[:, QT * x.batch + x.tile, :]
                        pool.wait_ge(scaled, 2 * (UNITS * p + x.u + 1))
                        for h in range(2):
                            if h:
                                pool.wait_ge(added, 2 * (UNITS * p + x.u) + 1)
                            pool.tensor_tensor(y, y, y_head[x.u % 2][:, h, :], ALU.add).then_inc(added, 1)

                    def body(p):
                        for u in range(UNITS):
                            add(p, u - 2)
                            if u % 4 == 3:
                                diagonal(p, u // 4 + 2)
                    pool.wait_ge(ones_ready, 4)
                    for j in range(2):
                        diagonal(0, j)
                    pairs(pool, body)
                    for u in range(UNITS - 2, UNITS):
                        add(LAST, u)

                @block.scalar
                def _(act):
                    def high(p, t):
                        at = slot_at(p, t)
                        if at is None:
                            return
                        p, t = at
                        n = SLOTS[t].n
                        wait(act, pv_done, NS * p + t - 2)
                        act.wait_ge(turn_ready, NS * p + t + 1)
                        act.activation(pT_hi[t % 3][:, 0:n, :], t_ps[t % 3][:, 0:2 * P * n], ACT.Copy).then_inc(hi_out, 1)

                    def exps(p, u, h):
                        at = unit_at(p, u)
                        if at is None:
                            return
                        p, x = at
                        row = probs[ROW_BUFFER[x.u]][h][:, 0:P * x.blocks]
                        act.wait_ge(scores_read, SCORES * p + FIRST_CHUNK[x.u] + (h + 1) * len(x.chunks))
                        act.activation(row, row, ACT.Exp, scale=-1.0, bias=neg_max[:, x.u, h:h + 1],
                                       accum_out=row_sum[:, x.u, h:h + 1]).then_inc(probs_ready, 1)

                    def query(number, j, half):
                        wait(act, q_in, MOVES * half)
                        act.wait_ge(q_ready, number + 1)
                        act.activation(q_hi[:, j // 2, :], m_ps[:], ACT.Copy, scale=DH ** -0.5).then_inc(q_hi_ready, 1)

                    def scale(p, u):
                        at = unit_at(p, u)
                        if at is None:
                            return
                        p, x = at
                        wait(act, added, 2 * (UNITS * p + x.u - 1))
                        act.wait_ge(inv_ready, QT * p + x.u // 2 + 1)
                        act.wait_ge(projected, UNITS * p + x.u + 1)
                        for h in range(2):
                            act.activation(y_head[x.u % 2][:, h, :], m_ps[:, D * h:D * h + D], ACT.Copy,
                                           scale=inv_sum[:, x.u, h:h + 1]).then_inc(scaled, 1)

                    def body(p):
                        for t, slot in enumerate(SLOTS):
                            u = slot.u
                            if u % 2 and t == FIRST_SLOT[u]:
                                act.wait_ge(null_arg_ready, QT * p + u // 2 + 1)
                                act.activation(null_exp[:, u - 1:u + 1, :], null_arg[:, u - 1:u + 1, :], ACT.Exp).then_inc(null_exp_ready, 1)
                            high(p, t + 1)
                            if t - 1 in PROJECT_AT:
                                scale(p, PROJECT_AT[t - 1])
                            q = query_step(p, t - 1)
                            if q:
                                query(*q)
                            for v, h in EXPS_AT[t]:
                                exps(p, v, h)

                    for q in AHEAD[:2]:
                        query(*q)
                    for at in EXPS_AT:
                        for v, h in at:
                            if v >= UNITS:
                                exps(0, v - UNITS, h)
                    query(*AHEAD[2])
                    high(0, 0)
                    pairs(act, body)
                    for u in range(UNITS - 2, UNITS):
                        scale(LAST, u)

                @block.vector
                def _(dve):
                    def scores(p, u, i):
                        at = unit_at(p, u)
                        if at is None:
                            return
                        p, x = at
                        h, n = i // len(x.chunks), i % len(x.chunks)
                        first, k = x.chunks[n]
                        c = FIRST_CHUNK[x.u] + i
                        cols = slice(P * first, P * (first + k))
                        if i == 0:
                            dve.wait_ge(bias_ready, 4 * (QT // 2 * p + x.round + 1))
                            before = max(v for v in range(x.u - UNITS, x.u) if ROW_BUFFER[v] == ROW_BUFFER[x.u])
                            wait(dve, turn_ready, NS * p + (FIRST_SLOT[before + 1] if before >= 0 else FIRST_SLOT[before + UNITS + 1] - NS))
                        start = part_max[:, x.u, h:h + 1] if n else neg_pair[:, x.u, h:h + 1]
                        to = neg_max if n == len(x.chunks) - 1 else part_max
                        if n:
                            dve.wait_ge(scores_read, SCORES * p + c)
                        dve.wait_ge(scores_ready, SCORES * p + c + 1)
                        apart(dve, marks_dve)
                        dve.tensor_tensor_reduce(probs[ROW_BUFFER[x.u]][h][:, cols], s_ps[c % 2][:, 0:P * k],
                                                 bias_row[x.round % 2][x.short][h][:, cols], -1.0, start, ALU.add, ALU.min,
                                                 to[:, x.u, h:h + 1]).then_inc(scores_read, 1)

                    def low(p, t):
                        at = slot_at(p, t)
                        if at is None:
                            return
                        p, t = at
                        n = SLOTS[t].n
                        dve.wait_ge(hi_out, NS * p + t + 1)
                        dve.tensor_tensor(pT_lo[t % 3][:, 0:n, :], t_ps[t % 3][:, 0:2 * P * n].rearrange("p (n q) -> p n q", n=n),
                                          pT_hi[t % 3][:, 0:n, :].bitcast(F32), ALU.subtract).then_inc(lo_out, 1)

                    def outputs(p, u):
                        at = unit_at(p, u)
                        if at is None:
                            return
                        p, x = at
                        wait(dve, projected, UNITS * p + x.u - 1)
                        dve.wait_ge(pv_done, NS * p + FIRST_SLOT[x.u + 1])
                        dve.tensor_copy(oT[x.u % 2][:], o_ps[x.u % 2]).then_inc(oT_ready, 1)

                    def query(number, j, half):
                        dve.wait_ge(q_hi_ready, number + 1)
                        dve.scalar_tensor_tensor(q_lo[:, j // 2, :], m_ps[:], DH ** -0.5, q_hi[:, j // 2, :].bitcast(F32),
                                                 ALU.mult, ALU.subtract).then_inc(q_lo_ready, 1)

                    def null_scores(p, half, count):
                        rows = slice(8 * half, 8 * half + 8)
                        apart(dve, marks_dve)
                        dve.tensor_copy(neg_pair[:, rows, :], neg_null[:, rows, bass.ds(2 * p, 2)]).then_inc(neg_ready, 1)
                        dve.wait_ge(neg_ready, count)

                    def body(p):
                        for t, slot in enumerate(SLOTS):
                            u = slot.u
                            if t == FIRST_SLOT[u]:
                                outputs(p, u - 1)
                            if t == FIRST_SLOT[2]:
                                null_scores(p, 1, 2 * p + 2)
                            if t == FIRST_SLOT[8] and not is_last(p):
                                null_scores(p + 1, 0, 2 * p + 3)
                            for v, i in CHUNKS_AT[t]:
                                scores(p, v, i)
                            q = query_step(p, t - 1)
                            if q:
                                query(*q)
                            low(p, t + 1)
                            rows = slice(u // 2 * 2, u // 2 * 2 + 2)
                            n = QT * p + u // 2 + 1
                            if u % 2 == 0 and t == FIRST_SLOT[u + 1] - 1:
                                dve.wait_ge(scores_read, SCORES * p + FIRST_CHUNK[u + 2])
                                dve.tensor_tensor(null_arg[:, rows, :], neg_max[:, rows, :], neg_pair[:, rows, :],
                                                  ALU.subtract).then_inc(null_arg_ready, 1)
                            if u % 2 and t == FIRST_SLOT[u]:
                                dve.wait_ge(null_exp_ready, n)
                                dve.wait_ge(probs_ready, 2 * UNITS * p + 2 * u + 2)
                                dve.tensor_tensor(full_sum[:, rows, :], row_sum[:, rows, :], null_exp[:, rows, :], ALU.add).then_inc(sum_ready, 1)
                                dve.wait_ge(sum_ready, n)
                                dve.reciprocal(inv_sum[:, rows, :], full_sum[:, rows, :]).then_inc(inv_ready, 1)
                                dve.wait_ge(inv_ready, n)
                                dve.tensor_tensor(null_w[:, rows, bass.ds(2 * p, 2)], null_exp[:, rows, :], inv_sum[:, rows, :],
                                                  ALU.mult).then_inc(null_w_ready, 1)

                    dve.wait_ge(ones_ready, 4)
                    null_scores(0, 0, 1)
                    for q in AHEAD[:2]:
                        query(*q)
                    for at in CHUNKS_AT:
                        for v, i in at:
                            if v >= UNITS:
                                scores(0, v - UNITS, i)
                    query(*AHEAD[2])
                    low(0, 0)
                    pairs(dve, body)
                    outputs(LAST, UNITS - 1)

                @block.tensor
                def _(pe):
                    def scores(p, u, i):
                        at = unit_at(p, u)
                        if at is None:
                            return
                        p, x = at
                        h, n = i // len(x.chunks), i % len(x.chunks)
                        first, k = x.chunks[n]
                        c = FIRST_CHUNK[x.u] + i
                        cols = slice(S * x.batch + P * first, S * x.batch + P * (first + k))
                        rows = slice(x.query, x.query + P)
                        if i == 0:
                            pe.wait_ge(q_in, MOVES * (2 * p + 1 + x.u // 8))
                        wait(pe, scores_read, SCORES * p + c - 1)
                        pe.matmul(s_ps[c % 2][:, 0:P * k], q_hilo[h][:, rows], k_hi[:, cols], start=True, stop=False)
                        pe.matmul(s_ps[c % 2][:, 0:P * k], q_one[h][:, rows], k_lo[:, cols],
                                  start=False, stop=True).then_inc(scores_ready, 1)

                    def turn(p, t):
                        at = slot_at(p, t)
                        if at is None:
                            return
                        p, t = at
                        slot = SLOTS[t]
                        x = BODY[slot.u]
                        if t == FIRST_SLOT[slot.u]:
                            pe.wait_ge(probs_ready, 2 * (UNITS * p + slot.u + 1))
                        wait(pe, lo_out, NS * p + t - 2)
                        for n in range(slot.n):
                            for h in range(2):
                                last = pe.transpose(t_ps[t % 3][:, P * (2 * n + h):P * (2 * n + h) + P],
                                                    probs[ROW_BUFFER[x.u]][h][:, P * (slot.first + n):P * (slot.first + n) + P], ident[:])
                        last.then_inc(turn_ready, 1)

                    def weigh(p, t):
                        slot = SLOTS[t]
                        x = BODY[slot.u]
                        if slot.first == 0:
                            wait(pe, oT_ready, UNITS * p + x.u - 1)
                        pe.wait_ge(lo_out, NS * p + t + 1)
                        for n in range(slot.n):
                            k = slot.first + n
                            v = values[:, QT * x.batch + k, :]
                            pe.matmul(o_ps[x.u % 2], v, pT_hi[t % 3][:, n, :], start=(k == 0), stop=False)
                            last = pe.matmul(o_ps[x.u % 2], v, pT_lo[t % 3][:, n, :], start=False, stop=(k == x.blocks - 1))
                        last.then_inc(pv_done, 1)

                    def project(p, u, queries):
                        at = unit_at(p, u)
                        if at is None:
                            return
                        p, x = at
                        pe.wait_ge(oT_ready, UNITS * p + x.u + 1)
                        wait(pe, scaled, 2 * (UNITS * p + x.u))
                        wait(pe, q_lo_ready, queries)
                        for h in range(2):
                            last = pe.matmul(m_ps[:, D * h:D * h + D], oT[x.u % 2][:, P * h:P * h + P], wo[:, bass.ds(2 * p + h, 1), :],
                                             start=True, stop=True)
                        last.then_inc(projected, 1)

                    def query(number, j, pair, units):
                        pe.wait_ge(wq_in, 16 * (pair + 1))
                        wait(pe, q_lo_ready, number)
                        wait(pe, scaled, 2 * units)
                        b, half = j // 2, j % 2
                        for c in range(DC):
                            tokens = xnT[:, c, S * b:S * b + S].rearrange("p (q n) -> p q n", q=4)
                            tokens = tokens[:, 0::3, :] if half else tokens[:, 1:3, :]
                            last = pe.matmul(m_ps[:], wq[:, c, :], tokens, start=(c == 0), stop=(c == DC - 1))
                        last.then_inc(q_ready, 1)

                    def body(p):
                        queries = 4 * p + 3
                        units = UNITS * p - 2
                        for t in range(NS):
                            for v, i in CHUNKS_AT[t][:1]:
                                scores(p, v, i)
                            turn(p, t + 2)
                            for v, i in CHUNKS_AT[t][1:]:
                                scores(p, v, i)
                            weigh(p, t)
                            if t in PROJECT_AT:
                                project(p, PROJECT_AT[t], queries)
                                units = UNITS * p + PROJECT_AT[t] + 1
                            q = query_step(p, t)
                            if q:
                                query(q[0], q[1], p + (t > min(QUERIES_AT)), units)
                                queries = q[0] + 1

                    for number, j, _ in AHEAD[:2]:
                        query(number, j, 0, 0)
                    pe.wait_ge(ones_ready, 4)
                    for at in CHUNKS_AT:
                        for v, i in at:
                            if v >= UNITS:
                                scores(0, v - UNITS, i)
                    query(AHEAD[2][0], AHEAD[2][1], 0, 0)
                    for t in range(2):
                        turn(0, t)
                    pairs(pe, body)
                    for u in range(UNITS - 2, UNITS):
                        project(LAST, u, 0)

        with ExitStack() as st:
            null_wT = sbuf(st, "null_wT", [H, UNITS, P])
            nt_ps = [psum(st, f"nt_ps{i}", [P, CW]) for i in range(4)]
            ny_ps = [psum(st, f"ny_ps{i}", [P, B, D]) for i in range(4)]
            null_turned, null_wT_ready, null_projected, null_added = (
                sem(n) for n in ("null_turned", "null_wT_ready", "null_projected", "null_added"))
            with nc.Block() as block:
                @block.tensor
                def _(pe):
                    for i in range(4):
                        for n in range(4):
                            last = pe.transpose(nt_ps[i][0:H, P * n:P * n + P], null_w[:, 4 * i + n, :], ident[:])
                        last.then_inc(null_turned, 1)
                    for i in range(QT):
                        pe.wait_ge(null_wT_ready, i // 2 + 1)
                        wait(pe, null_added, i - 3)
                        for b in range(B):
                            last = pe.matmul(ny_ps[i % 4][:, b, :], null_wT[:, 2 * i + b, :], null_wo[:], start=True, stop=True)
                        last.then_inc(null_projected, 1)

                @block.scalar
                def _(act):
                    for i in range(4):
                        act.wait_ge(null_turned, i + 1)
                        act.activation(null_wT[:, 4 * i:4 * i + 4, :], nt_ps[i][0:H, :], ACT.Copy).then_inc(null_wT_ready, 1)

                @block.vector
                def _(dve):
                    for i in range(QT):
                        dve.wait_ge(null_projected, i + 1)
                        for b in range(B):
                            x = BODY[2 * i + b]
                            y = yacc[:, QT * x.batch + x.tile, :]
                            last = dve.tensor_tensor(y, ny_ps[i % 4][:, b, :], y, ALU.add)
                        last.then_inc(null_added, 1)

        attn.close()

        with ExitStack() as later:
            xT_hi = sbuf(later, "xT_hi", [P, DC, T], F32R)
            xT_lo = sbuf(later, "xT_lo", [P, DC, T], F32R)
            gates = sbuf(later, "gates", [P, NT, EXPERTS])
            gates2 = sbuf(later, "gates2", [P, NT, E])
            ident_bf = sbuf(later, "ident_bf", [P, P], BF16)
            power4 = sbuf(later, "power4", [P, 4])
            set_up = sem("set_up")
            with nc.Block() as block:
                @block.vector
                def _(dve):
                    dve.memset(power4[:], -0.5).then_inc(set_up, 1)
                    dve.tensor_copy(ident_bf[:], ident[:]).then_inc(set_up, 1)
            feed_forward_stage(nc, sbuf, psum, sem, aps, (xs, yacc, ident[:], ident_bf[:], xT_hi, xT_lo, gates, power4[:]))
            first_mixture_stage(nc, sbuf, psum, sem, aps, (yacc, xT_hi, xT_lo, gates))
            pair_attention_stage(nc, sbuf, psum, sem, aps, (xs, yacc, ident[:], xT_hi, xT_lo, gates2, power4[:]))
            second_mixture_stage(nc, sbuf, psum, sem, aps, (xs, xT_hi, xT_lo, gates2, out))


def kernel(**inputs):
    import numpy as np
    import concourse.bacc as bacc
    from concourse.bass_utils import run_bass_kernel_spmd

    def by_partition(w):
        e, k, n = w.shape
        return w.reshape(e, k // P, P, n).transpose(0, 2, 1, 3).reshape(e, P, k // P * n)

    def halves(w, axis):
        return np.stack(np.split(w, 2, axis=axis))

    gate = np.concatenate([inputs["L1_cond_w_gate"], halves(inputs["L1_cond_sw_gate"], 1)])
    up = np.concatenate([inputs["L1_cond_w_up"], halves(inputs["L1_cond_sw_up"], 1)])
    down = np.concatenate([inputs["L1_cond_w_down"], halves(inputs["L1_cond_sw_down"], 0)])
    first_weights = np.concatenate([by_partition(np.concatenate([gate, up], 2)), by_partition(down)], 2)
    second_weights = np.concatenate([by_partition(inputs["L1_ffn_moe_w1"]), by_partition(inputs["L1_ffn_moe_w2"])], 2)
    nc = bacc.Bacc("TRN2", target_bir_lowering=False, num_devices=1)
    laid = {
        "x": inputs["x"].reshape(T, D),
        "bias": inputs["fside_16xSxS_0"],
        "cond": inputs["cond_64"],
        "mask": inputs["mask_BxS_bk0"].reshape(1, T),
        "g_in": inputs["L0_cond_g_in"].reshape(DC, P).T,
        "nab": inputs["L0_cond_null_attn_bias"],
        "Wq": inputs["L0_cond_Wq"],
        "Wkv": inputs["L0_cond_Wkv"],
        "Wo": inputs["L0_cond_Wo"],
        "g_out": inputs["L0_cond_g_out"].reshape(1, D),
        "ffT": inputs["L0_ffn_weight"].T,
        "wtT": inputs["L1_cond_wt"].T,
        "wgT": inputs["L1_cond_wg"].T,
        "condT": inputs["cond_64"].T,
        "order": np.tril(np.ones((E, E), np.float32), -1).reshape(1, E * E),
        "m1_w": first_weights,
        "ln1_w": inputs["L1_ffn_ln1_weight"].reshape(DC, P).T,
        "ln1_b": inputs["L1_ffn_ln1_bias"].reshape(DC, P).T,
        "ln2_w": inputs["L1_ffn_ln2_weight"].reshape(DC, P).T,
        "ln2_b": inputs["L1_ffn_ln2_bias"].reshape(DC, P).T,
        "qkvT": inputs["L1_ffn_qkv_weight"].T,
        "projT": inputs["L1_ffn_proj_weight"].T,
        "routerT": inputs["L1_ffn_router_weight"].T,
        "m2_w": second_weights,
    }
    laid = {n: np.ascontiguousarray(a) for n, a in laid.items()}
    aps = {n: nc.dram_tensor(n + "_dram", a.shape, mybir.dt.from_np(a.dtype), kind="ExternalInput").ap() for n, a in laid.items()}
    out = nc.dram_tensor("out_dram", (T, D), F32, kind="ExternalOutput").ap()
    program(nc, **aps, out=out)
    r = run_bass_kernel_spmd(nc, [{n + "_dram": a for n, a in laid.items()}], core_ids=[0])
    return r.results[0]["out_dram"].reshape(B, S, D)
```

```python
import concourse.bass as bass
from concourse import mybir
from contextlib import ExitStack

F32 = mybir.dt.float32
F32R = mybir.dt.float32r
BF16 = mybir.dt.bfloat16
U8 = mybir.dt.uint8
I32 = mybir.dt.int32
ALU = mybir.AluOpType
ACT = mybir.ActivationFunctionType
AX = mybir.AxisListType

P = 128
B, S, D = 2, 1024, 256
T = B * S
NT = T // P
DC = D // P
H, DH = 16, 64
QT = S // P
PAIRS = H // 2
CW = 512
MASKED = 1.0e30
EPS = 1e-5
ROUND = 1.5 * 2 ** 23
E = 8
M1 = 128
LEAKY = 0.01
COND = 64
KV, HD = 4, 16
QKV = (H + 2 * KV) * HD
F2 = 512
TOP = 2
SLAB = T + P
GROUP = 4
PAIR = 2 * GROUP
EARLY = 2
ROW = D + E + 1
ROUTED = (TOP * T + E * (P - 1)) // P
BUFS = 8
SPARES = ROUTED - TOP * T // P
OUT_ROWS = T + P * (1 + SPARES)
W1COLS = DC * 2 * M1 + D
W2COLS = DC * F2 + F2 // P * D


class Steps:

    def __init__(self, per_body):
        self.per_body = per_body
        self.n = 0

    def up(self):
        self.n += 1
        return 1

    def here(self, it):
        return self.per_body * it + self.n


def flat(tiles):
    return tiles[:].rearrange("p t d -> p (t d)")


def by_group(tiles):
    return tiles[:].rearrange("p (r t) e -> p r t e", r=2)


def gate_top_two(dve, step, steps, it, gate, scratch, weights):
    above, more, ties, rank = scratch
    this = gate.unsqueeze(3).broadcast_to([P, PAIR, E, E])
    other = gate.unsqueeze(2).broadcast_to([P, PAIR, E, E])
    dve.tensor_tensor(more, other, this, ALU.subtract).then_inc(step, steps.up())
    dve.wait_ge(step, steps.here(it))
    dve.tensor_tensor(above, more, ties.unsqueeze(1).broadcast_to([P, PAIR, E, E]), ALU.is_gt).then_inc(step, steps.up())
    dve.wait_ge(step, steps.here(it))
    dve.tensor_reduce(rank, above, AX.X, ALU.add).then_inc(step, steps.up())
    dve.wait_ge(step, steps.here(it))
    return dve.scalar_tensor_tensor(weights, rank, 1.5, gate, ALU.is_lt, ALU.mult)


class Routing:
    LOADS = 16 * 7

    def __init__(self, sbuf, st):
        self.order = sbuf(st, "rt_order", [P, E, E])
        self.ties = sbuf(st, "rt_ties", [P, E, E])
        self.slabs = sbuf(st, "rt_slabs", [P, E])
        self.ids = sbuf(st, "rt_ids", [P, NT], I32)
        self.before_f = sbuf(st, "rt_before_f", [P, P])
        self.before = sbuf(st, "rt_before", [P, P], BF16)
        self.ones = sbuf(st, "rt_ones", [P, P], BF16)
        self.numbers = sbuf(st, "rt_numbers", [1, ROUTED])
        self.spare_rows = sbuf(st, "rt_spare_rows", [1, ROUTED])
        self.all_before = sbuf(st, "rt_all_before", [1, ROUTED])
        self.padding = sbuf(st, "rt_padding", [P, ROW])
        self.rows = sbuf(st, "rt_rows", [P, PAIR, ROW])
        self.group_rows = [self.rows[:, GROUP * r:GROUP * (r + 1), :] for r in range(2)]
        self.rank = sbuf(st, "rt_rank", [P, PAIR, E])
        self.chosen = sbuf(st, "rt_chosen", [P, PAIR, E], BF16)
        self.rows_at = sbuf(st, "rt_rows_at", [P, PAIR, TOP], I32)
        self.carry = sbuf(st, "rt_carry", [P, E])
        self.base = sbuf(st, "rt_base", [P, PAIR, E])
        self.place = sbuf(st, "rt_place", [P, PAIR, TOP, E])
        self.next_rows = sbuf(st, "rt_next_rows", [P, PAIR, TOP])
        self.n_tiles, self.first_tile, self.end_tile, self.first_row = (
            sbuf(st, "rt_" + n, [1, E]) for n in ("n_tiles", "first_tile", "end_tile", "first_row"))
        self.earlier = sbuf(st, "rt_earlier", [1, E, E])
        self.begun, self.over, self.tile_row = (sbuf(st, "rt_" + n, [1, ROUTED, E]) for n in ("begun", "over", "tile_row"))
        self.overs, self.spare, self.rows_f = (sbuf(st, "rt_" + n, [1, ROUTED]) for n in ("overs", "spare", "rows_f"))
        self.slab_ends = sbuf(st, "rt_slab_ends", [1, E], I32)
        self.row_of = sbuf(st, "rt_row_of", [1, ROUTED], I32)
        self.expert_of = sbuf(st, "rt_expert_of", [1, ROUTED], I32)
        self.clear_at = sbuf(st, "rt_clear_at", [1, ROUTED], I32)

    def load(self, sp, aps, loaded):
        sp.dma_start(self.order[:], aps["order"].broadcast_to([P, E * E])).then_inc(loaded, 16)
        sp.dma_start(self.slabs[:], aps["slabs"].broadcast_to([P, E])).then_inc(loaded, 16)
        sp.dma_start(self.ids[:], aps["ids"]).then_inc(loaded, 16)
        sp.dma_start(self.before_f[:], aps["before"]).then_inc(loaded, 16)
        sp.dma_start(self.numbers[:], aps["numbers"]).then_inc(loaded, 16)
        sp.dma_start(self.spare_rows[:], aps["spare_rows"]).then_inc(loaded, 16)
        sp.dma_start(self.all_before[:], aps["all_before"]).then_inc(loaded, 16)


def scatter_rows(pool, rt, tiles, routed_rows, scattered):
    for j in tiles:
        for k in range(TOP):
            pool.indirect_dma_start(routed_rows, bass.IndirectOffsetOnAxis(ap=rt.rows_at[:, j, k:k + 1], axis=0),
                                    rt.rows[:, j, :], None).then_inc(scattered, 16)


def store_padding(sp, rt, routed_rows, stored):
    for e in range(E):
        end = sp.value_load(rt.slab_ends[0:1, e:e + 1], min_val=e * SLAB, max_val=e * SLAB + T)
        sp.dma_start(routed_rows[bass.ds(end, P), :], rt.padding[:]).then_inc(stored, 16)


def load_first_rows(sp, nc, rt, routed_rows, rows, rows_in):
    at = nc.values_load_multi_w_load_instructions(rt.row_of[0:1, 0:BUFS], engines=[mybir.EngineType.SP], min_val=0,
                                                  max_val=E * SLAB + P * (SPARES - 1))[1]
    for k in range(BUFS):
        sp.dma_start(rows[k], routed_rows[bass.ds(at[k], P), :]).then_inc(rows_in[k], 16)


def count_chosen(pe, rt, counts, totals):
    pe.matmul(counts, rt.before[:], rt.chosen[:], start=True, stop=False)
    for k in range(1, PAIR):
        pe.matmul(counts[:, k:PAIR, :], rt.ones[:], rt.chosen[:, 0:PAIR - k, :], start=False, stop=(k == PAIR - 1))
    for j in range(PAIR):
        last = pe.matmul(totals, rt.ones[:], rt.chosen[:, j, :], start=(j == 0), stop=(j == PAIR - 1))
    return last


def place_rows(dve, step, steps, it, rt, counts, totals):
    dve.tensor_tensor(rt.base[:], counts, rt.carry[:].unsqueeze(1).broadcast_to([P, PAIR, E]), ALU.add).then_inc(step, steps.up())
    dve.wait_ge(step, steps.here(it))
    dve.tensor_tensor(rt.carry[:], totals, rt.carry[:], ALU.add)
    dve.scalar_tensor_tensor(rt.place[:, :, 0, :], rt.rank[:], 0.5, rt.base[:], ALU.is_lt, ALU.mult)
    dve.scalar_tensor_tensor(rt.place[:, :, 1, :], rt.rank[:], 1.0, rt.base[:], ALU.is_equal, ALU.mult).then_inc(step, steps.up())
    dve.wait_ge(step, steps.here(it))
    dve.tensor_reduce(rt.next_rows[:], rt.place[:], AX.X, ALU.add).then_inc(step, steps.up())
    dve.wait_ge(step, steps.here(it))
    return dve.tensor_copy(rt.rows_at[:], rt.next_rows[:])


def make_table(dve, rt, step, ready):
    steps = Steps(0)
    number = rt.numbers[:].unsqueeze(2).broadcast_to([1, ROUTED, E])

    def by_expert(row):
        return row[:].unsqueeze(1).broadcast_to([1, ROUTED, E])

    dve.tensor_copy(rt.slab_ends[:], rt.carry[0:1, :])
    dve.tensor_tensor(rt.n_tiles[:], rt.carry[0:1, :], rt.slabs[0:1, :], ALU.subtract).then_inc(step, steps.up())
    dve.wait_ge(step, steps.here(0))
    dve.tensor_scalar(rt.n_tiles[:], rt.n_tiles[:], 1.0 / P, (P - 1) / (2.0 * P), ALU.mult, ALU.add).then_inc(step, steps.up())
    dve.wait_ge(step, steps.here(0))
    dve.tensor_scalar(rt.n_tiles[:], rt.n_tiles[:], ROUND, ROUND, ALU.add, ALU.subtract).then_inc(step, steps.up())
    dve.wait_ge(step, steps.here(0))
    dve.tensor_tensor(rt.earlier[:], rt.order[0:1], rt.n_tiles[:].unsqueeze(1).broadcast_to([1, E, E]), ALU.mult).then_inc(step, steps.up())
    dve.wait_ge(step, steps.here(0))
    dve.tensor_reduce(rt.first_tile[:], rt.earlier[:], AX.X, ALU.add).then_inc(step, steps.up())
    dve.wait_ge(step, steps.here(0))
    dve.tensor_tensor(rt.end_tile[:], rt.first_tile[:], rt.n_tiles[:], ALU.add)
    dve.scalar_tensor_tensor(rt.first_row[:], rt.first_tile[:], -float(P), rt.slabs[0:1, :], ALU.mult, ALU.add).then_inc(step, steps.up())
    dve.wait_ge(step, steps.here(0))
    dve.tensor_tensor(rt.begun[:], number, by_expert(rt.first_tile), ALU.is_ge)
    dve.tensor_tensor(rt.over[:], number, by_expert(rt.end_tile), ALU.is_ge)
    dve.scalar_tensor_tensor(rt.tile_row[:], number, float(P), by_expert(rt.first_row), ALU.mult, ALU.add).then_inc(step, steps.up())
    dve.wait_ge(step, steps.here(0))
    dve.tensor_tensor(rt.begun[:], rt.begun[:], rt.over[:], ALU.subtract)
    dve.tensor_reduce(rt.overs[:], rt.over[:], AX.X, ALU.add).then_inc(step, steps.up())
    dve.wait_ge(step, steps.here(0))
    dve.tensor_tensor(rt.tile_row[:], rt.tile_row[:], rt.begun[:], ALU.mult)
    dve.scalar_tensor_tensor(rt.spare[:], rt.overs[:], E - 0.5, rt.spare_rows[:], ALU.is_gt, ALU.mult).then_inc(step, steps.up())
    dve.wait_ge(step, steps.here(0))
    dve.tensor_reduce(rt.rows_f[:], rt.tile_row[:], AX.X, ALU.add)
    dve.tensor_scalar(rt.expert_of[:], rt.overs[:], E - 1.0, None, ALU.min).then_inc(step, steps.up())
    dve.wait_ge(step, steps.here(0))
    dve.tensor_tensor(rt.row_of[:], rt.rows_f[:], rt.spare[:], ALU.add).then_inc(ready, 1)
    dve.wait_ge(ready, 1)
    dve.tensor_tensor(rt.spare[:, 1:ROUTED], rt.overs[:, 1:ROUTED], rt.overs[:, 0:ROUTED - 1], ALU.is_equal).then_inc(step, steps.up())
    dve.wait_ge(step, steps.here(0))
    dve.tensor_copy(rt.clear_at[:, 0:1], rt.all_before[:, 0:1])
    dve.scalar_tensor_tensor(rt.clear_at[:, 1:ROUTED], rt.spare[:, 1:ROUTED], -16.0, rt.all_before[:, 1:ROUTED], ALU.mult, ALU.add)


class FeedForwardInputs:
    LOADS = 16 * 5

    def __init__(self, sbuf, st):
        self.g_out = sbuf(st, "g_out", [P, D])
        self.w_raw = sbuf(st, "ff_w_raw", [P, DC, D])
        self.cond_c = sbuf(st, "cond_c", [COND, B])
        self.wg = sbuf(st, "wg", [COND, E])
        self.wt = sbuf(st, "wt", [P, DC, E])

    def load(self, sp, aps, loaded):
        sp.dma_start(self.w_raw[:], aps["ffT"].rearrange("(c p) o -> p c o", p=P)).then_inc(loaded, 16)
        sp.dma_start(self.g_out[:], aps["g_out"].broadcast_to([P, D])).then_inc(loaded, 16)
        sp.dma_start(self.wt[:], aps["wtT"].rearrange("(c p) e -> p c e", p=P)).then_inc(loaded, 16)
        sp.dma_start(self.wg[:], aps["wgT"]).then_inc(loaded, 16)
        sp.dma_start(self.cond_c[:], aps["condT"]).then_inc(loaded, 16)


def feed_forward_stage(nc, sbuf, psum, sem, aps, keep, ahead, routing, routed_rows, scattered):
    xs, yacc, ident, ident_bf, xT_hi, xT_lo, power4 = keep
    inputs, loaded, shared_raw, shared_in, w1, w1_in = ahead
    g_out, w_raw, cond_c, wg, wt = inputs.g_out, inputs.w_raw, inputs.cond_c, inputs.wg, inputs.wt
    rt = routing
    with ExitStack() as st:
        spare = sbuf(st, "ff_spare", [P, SPARES, ROW])
        w_u = sbuf(st, "ff_w_u", [P, DC, D])
        w_ter = sbuf(st, "ff_w_ter", [P, DC, D], BF16)
        w_abs = sbuf(st, "ff_w_abs", [P, 1])
        w_scale = sbuf(st, "ff_w_scale", [P, 1])
        w_inv = sbuf(st, "ff_w_inv", [P, 1])
        w_scale127 = sbuf(st, "ff_w_scale127", [P, 1])
        ones = sbuf(st, "ff_ones", [P, P])
        cond_b = sbuf(st, "cond_b", [COND, B, P])
        half_cond = sbuf(st, "half_cond", [P, B, E])
        stats = [sbuf(st, f"ff_stats{r}", [P, 4, 6]) for r in range(2)]
        mv = [sbuf(st, f"ff_mv{r}", [P, 4, 2]) for r in range(2)]
        rstd = [sbuf(st, f"ff_rstd{r}", [P, 4]) for r in range(2)]
        yl = [sbuf(st, f"ff_yl{r}", [P, 4, D]) for r in range(2)]
        a_scale = [sbuf(st, f"a_scale{r}", [P, 4]) for r in range(2)]
        a_inv = [sbuf(st, f"a_inv{r}", [P, 4]) for r in range(2)]
        out_scale = [sbuf(st, f"out_scale{r}", [P, 4]) for r in range(2)]
        z = [sbuf(st, f"z{r}", [P, 4, D], BF16) for r in range(2)]
        zT = [sbuf(st, f"zT{r}", [P, DC, CW], BF16) for r in range(2)]
        x1 = [rt.group_rows[r][:, :, 0:D] for r in range(2)]
        x1T = [sbuf(st, f"x1T{r}", [P, DC, CW]) for r in range(2)]
        gate = sbuf(st, "ff_gate", [P, PAIR, E])
        top = sbuf(st, "ff_top", [P, PAIR, E])
        row = sbuf(st, "ff_row", [P, PAIR])
        above = sbuf(st, "ff_above", [P, PAIR, E, E])
        more = sbuf(st, "ff_more", [P, PAIR, E, E])
        zT_ps = psum(st, "zT_ps", [P, DC, CW], BF16)
        f_all = psum(st, "f_ps", [P, 2, GROUP, D])
        f_ps = [f_all[:, r] for r in range(2)]
        x_ps = [psum(st, f"x_ps{c}", [P, CW]) for c in range(DC)]
        both_logits = f_all[:, :, 0, 0:GROUP * E].rearrange("p r (t e) -> p r t e", e=E)
        logits = [both_logits[:, r] for r in range(2)]
        counts = f_all[:, 0, 0, GROUP * E:(GROUP + PAIR) * E].rearrange("p (t e) -> p t e", e=E)
        totals = f_all[:, 0, 0, (GROUP + PAIR) * E:(GROUP + PAIR + 1) * E]
        w_total = x_ps[0][:, 0:1]
        cond_ps = x_ps[1][:, 0:B * E].rearrange("p (b e) -> p b e", e=E)

        step, ones_set = sem("ff_step"), sem("ff_ones_set")
        w_abs_ready, totals_ready, w_ready, cond_ready = (sem(f"ff_{n}") for n in ("w_abs_ready", "totals_ready", "w_ready", "cond_ready"))
        var_ready, rstd_ready, z_ready, z_turned, zT_ready, f_ready = (
            sem(f"ff_{n}") for n in ("var_ready", "rstd_ready", "z_ready", "z_turned", "zT_ready", "f_ready"))
        x1_ready, x1_turned, x1T_ready, xs_ready, hi_ready, lo_ready = (
            sem(f"ff_{n}") for n in ("x1_ready", "x1_turned", "x1T_ready", "xs_ready", "hi_ready", "lo_ready"))
        logits_ready, logits_read, exp_ready = (sem(f"ff_{n}") for n in ("logits_ready", "logits_read", "exp_ready"))
        chosen_ready, counted, placed, rows_free, padding_ready, stored = (
            sem(f"ff_{n}") for n in ("chosen_ready", "counted", "placed", "rows_free", "padding_ready", "stored"))
        marks = sem("ff_marks")
        LOADS = inputs.LOADS + rt.LOADS
        SETUP, PER_BODY = 5, 33
        xs_f, yacc_f = flat(xs), flat(yacc)

        def tile(it, r, t):
            return bass.ds(D * (QT * it + 4 * r + t), D)

        with nc.Block() as block:
            @block.sync
            def _(sp):
                for i in range(2):
                    sp.dma_start(shared_raw[i][:], aps["m1_w"][E + i]).then_inc(shared_in[i], 16)
                for e in range(E):
                    sp.dma_start(w1[:, e, :].bitcast(F32), aps["m1_w"][e]).then_inc(w1_in, 16)
                sp.wait_ge(padding_ready, 1)
                sp.dma_start(routed_rows[E * SLAB:E * SLAB + P * SPARES, :].rearrange("(n p) c -> p n c", p=P), spare[:]).then_inc(stored, 16)
                sp.wait_ge(stored, 16)

            @block.gpsimd
            def _(pool):
                pool.memset(ones[:], 1.0).then_inc(ones_set, 1)
                pool.sem_inc(rows_free, 1)
                for it in range(B):
                    for r in range(2):
                        pool.wait_ge(var_ready, 2 * it + r + 1)
                        pool.tensor_tensor(rstd[r][:], rstd[r][:], power4, ALU.pow).then_inc(rstd_ready, 1)
                    if it:
                        pool.wait_ge(placed, it)
                        scatter_rows(pool, rt, range(PAIR), routed_rows, scattered)
                        pool.wait_ge(scattered, 16 * QT * TOP * it)
                        pool.sem_inc(rows_free, 1)

            @block.vector
            def _(dve):
                dve.memset(rt.padding[:, 0:D + E], 0.0)
                dve.memset(spare[:, :, 0:D + E], 0.0)
                dve.memset(rt.ones[:], 1.0)
                dve.wait_ge(loaded, LOADS)
                dve.tensor_scalar(rt.padding[:, D + E:ROW].bitcast(I32), rt.ids[:, 0:1], float(T), None, ALU.add)
                dve.tensor_scalar(spare[:, :, D + E].bitcast(I32), rt.ids[:, 1:1 + SPARES], float(T), None, ALU.add).then_inc(padding_ready, 1)
                dve.tensor_copy(rt.carry[:], rt.slabs[:])
                dve.tensor_copy(rt.before[:], rt.before_f[:])
                dve.tensor_scalar(rt.ties[:], rt.order[:], -2.0 ** -126, None, ALU.mult)
                dve.tensor_reduce(w_abs[:], w_raw[:].rearrange("p c o -> p (c o)"), AX.X, ALU.add,
                                  apply_absolute_value=True).then_inc(w_abs_ready, 1)
                for b in range(B):
                    last = dve.tensor_copy(cond_b[:, b, :], cond_c[:, b:b + 1].broadcast_to([COND, P]))
                last.then_inc(cond_ready, 1)
                dve.wait_ge(totals_ready, 1)
                dve.tensor_scalar(w_scale[:], w_total, 1.0 / (D * D), 1e-8, ALU.mult, ALU.add).then_inc(step, 1)
                dve.wait_ge(step, 1)
                dve.reciprocal(w_inv[:], w_scale[:]).then_inc(step, 1)
                dve.wait_ge(step, 2)
                dve.tensor_scalar(w_u[:], w_raw[:], w_inv[:, 0:1], None, ALU.mult)
                dve.tensor_scalar(w_scale127[:], w_scale[:], 1.0 / 127.0, None, ALU.mult).then_inc(step, 1)
                dve.wait_ge(step, 3)
                dve.tensor_scalar(w_u[:], w_u[:], ROUND, ROUND, ALU.add, ALU.subtract).then_inc(step, 1)
                dve.wait_ge(step, 4)
                dve.tensor_scalar(w_ter[:], w_u[:], 1.0, -1.0, ALU.min, ALU.max).then_inc(w_ready, 1)
                dve.wait_ge(totals_ready, 2)
                dve.tensor_scalar(half_cond[:], cond_ps, 0.5, None, ALU.mult).then_inc(step, 1)
                dve.wait_ge(step, 5)

                with dve.Fori(0, B) as it:
                    steps = Steps(PER_BODY)
                    steps.n = SETUP
                    dve.wait_ge(exp_ready, it + 1)
                    for r in range(2):
                        for t in range(4):
                            last = dve.bn_stats(stats[r][:, t, :], yacc_f[:, tile(it, r, t)])
                        last.then_inc(step, steps.up())
                        dve.wait_ge(step, steps.here(it))
                        apart(dve, marks)
                        for t in range(4):
                            last = dve.bn_aggr(mv[r][:, t, :], stats[r][:, t, :])
                        last.then_inc(step, steps.up())
                        dve.wait_ge(step, steps.here(it))
                        dve.tensor_scalar(rstd[r][:], mv[r][:, :, 1], EPS, None, ALU.add).then_inc(var_ready, 1)
                    for r in range(2):
                        dve.wait_ge(rstd_ready, 2 * it + r + 1)
                        for t in range(4):
                            last = dve.tensor_scalar(yl[r][:, t, :], yacc_f[:, tile(it, r, t)], mv[r][:, t, 0:1],
                                                     rstd[r][:, t:t + 1], ALU.subtract, ALU.mult)
                        last.then_inc(step, steps.up())
                        dve.wait_ge(step, steps.here(it))
                        dve.tensor_tensor(yl[r][:], yl[r][:], g_out[:].unsqueeze(1).broadcast_to([P, 4, D]),
                                          ALU.mult).then_inc(step, steps.up())
                        dve.wait_ge(step, steps.here(it))
                        dve.tensor_reduce(a_scale[r][:], yl[r][:], AX.X, ALU.max, apply_absolute_value=True).then_inc(step, steps.up())
                        dve.wait_ge(step, steps.here(it))
                        dve.tensor_scalar(a_scale[r][:], a_scale[r][:], 1e-8, None, ALU.add).then_inc(step, steps.up())
                        dve.wait_ge(step, steps.here(it))
                        dve.tensor_scalar(out_scale[r][:], a_scale[r][:], w_scale127[:, 0:1], None, ALU.mult)
                        dve.reciprocal(a_inv[r][:], a_scale[r][:]).then_inc(step, steps.up())
                        dve.wait_ge(step, steps.here(it))
                        for t in range(4):
                            last = dve.tensor_scalar(yl[r][:, t, :], yl[r][:, t, :], a_inv[r][:, t:t + 1], 127.0,
                                                     ALU.mult, ALU.mult)
                        last.then_inc(step, steps.up())
                        dve.wait_ge(step, steps.here(it))
                        dve.tensor_scalar(yl[r][:], yl[r][:], 127.0, -128.0, ALU.min, ALU.max).then_inc(step, steps.up())
                        dve.wait_ge(step, steps.here(it))
                        dve.tensor_scalar(z[r][:], yl[r][:], ROUND, ROUND, ALU.add, ALU.subtract).then_inc(z_ready, 1)
                    dve.wait_ge(rows_free, it + 1)
                    for r in range(2):
                        dve.wait_ge(f_ready, 2 * it + r + 1)
                        for t in range(4):
                            last = dve.scalar_tensor_tensor(x1[r][:, t, :], f_ps[r][:, t, :], out_scale[r][:, t:t + 1],
                                                            xs_f[:, tile(it, r, t)], ALU.mult, ALU.add)
                        last.then_inc(x1_ready, 1)
                    for r in range(2):
                        for c in range(DC):
                            dve.wait_ge(hi_ready, 2 * DC * it + DC * r + c + 1)
                            cols = bass.ds(2 * CW * it + CW * r, CW)
                            last = dve.tensor_tensor(xT_lo[:, c, cols], x1T[r][:, c, :], xT_hi[:, c, cols].bitcast(F32), ALU.subtract)
                        last.then_inc(lo_ready, 1)
                    dve.wait_ge(logits_ready, 2 * it + 2)
                    for r in range(2):
                        last = dve.scalar_tensor_tensor(gate[:, GROUP * r:GROUP * (r + 1), :], logits[r], 0.5,
                                                        half_cond[:, bass.ds(it, 1), :].broadcast_to([P, GROUP, E]), ALU.mult, ALU.add)
                    last.then_inc(step, steps.up())
                    dve.wait_ge(step, steps.here(it))
                    dve.tensor_reduce(row[:], gate[:], AX.X, ALU.max).then_inc(step, steps.up())
                    dve.wait_ge(step, steps.here(it))
                    dve.tensor_tensor(gate[:], gate[:], row[:].unsqueeze(2).broadcast_to([P, PAIR, E]),
                                      ALU.subtract).then_inc(logits_read, 1)
                    dve.wait_ge(exp_ready, it + 2)
                    dve.tensor_reduce(row[:], gate[:], AX.X, ALU.add).then_inc(step, steps.up())
                    dve.wait_ge(step, steps.here(it))
                    dve.reciprocal(row[:], row[:]).then_inc(step, steps.up())
                    dve.wait_ge(step, steps.here(it))
                    dve.tensor_tensor(gate[:], gate[:], row[:].unsqueeze(2).broadcast_to([P, PAIR, E]),
                                      ALU.mult).then_inc(step, steps.up())
                    dve.wait_ge(step, steps.here(it))
                    gate_top_two(dve, step, steps, it, gate[:], (above[:], more[:], rt.ties[:], rt.rank[:]), top[:]
                                 ).then_inc(step, steps.up())
                    dve.tensor_scalar(rt.chosen[:], rt.rank[:], 1.5, None, ALU.is_lt).then_inc(chosen_ready, 1)
                    dve.wait_ge(step, steps.here(it))
                    dve.tensor_reduce(row[:], top[:], AX.X, ALU.add).then_inc(step, steps.up())
                    dve.wait_ge(step, steps.here(it))
                    dve.tensor_scalar(row[:], row[:], 1e-20, None, ALU.add).then_inc(step, steps.up())
                    dve.wait_ge(step, steps.here(it))
                    dve.reciprocal(row[:], row[:]).then_inc(step, steps.up())
                    dve.wait_ge(step, steps.here(it))
                    dve.tensor_tensor(rt.rows[:, :, D:D + E], top[:], row[:].unsqueeze(2).broadcast_to([P, PAIR, E]), ALU.mult)
                    dve.tensor_copy(rt.rows[:, :, D + E].bitcast(I32), rt.ids[:, bass.ds(QT * it, PAIR)])
                    dve.wait_ge(counted, it + 1)
                    place_rows(dve, step, steps, it, rt, counts, totals).then_inc(placed, 1)
                    dve.wait_ge(placed, it + 1)
                    assert steps.n == SETUP + PER_BODY, steps.n - SETUP

            @block.scalar
            def _(act):
                act.wait_ge(loaded, LOADS)
                act.sem_inc(exp_ready, 1)
                with act.Fori(0, B) as it:
                    for r in range(2):
                        act.wait_ge(z_turned, 2 * it + r + 1)
                        act.activation(zT[r][:], zT_ps[:], ACT.Copy).then_inc(zT_ready, 1)
                    for r in range(2):
                        for c in range(DC):
                            act.wait_ge(x1_turned, 2 * DC * it + DC * r + c + 1)
                            act.activation(x1T[r][:, c, :], x_ps[c][:], ACT.Copy).then_inc(x1T_ready, 1)
                        for c in range(DC):
                            act.wait_ge(x1T_ready, 2 * DC * it + DC * r + c + 1)
                            act.activation(xT_hi[:, c, bass.ds(2 * CW * it + CW * r, CW)], x1T[r][:, c, :],
                                           ACT.Copy).then_inc(hi_ready, 1)
                        act.wait_ge(x1_ready, 2 * it + r + 1)
                        act.activation(xs[:, bass.ds(QT * it + 4 * r, 4), :], x1[r], ACT.Copy).then_inc(xs_ready, 1)
                    act.wait_ge(logits_read, it + 1)
                    act.activation(gate[:], gate[:], ACT.Exp).then_inc(exp_ready, 1)

            @block.tensor
            def _(pe):
                pe.wait_ge(ones_set, 1)
                pe.wait_ge(w_abs_ready, 1)
                pe.matmul(w_total, ones[:], w_abs[:], start=True, stop=True).then_inc(totals_ready, 1)
                pe.wait_ge(cond_ready, 1)
                for b in range(B):
                    last = pe.matmul(cond_ps[:, b, :], cond_b[:, b, :], wg[:], start=True, stop=True)
                last.then_inc(totals_ready, 1)
                pe.wait_ge(w_ready, 1)
                with pe.Fori(0, B) as it:
                    for r in range(2):
                        pe.wait_ge(z_ready, 2 * it + r + 1)
                        for c in range(DC):
                            for t in range(4):
                                last = pe.transpose(zT_ps[:, c, P * t:P * t + P], z[r][:, t, P * c:P * c + P], ident_bf)
                        last.then_inc(z_turned, 1)
                        pe.wait_ge(zT_ready, 2 * it + r + 1)
                        for t in range(4):
                            for c in range(DC):
                                last = pe.matmul(f_ps[r][:, t, :], zT[r][:, c, P * t:P * t + P], w_ter[:, c, :],
                                                 start=(c == 0), stop=(c == DC - 1))
                        last.then_inc(f_ready, 1)
                    for r in range(2):
                        pe.wait_ge(x1_ready, 2 * it + r + 1)
                        for c in range(DC):
                            if r:
                                pe.wait_ge(x1T_ready, 2 * DC * it + c + 1)
                            for t in range(4):
                                last = pe.transpose(x_ps[c][:, P * t:P * t + P], x1[r][:, t, P * c:P * c + P], ident)
                            last.then_inc(x1_turned, 1)
                    for r in range(2):
                        pe.wait_ge(x1T_ready, 2 * DC * it + DC * (r + 1))
                        for t in range(4):
                            for c in range(DC):
                                last = pe.matmul(logits[r][:, t, :], x1T[r][:, c, P * t:P * t + P], wt[:, c, :],
                                                 start=(c == 0), stop=(c == DC - 1))
                        last.then_inc(logits_ready, 1)
                    pe.wait_ge(chosen_ready, it + 1)
                    count_chosen(pe, rt, counts, totals).then_inc(counted, 1)


def shared_expert_stage(nc, sbuf, psum, sem, aps, keep, routing, routed_rows, mixed, scattered):
    yacc, xT_hi, xT_lo, w_raw, w_in, w1_hi, w1_lo, w1_in, rows, rows_in = keep
    rt = routing
    GU = 2 * M1
    STEPS = 8
    assert STEPS == E
    with ExitStack() as st:
        w_hi = [sbuf(st, f"sh_hi{i}", [P, W1COLS], F32R) for i in range(2)]
        w_lo = [sbuf(st, f"sh_lo{i}", [P, W1COLS], F32R) for i in range(2)]
        slope = sbuf(st, "sh_slope", [P, CW])
        leaky = sbuf(st, "sh_leaky", [P, CW])
        h = [sbuf(st, f"sh_h{i}", [P, CW]) for i in range(2)]
        h_hi = [sbuf(st, f"sh_h_hi{i}", [P, CW], F32R) for i in range(2)]
        h_lo = [sbuf(st, f"sh_h_lo{i}", [P, CW], F32R) for i in range(2)]
        g_ps = [psum(st, f"sh_g_ps{i}", [P, CW]) for i in range(2)]
        u_ps = [psum(st, f"sh_u_ps{i}", [P, CW]) for i in range(2)]
        o_ps = [psum(st, f"sh_o_ps{i}", [P, 4, D]) for i in range(2)]
        w_hi_ready, w_lo_ready, up_ready, slope_ready, leaky_ready, h_ready, h_hi_ready, h_lo_ready, down_ready, added = (
            sem("sh_" + n) for n in ("w_hi_ready", "w_lo_ready", "up_ready", "slope_ready", "leaky_ready", "h_ready", "h_hi_ready",
                                     "h_lo_ready", "down_ready", "added"))
        w1_hi_ready = sem("sh_w1_hi_ready")
        table_step, table_ready, stored = sem("sh_table_step"), sem("sh_table_ready"), sem("sh_stored")

        with nc.Block() as block:
            @block.sync
            def _(sp):
                sp.dma_start(mixed[T:OUT_ROWS, :].rearrange("(n p) d -> p n d", p=P),
                             rt.padding[:, 0:D].unsqueeze(1).broadcast_to([P, 1 + SPARES, D])).then_inc(stored, 16)
                sp.wait_ge(table_ready, 1)
                store_padding(sp, rt, routed_rows, stored)
                sp.wait_ge(stored, 16 * (1 + E))
                sp.wait_ge(scattered, 16 * NT * TOP)
                load_first_rows(sp, nc, rt, routed_rows, rows, rows_in)
                tiles = mixed[0:T, :].rearrange("(n p) d -> p n d", p=P)
                for g in range(4):
                    sp.wait_ge(added, 4 + g + 1)
                    sp.dma_start(tiles[:, 4 * g:4 * g + 4, :], yacc[:, 4 * g:4 * g + 4, :]).then_inc(stored, 16)
                sp.wait_ge(stored, 16 * (1 + E + 4))

            @block.gpsimd
            def _(pool):
                scatter_rows(pool, rt, range(PAIR), routed_rows, scattered)
                pool.wait_ge(scattered, 16 * NT * TOP)

            @block.scalar
            def _(act):
                for i in range(2):
                    act.wait_ge(w_in[i], 16)
                    act.activation(w_hi[i][:], w_raw[i][:], ACT.Copy).then_inc(w_hi_ready, 1)
                for s in range(STEPS):
                    act.wait_ge(up_ready, s + 1)
                    wait(act, leaky_ready, s)
                    act.activation(slope[:], g_ps[s % 2][:], ACT.Copy, scale=LEAKY).then_inc(slope_ready, 1)
                    wait(act, down_ready, s - 1)
                    act.wait_ge(h_ready, s + 1)
                    act.activation(h_hi[s % 2][:], h[s % 2][:], ACT.Copy).then_inc(h_hi_ready, 1)
                    if s == 0:
                        act.wait_ge(w1_in, 16 * E)
                    act.activation(w1_hi[:, s, :], w1_lo[:, s, :].bitcast(F32), ACT.Copy).then_inc(w1_hi_ready, 1)

            @block.vector
            def _(dve):
                def hidden(s):
                    dve.wait_ge(slope_ready, s + 1)
                    dve.tensor_tensor(leaky[:], slope[:], g_ps[s % 2][:], ALU.max).then_inc(leaky_ready, 1)
                    dve.wait_ge(leaky_ready, s + 1)
                    dve.tensor_tensor(h[s % 2][:], leaky[:], u_ps[s % 2][:], ALU.mult).then_inc(h_ready, 1)

                def low(s):
                    dve.wait_ge(h_hi_ready, s + 1)
                    dve.tensor_tensor(h_lo[s % 2][:], h[s % 2][:], h_hi[s % 2][:].bitcast(F32), ALU.subtract).then_inc(h_lo_ready, 1)

                for i in range(2):
                    dve.wait_ge(w_hi_ready, i + 1)
                    dve.tensor_tensor(w_lo[i][:], w_raw[i][:], w_hi[i][:].bitcast(F32), ALU.subtract).then_inc(w_lo_ready, 1)
                make_table(dve, rt, table_step, table_ready)
                hidden(0)
                low(0)
                for s in range(STEPS):
                    if s + 1 < STEPS:
                        hidden(s + 1)
                    dve.wait_ge(down_ready, s + 1)
                    sums = yacc[:, 4 * (s % 4):4 * (s % 4) + 4, :]
                    if s < 4:
                        dve.tensor_copy(sums, o_ps[s % 2][:]).then_inc(added, 1)
                    else:
                        dve.wait_ge(added, s - 3)
                        dve.tensor_tensor(sums, o_ps[s % 2][:], sums, ALU.add).then_inc(added, 1)
                    if s + 1 < STEPS:
                        low(s + 1)
                    dve.wait_ge(w1_hi_ready, s + 1)
                    dve.tensor_tensor(w1_lo[:, s, :], w1_lo[:, s, :].bitcast(F32), w1_hi[:, s, :].bitcast(F32), ALU.subtract)

            @block.tensor
            def _(pe):
                def up(s):
                    i, x = s // 4, slice(CW * (s % 4), CW * (s % 4) + CW)
                    pe.wait_ge(w_lo_ready, i + 1)
                    for ps, first in ((g_ps[s % 2], 0), (u_ps[s % 2], M1)):
                        for c in range(DC):
                            cols = slice(GU * c + first, GU * c + first + M1)
                            pe.matmul(ps[:], w_hi[i][:, cols], xT_hi[:, c, x], start=(c == 0), stop=False)
                            pe.matmul(ps[:], w_hi[i][:, cols], xT_lo[:, c, x], start=False, stop=False)
                            last = pe.matmul(ps[:], w_lo[i][:, cols], xT_hi[:, c, x], start=False, stop=(c == DC - 1))
                    last.then_inc(up_ready, 1)

                def down(s):
                    i, cols = s // 4, slice(DC * GU, W1COLS)
                    wait(pe, added, s - 1)
                    pe.wait_ge(h_lo_ready, s + 1)
                    for t in range(4):
                        tokens = slice(P * t, P * t + P)
                        pe.matmul(o_ps[s % 2][:, t, :], h_hi[s % 2][:, tokens], w_hi[i][:, cols], start=True, stop=False)
                        pe.matmul(o_ps[s % 2][:, t, :], h_hi[s % 2][:, tokens], w_lo[i][:, cols], start=False, stop=False)
                        last = pe.matmul(o_ps[s % 2][:, t, :], h_lo[s % 2][:, tokens], w_hi[i][:, cols], start=False, stop=True)
                    last.then_inc(down_ready, 1)

                up(0)
                for s in range(STEPS):
                    if s + 1 < STEPS:
                        up(s + 1)
                    down(s)


def pair_attention_stage(nc, sbuf, psum, sem, aps, keep, routing, routed_rows, mixed, out):
    xs, yacc, ident, power4, w2, w2_in, scattered = keep
    rt = routing
    srow = rt.group_rows
    with ExitStack() as st:
        ln_w = [sbuf(st, f"ln{i}_w", [P, DC]) for i in (1, 2)]
        ln_b = [sbuf(st, f"ln{i}_b", [P, DC]) for i in (1, 2)]
        w_qkv = sbuf(st, "w_qkv", [P, DC, QKV])
        w_proj = sbuf(st, "w_proj", [P, DC, D])
        w_router = sbuf(st, "w_router", [P, DC, E])
        stats = [sbuf(st, f"pa_stats{r}", [P, 4, 6]) for r in range(2)]
        mv = [sbuf(st, f"pa_mv{r}", [P, 4, 2]) for r in range(2)]
        rstd = [sbuf(st, f"pa_rstd{r}", [P, 4]) for r in range(2)]
        xh = [sbuf(st, f"pa_xh{r}", [P, 4, D]) for r in range(2)]
        lT = [sbuf(st, f"pa_lT{r}", [P, DC, CW]) for r in range(2)]
        qkv_sb = [sbuf(st, f"pa_qkv{r}", [P, 4, QKV]) for r in range(2)]
        prod = sbuf(st, "pa_prod", [P, 2, 2, H, HD])
        score = [sbuf(st, f"pa_score{r}", [P, 2, 2, H]) for r in range(2)]
        peak = [sbuf(st, f"pa_peak{r}", [P, 2, H]) for r in range(2)]
        attn = [sbuf(st, f"pa_attn{r}", [P, 4, D]) for r in range(2)]
        attnT = [sbuf(st, f"pa_attnT{r}", [P, DC, CW]) for r in range(2)]
        ha = [sbuf(st, f"pa_ha{r}", [P, 4, D]) for r in range(2)]
        gate = sbuf(st, "pa_gate", [P, PAIR, E])
        row = sbuf(st, "pa_row", [P, PAIR])
        above = sbuf(st, "pa_above", [P, PAIR, E, E])
        more = sbuf(st, "pa_more", [P, PAIR, E, E])
        x_ps = [psum(st, f"pa_x_ps{c}", [P, CW]) for c in range(DC)]
        q_ps = [psum(st, f"pa_q_ps{j}", [P, CW]) for j in range(4)]
        p_ps = psum(st, "pa_p_ps", [P, 4, D])
        both_logits = p_ps[:].rearrange("p (r h) d -> p r h d", r=2)[:, :, 0, 0:GROUP * E].rearrange("p r (j e) -> p r j e", e=E)
        logits = [both_logits[:, r] for r in range(2)]
        counts = p_ps[:, 0, GROUP * E:(GROUP + PAIR) * E].rearrange("p (j e) -> p j e", e=E)
        totals = p_ps[:, 0, (GROUP + PAIR) * E:(GROUP + PAIR + 1) * E]
        names = ("loaded step var_ready rstd_ready xh_ready turned lT_ready qkv_ready qkv_read prod_ready first_ready scores_ready "
                 "exp_ready attn_ready attnT_ready proj_ready ha_ready summed logits_ready logits_read gate_exp_ready "
                 "chosen_ready counted placed rows_free table_step table_ready stored mixed_in tiles_in").split()
        (loaded, step, var_ready, rstd_ready, xh_ready, turned, lT_ready, qkv_ready, qkv_read, prod_ready, first_ready, scores_ready,
         exp_ready, attn_ready, attnT_ready, proj_ready, ha_ready, summed, logits_ready, logits_read,
         gate_exp_ready, chosen_ready, counted, placed, rows_free, table_step, table_ready, stored, mixed_in, tiles_in) = (sem("pa_" + n) for n in names)
        marks = sem("pa_marks")
        LOADS = 16 * 7
        PER_BODY = 30
        SCATTERS = 16 * 2 * 4 * TOP
        POS = QT // 4

        def group_tiles(tiles, it, r):
            return tiles[:].rearrange("p (b i) d -> p b i d", b=B)[:, :, bass.ds(4 * it + 2 * r, 2), :]

        def tile(it, r, j):
            return bass.ds(D * (4 * it + QT * (j // 2) + 2 * r + j % 2), D)

        def heads(ap):
            return ap.rearrange("p (k d) -> p k d", d=HD).unsqueeze(2).broadcast_to([P, KV, H // KV, HD])

        def by_kv(ap):
            return ap.rearrange("p (k r d) -> p k r d", k=KV, d=HD)

        def per_head(ap):
            return ap.rearrange("p (k r) -> p k r", k=KV).unsqueeze(3).broadcast_to([P, KV, H // KV, HD])

        def qkv(r, b, i, part):
            first, last = ((0, D), (D, D + KV * HD), (D + KV * HD, QKV))[part]
            return qkv_sb[r][:, 2 * b + i, first:last]

        with nc.Block() as block:
            @block.sync
            def _(sp):
                def load_tiles(it):
                    tiles = mixed[0:T, :].rearrange("(n p) d -> p n d", p=P)
                    for b in range(B):
                        group = slice(QT * b + 4 * it, QT * b + 4 * it + 4)
                        sp.dma_start(yacc[:, group, :], tiles[:, group, :]).then_inc(mixed_in, 16)

                load_tiles(0)
                for i in range(2):
                    sp.dma_start(ln_w[i][:], aps[f"ln{i + 1}_w"]).then_inc(loaded, 16)
                    sp.dma_start(ln_b[i][:], aps[f"ln{i + 1}_b"]).then_inc(loaded, 16)
                sp.dma_start(w_qkv[:], aps["qkvT"].rearrange("(c p) o -> p c o", p=P)).then_inc(loaded, 16)
                sp.dma_start(w_proj[:], aps["projT"].rearrange("(c p) o -> p c o", p=P)).then_inc(loaded, 16)
                sp.dma_start(w_router[:], aps["routerT"].rearrange("(c p) e -> p c e", p=P)).then_inc(loaded, 16)
                for it in range(POS):
                    if it:
                        load_tiles(it)
                    sp.wait_ge(mixed_in, 16 * B * (it + 1))
                    sp.sem_inc(tiles_in, 1)
                for e in range(E):
                    sp.dma_start(w2[:, e, :].bitcast(F32), aps["m2_w"][e]).then_inc(w2_in, 16)
                sp.dma_start(out[T:OUT_ROWS, :].rearrange("(n p) d -> p n d", p=P),
                             rt.padding[:, 0:D].unsqueeze(1).broadcast_to([P, 1 + SPARES, D])).then_inc(stored, 16)
                tiles = out[0:T, :].rearrange("(n p) d -> p n d", p=P)
                with sp.Fori(0, POS) as it:
                    sp.wait_ge(summed, 2 * it + 3)
                    for b in range(B):
                        group = bass.ds(QT * b + 4 * it, 4)
                        sp.dma_start(tiles[:, group, :], xs[:, group, :]).then_inc(stored, 16)
                sp.wait_ge(stored, 16 * (1 + POS * B))

            @block.gpsimd
            def _(pool):
                pool.sem_inc(summed, 1)
                pool.sem_inc(rows_free, 1)

                def scatter(it):
                    pool.wait_ge(placed, it + 1)
                    scatter_rows(pool, rt, range(PAIR), routed_rows, scattered)
                    pool.wait_ge(scattered, SCATTERS * (it + 1))
                    pool.sem_inc(rows_free, 1)

                def body(it, first):
                    for norm in range(2):
                        for r in range(2):
                            pool.wait_ge(var_ready, 4 * it + 2 * norm + r + 1)
                            pool.tensor_tensor(rstd[r][:], rstd[r][:], power4, ALU.pow).then_inc(rstd_ready, 1)
                        if norm == 0 and not first:
                            scatter(it - 1)
                    for r in range(2):
                        pool.wait_ge(ha_ready, 2 * it + r + 1)
                        pool.tensor_tensor(group_tiles(xs, it, r), group_tiles(xs, it, r),
                                           ha[r][:].rearrange("p (b i) d -> p b i d", b=B), ALU.add).then_inc(summed, 1)

                body(0, True)
                with pool.Fori(1, POS) as it:
                    body(it, False)
                pool.wait_ge(placed, POS)
                scatter_rows(pool, rt, range(EARLY), routed_rows, scattered)

            @block.vector
            def _(dve):
                yacc_f = flat(yacc)
                dve.tensor_copy(rt.carry[:], rt.slabs[:])
                with dve.Fori(0, POS) as it:
                    steps = Steps(PER_BODY)
                    dve.wait_ge(gate_exp_ready, it + 1)
                    dve.wait_ge(summed, 2 * it + 1)
                    dve.wait_ge(tiles_in, it + 1)

                    def moments(source, r):
                        for j in range(4):
                            last = dve.bn_stats(stats[r][:, j, :], source(j))
                        last.then_inc(step, steps.up())
                        dve.wait_ge(step, steps.here(it))
                        apart(dve, marks)
                        for j in range(4):
                            last = dve.bn_aggr(mv[r][:, j, :], stats[r][:, j, :])
                        last.then_inc(step, steps.up())
                        dve.wait_ge(step, steps.here(it))
                        dve.tensor_scalar(rstd[r][:], mv[r][:, :, 1], EPS, None, ALU.add).then_inc(var_ready, 1)

                    def normalise(source, r, norm, out):
                        dve.wait_ge(rstd_ready, 4 * it + 2 * norm + r + 1)
                        for j in range(4):
                            last = dve.tensor_scalar(out[r][:, j, 0:D], source(j), mv[r][:, j, 0:1], rstd[r][:, j:j + 1],
                                                     ALU.subtract, ALU.mult)
                        last.then_inc(xh_ready, 1)

                    for r in range(2):
                        moments(lambda j: yacc_f[:, tile(it, r, j)], r)
                    for r in range(2):
                        normalise(lambda j: yacc_f[:, tile(it, r, j)], r, 0, xh)
                    for r in range(2):
                        if r:
                            dve.wait_ge(attn_ready, 2 * it + r)
                        dve.wait_ge(qkv_read, 2 * it + r + 1)
                        for i in range(2):
                            for b in range(B):
                                last = dve.tensor_tensor(prod[:, i, b].rearrange("p (k r) d -> p k r d", k=KV),
                                                         by_kv(qkv(r, 1, i, 0)), heads(qkv(r, b, i, 1)), ALU.mult)
                        last.then_inc(step, steps.up())
                        dve.wait_ge(step, steps.here(it))
                        dve.tensor_reduce(score[r][:], prod[:], AX.X, ALU.add).then_inc(step, steps.up())
                        dve.wait_ge(step, steps.here(it))
                        dve.tensor_tensor(peak[r][:], score[r][:, :, 0, :], score[r][:, :, 1, :], ALU.max).then_inc(step, steps.up())
                        dve.wait_ge(step, steps.here(it))
                        dve.tensor_tensor(score[r][:], score[r][:], peak[r][:].unsqueeze(2).broadcast_to([P, 2, 2, H]),
                                          ALU.subtract).then_inc(scores_ready, 1)
                        dve.wait_ge(exp_ready, 2 * it + r + 1)
                        dve.tensor_tensor(peak[r][:], score[r][:, :, 0, :], score[r][:, :, 1, :], ALU.add).then_inc(step, steps.up())
                        dve.wait_ge(step, steps.here(it))
                        dve.reciprocal(peak[r][:], peak[r][:]).then_inc(step, steps.up())
                        dve.wait_ge(step, steps.here(it))
                        dve.tensor_tensor(score[r][:], score[r][:], peak[r][:].unsqueeze(2).broadcast_to([P, 2, 2, H]),
                                          ALU.mult).then_inc(step, steps.up())
                        dve.wait_ge(step, steps.here(it))
                        for i in range(2):
                            for b in range(B):
                                last = dve.tensor_tensor(prod[:, i, b].rearrange("p (k r) d -> p k r d", k=KV),
                                                         heads(qkv(r, b, i, 2)), per_head(score[r][:, i, b]), ALU.mult)
                        last.then_inc(prod_ready, 1)
                        dve.wait_ge(prod_ready, 2 * it + r + 1)
                        dve.tensor_tensor(attn[r][:, 2:4, :], prod[:, :, 0].rearrange("p i h d -> p i (h d)"),
                                          prod[:, :, 1].rearrange("p i h d -> p i (h d)"), ALU.add).then_inc(attn_ready, 1)
                    for r in range(2):
                        dve.wait_ge(proj_ready, 2 * it + r + 1)
                        dve.tensor_tensor(ha[r][:].rearrange("p (b i) d -> p b i d", b=B),
                                          p_ps[:].rearrange("p (b i) d -> p b i d", b=B),
                                          group_tiles(yacc, it, r), ALU.add).then_inc(ha_ready, 1)
                        dve.wait_ge(ha_ready, 2 * it + r + 1)
                        moments(lambda j: ha[r][:, j, :], r)
                        if r == 0:
                            dve.wait_ge(rows_free, it + 1)
                        normalise(lambda j: ha[r][:, j, :], r, 1, srow)
                    for r in range(2):
                        dve.tensor_copy(srow[r][:, :, D + E].bitcast(I32).rearrange("p (b i) -> p b i", b=B),
                                        rt.ids[:].rearrange("p (b i) -> p b i", b=B)[:, :, bass.ds(4 * it + 2 * r, 2)])
                    dve.wait_ge(logits_ready, 2 * it + 2)
                    dve.tensor_reduce(row[:].rearrange("p (r j) -> p r j", r=2), both_logits, AX.X, ALU.max).then_inc(step, steps.up())
                    dve.wait_ge(step, steps.here(it))
                    dve.tensor_tensor(by_group(gate), both_logits,
                                      row[:].rearrange("p (r j) -> p r j", r=2).unsqueeze(3).broadcast_to([P, 2, GROUP, E]),
                                      ALU.subtract).then_inc(logits_read, 1)
                    dve.wait_ge(gate_exp_ready, it + 2)
                    dve.tensor_reduce(row[:], gate[:], AX.X, ALU.add).then_inc(step, steps.up())
                    dve.wait_ge(step, steps.here(it))
                    dve.reciprocal(row[:], row[:]).then_inc(step, steps.up())
                    dve.wait_ge(step, steps.here(it))
                    dve.tensor_tensor(gate[:], gate[:], row[:].unsqueeze(2).broadcast_to([P, PAIR, E]),
                                      ALU.mult).then_inc(step, steps.up())
                    dve.wait_ge(step, steps.here(it))
                    gate_top_two(dve, step, steps, it, gate[:], (above[:], more[:], rt.ties[:], rt.rank[:]), rt.rows[:, :, D:D + E])
                    dve.tensor_scalar(rt.chosen[:], rt.rank[:], 1.5, None, ALU.is_lt).then_inc(chosen_ready, 1)
                    dve.wait_ge(counted, it + 1)
                    place_rows(dve, step, steps, it, rt, counts, totals).then_inc(placed, 1)
                    dve.wait_ge(placed, it + 1)
                    assert steps.n == PER_BODY, steps.n

                make_table(dve, rt, table_step, table_ready)

            @block.scalar
            def _(act):
                act.wait_ge(loaded, LOADS)
                act.sem_inc(gate_exp_ready, 1)
                with act.Fori(0, POS) as it:
                    def evacuate(r, norm, out, n):
                        for c in range(DC):
                            act.wait_ge(turned, 6 * DC * it + n + DC * r + c + 1)
                            if norm is None:
                                act.activation(out[r][:, c, :], x_ps[c][:], ACT.Copy).then_inc(attnT_ready, 1)
                            else:
                                act.activation(out[r][:, c, :], x_ps[c][:], ACT.Identity, scale=ln_w[norm][:, c:c + 1],
                                               bias=ln_b[norm][:, c:c + 1]).then_inc(lT_ready, 1)

                    for r in range(2):
                        evacuate(r, 0, lT, 0)
                    for r in range(2):
                        act.wait_ge(qkv_ready, 2 * it + r + 1)
                        for j in range(4):
                            last = act.activation(qkv_sb[r][:, j, :], q_ps[j][:, 0:QKV], ACT.Copy)
                        last.then_inc(qkv_read, 1)
                        act.wait_ge(qkv_read, 2 * it + r + 1)
                        for i in range(2):
                            last = act.activation(by_kv(attn[r][:, i, :]), heads(qkv(r, 0, i, 2)), ACT.Copy)
                        last.then_inc(first_ready, 1)
                        if r:
                            evacuate(0, None, attnT, 2 * DC)
                        act.wait_ge(scores_ready, 2 * it + r + 1)
                        act.activation(score[r][:], score[r][:], ACT.Exp, scale=HD ** -0.5).then_inc(exp_ready, 1)
                    evacuate(1, None, attnT, 2 * DC)
                    for r in range(2):
                        act.wait_ge(qkv_ready, 2 * it + 2)
                        evacuate(r, 1, lT, 4 * DC)
                    act.wait_ge(logits_read, it + 1)
                    act.activation(gate[:], gate[:], ACT.Exp).then_inc(gate_exp_ready, 1)

            @block.tensor
            def _(pe):
                pe.wait_ge(loaded, LOADS)
                with pe.Fori(0, POS) as it:
                    def turn(source, r, read):
                        for c in range(DC):
                            if read(c):
                                pe.wait_ge(*read(c))
                            for j in range(4):
                                last = pe.transpose(x_ps[c][:, P * j:P * j + P], source[r][:, j, P * c:P * c + P], ident)
                            last.then_inc(turned, 1)

                    for r in range(2):
                        pe.wait_ge(xh_ready, 4 * it + r + 1)
                        turn(xh, r, lambda c: (lT_ready, 4 * DC * it + c + 1) if r else None)
                    for r in range(2):
                        if r:
                            pe.wait_ge(qkv_read, 2 * it + r)
                        pe.wait_ge(lT_ready, 4 * DC * it + DC * (r + 1))
                        for j in range(4):
                            for c in range(DC):
                                last = pe.matmul(q_ps[j][:, 0:QKV], lT[r][:, c, P * j:P * j + P], w_qkv[:, c, :],
                                                 start=(c == 0), stop=(c == DC - 1))
                        last.then_inc(qkv_ready, 1)
                    for r in range(2):
                        pe.wait_ge(first_ready, 2 * it + r + 1)
                        pe.wait_ge(attn_ready, 2 * it + r + 1)
                        turn(attn, r, lambda c: (attnT_ready, 2 * DC * it + DC * (r - 1) + c + 1) if r else
                             (lT_ready, 4 * DC * it + DC + c + 1))
                        if r:
                            pe.wait_ge(ha_ready, 2 * it + r)
                        pe.wait_ge(attnT_ready, 2 * DC * it + DC * (r + 1))
                        for j in range(4):
                            for c in range(DC):
                                last = pe.matmul(p_ps[:, j, :], attnT[r][:, c, P * j:P * j + P], w_proj[:, c, :],
                                                 start=(c == 0), stop=(c == DC - 1))
                        last.then_inc(proj_ready, 1)
                    for r in range(2):
                        pe.wait_ge(xh_ready, 4 * it + 2 + r + 1)
                        turn(srow, r, lambda c: (lT_ready, 4 * DC * it + 2 * DC + c + 1) if r else
                             (attnT_ready, 2 * DC * it + DC + c + 1))
                        if r == 0:
                            pe.wait_ge(ha_ready, 2 * it + 2)
                        pe.wait_ge(lT_ready, 4 * DC * it + 2 * DC + DC * (r + 1))
                        for j in range(4):
                            for c in range(DC):
                                last = pe.matmul(logits[r][:, j, :], lT[r][:, c, P * j:P * j + P],
                                                 w_router[:, c, :], start=(c == 0), stop=(c == DC - 1))
                        last.then_inc(logits_ready, 1)
                    pe.wait_ge(chosen_ready, it + 1)
                    count_chosen(pe, rt, counts, totals).then_inc(counted, 1)


def routed_mixture_stage(nc, sbuf, psum, sem, name, keep, ln, routing, routed_rows, target, late):
    ident, w_hi, w_lo, w_in, rows, rows_in, y, scattered = keep
    rt = routing
    HIDDEN, UP = (F2, F2) if ln else (M1, 2 * M1)
    FC = HIDDEN // P
    W1 = DC * UP
    HALF = BUFS // 2
    FULL = ROUTED // BUFS
    with ExitStack() as st:
        x = [sbuf(st, f"{name}x{i}", [P, DC, P]) for i in range(2)]
        x_hi = [sbuf(st, f"{name}x_hi{i}", [P, DC, P], F32R) for i in range(2)]
        x_lo = [sbuf(st, f"{name}x_lo{i}", [P, DC, P], F32R) for i in range(2)]
        h = [sbuf(st, f"{name}h{i}", [P, HIDDEN]) for i in range(2)]
        h_hi = [sbuf(st, f"{name}h_hi{i}", [P, FC, P], F32R) for i in range(2)]
        h_lo = [sbuf(st, f"{name}h_lo{i}", [P, FC, P], F32R) for i in range(2)]
        x_ps = psum(st, name + "x_ps", [P, DC, P])
        u_ps = [psum(st, f"{name}u_ps{i}", [P, CW]) for i in range(2)]
        h_ps = [psum(st, f"{name}h_ps{i}", [P, CW]) for i in range(2)]
        o_ps = [psum(st, f"{name}o_ps{i}", [P, CW]) for i in range(2)]
        marks, padded, loaded, w_hi_ready, w_lo_ready = (sem(name + n) for n in ("marks", "padded", "loaded", "w_hi_ready", "w_lo_ready"))
        x_turned, x_ready, x_hi_ready, x_lo_ready, up_ready, slope_ready, leaky_ready, h_ready, h_turned, h_hi_ready, h_lo_ready = (
            sem(name + n) for n in ("x_turned", "x_ready", "x_hi_ready", "x_lo_ready", "up_ready", "slope_ready", "leaky_ready",
                                    "h_ready", "h_turned", "h_hi_ready", "h_lo_ready"))
        down_ready, scaled = sem(name + "down_ready"), sem(name + "scaled")
        added = [sem(f"{name}added{i}") for i in range(2)]
        if ln:
            ln_w = sbuf(st, name + "ln_w", [P, DC])
            ln_b = sbuf(st, name + "ln_b", [P, DC])
        else:
            slope = [sbuf(st, f"{name}slope{i}", [P, M1]) for i in range(2)]
            leaky = [sbuf(st, f"{name}leaky{i}", [P, M1]) for i in range(2)]

        def bodies(eng, body):
            body(0)
            with eng.Fori(1, FULL) as g:
                body(g)
            body(FULL)

        def exists(g, k):
            return not isinstance(g, int) or BUFS * g + k < ROUTED

        def load(table, engine, g, n, most):
            if isinstance(g, int):
                n = min(n, ROUTED - BUFS * g)
            return nc.values_load_multi_w_load_instructions(table[0:1, bass.ds(BUFS * g, n)], engines=[engine],
                                                            min_val=0, max_val=most)[1]

        with nc.Block() as block:
            @block.sync
            def _(sp):
                if ln:
                    sp.dma_start(ln_w[:], ln[0]).then_inc(loaded, 16)
                    sp.dma_start(ln_b[:], ln[1]).then_inc(loaded, 16)
                if late:
                    store_padding(sp, rt, routed_rows, padded)
                    sp.wait_ge(padded, 16 * E)
                    sp.wait_ge(scattered, 16 * NT * TOP)

                def body(g):
                    at = load(rt.row_of, mybir.EngineType.SP, g, BUFS, E * SLAB + P * (SPARES - 1))
                    for k in range(BUFS):
                        if not exists(g, k):
                            continue
                        wait(sp, added[k % 2], 16 * (HALF * (g - 1) + k // 2 + 1))
                        sp.dma_start(rows[k], routed_rows[bass.ds(at[k], P), :]).then_inc(rows_in[k], 16)
                if late:
                    load_first_rows(sp, nc, rt, routed_rows, rows, rows_in)
                with sp.Fori(1, FULL) as g:
                    body(g)
                body(FULL)

            @block.gpsimd
            def _(pool):
                if late:
                    scatter_rows(pool, rt, range(EARLY, PAIR), routed_rows, scattered)

                def body(g):
                    clear = load(rt.clear_at, mybir.EngineType.Pool, g, BUFS, 16 * ROUTED)
                    for k in range(BUFS):
                        if not exists(g, k):
                            continue
                        wait(pool, added[k % 2], 16 * (HALF * g + k // 2))
                        if isinstance(g, int) and BUFS * g + k < 3:
                            wait(pool, added[1 - k % 2], 16 * ((k + 1) // 2))
                        else:
                            apart(pool, marks)
                            pool.wait_ge(added[1 - k % 2], clear[k])
                            apart(pool, marks)
                        pool.wait_ge(scaled, BUFS * g + k + 3)
                        apart(pool, marks)
                        pool.indirect_dma_start(target, bass.IndirectOffsetOnAxis(ap=rows[k][:, D + E:ROW].bitcast(I32), axis=0),
                                                y[k], None, compute_op=ALU.add).then_inc(added[k % 2], 16)
                bodies(pool, body)
                for k in range(2):
                    pool.wait_ge(added[k], 16 * ((ROUTED + 1 - k) // 2))

            @block.scalar
            def _(act):
                def features(i, k):
                    act.wait_ge(x_turned, i + 1)
                    if ln:
                        for c in range(DC):
                            last = act.activation(x[k % 2][:, c, :], x_ps[:, c, :], ACT.Identity, scale=ln_w[:, c:c + 1], bias=ln_b[:, c:c + 1])
                    else:
                        last = act.activation(x[k % 2][:], x_ps[:], ACT.Copy)
                    last.then_inc(x_ready, 1)
                    act.wait_ge(x_ready, i + 1)
                    act.activation(x_hi[k % 2][:], x[k % 2][:], ACT.Copy).then_inc(x_hi_ready, 1)

                def hidden(i, k):
                    act.wait_ge(up_ready, i + 1)
                    if ln:
                        act.activation(h[k % 2][:], u_ps[k % 2][:], ACT.Gelu_apprx_tanh).then_inc(h_ready, 1)
                    else:
                        act.activation(slope[k % 2][:], u_ps[k % 2][:, 0:M1], ACT.Copy, scale=LEAKY).then_inc(slope_ready, 1)

                def high(i, k):
                    act.wait_ge(h_turned, i + 1)
                    act.activation(h_hi[k % 2][:], h_ps[k % 2][:, 0:HIDDEN].rearrange("p (f n) -> p f n", n=P), ACT.Copy).then_inc(h_hi_ready, 1)

                if w_in:
                    act.wait_ge(w_in, 16 * E)
                for e in range(E if w_in else 0):
                    act.activation(w_hi[:, e, :], w_lo[:, e, :].bitcast(F32), ACT.Copy).then_inc(w_hi_ready, 1)
                if ln:
                    act.wait_ge(loaded, 32)
                features(0, 0)
                features(1, 1)
                hidden(0, 0)
                features(2, 2)
                hidden(1, 1)
                high(0, 0)

                def body(g):
                    for k in range(BUFS):
                        i = BUFS * g + k
                        if exists(g, k + 3):
                            features(i + 3, k + 3)
                        if exists(g, k + 2):
                            hidden(i + 2, k + 2)
                        if exists(g, k + 1):
                            high(i + 1, k + 1)
                bodies(act, body)

            @block.vector
            def _(dve):
                def low(i, k):
                    dve.wait_ge(x_hi_ready, i + 1)
                    dve.tensor_tensor(x_lo[k % 2][:], x[k % 2][:], x_hi[k % 2][:].bitcast(F32), ALU.subtract).then_inc(x_lo_ready, 1)

                def hidden(i, k):
                    if ln:
                        return
                    dve.wait_ge(slope_ready, i + 1)
                    dve.tensor_tensor(leaky[k % 2][:], slope[k % 2][:], u_ps[k % 2][:, 0:M1], ALU.max).then_inc(leaky_ready, 1)
                    dve.wait_ge(leaky_ready, i + 1)
                    dve.tensor_tensor(h[k % 2][:], leaky[k % 2][:], u_ps[k % 2][:, M1:2 * M1], ALU.mult).then_inc(h_ready, 1)

                def hidden_low(i, k):
                    dve.wait_ge(h_hi_ready, i + 1)
                    dve.tensor_tensor(h_lo[k % 2][:], h_ps[k % 2][:, 0:HIDDEN].rearrange("p (f n) -> p f n", n=P),
                                      h_hi[k % 2][:].bitcast(F32), ALU.subtract).then_inc(h_lo_ready, 1)

                for e in range(E if w_in else 0):
                    dve.wait_ge(w_hi_ready, e + 1)
                    dve.tensor_tensor(w_lo[:, e, :], w_lo[:, e, :].bitcast(F32), w_hi[:, e, :].bitcast(F32), ALU.subtract).then_inc(w_lo_ready, 1)
                dve.sem_inc(scaled, 2)
                low(0, 0)
                low(1, 1)
                hidden(0, 0)
                low(2, 2)
                hidden(1, 1)
                hidden_low(0, 0)

                def body(g):
                    of = load(rt.expert_of, mybir.EngineType.DVE, g, BUFS, E - 1)
                    for k in range(BUFS):
                        if not exists(g, k):
                            continue
                        i = BUFS * g + k
                        if exists(g, k + 3):
                            low(i + 3, k + 3)
                        if exists(g, k + 2):
                            hidden(i + 2, k + 2)
                        if exists(g, k + 1):
                            hidden_low(i + 1, k + 1)
                        wait(dve, added[k % 2], 16 * (HALF * (g - 1) + k // 2 + 1))
                        dve.wait_ge(down_ready, i + 1)
                        dve.tensor_scalar(y[k], o_ps[k % 2][:, 0:D], rows[k][:, bass.ds(D + of[k], 1)], None, ALU.mult).then_inc(scaled, 1)
                bodies(dve, body)

            @block.tensor
            def _(pe):
                def turn_rows(i, g, k):
                    pe.wait_ge(rows_in[k % BUFS], 16 * (g + k // BUFS + 1))
                    wait(pe, x_ready, i)
                    for c in range(DC):
                        last = pe.transpose(x_ps[:, c, :], rows[k % BUFS][:, P * c:P * c + P], ident)
                    last.then_inc(x_turned, 1)

                def up(i, k, e):
                    pe.wait_ge(x_lo_ready, i + 1)
                    for c in range(DC):
                        cols = slice(UP * c, UP * c + UP)
                        high, low = (w[:, bass.ds(e, 1), cols] for w in (w_hi, w_lo))
                        pe.matmul(u_ps[k % 2][:, 0:UP], x_hi[k % 2][:, c, :], high, start=(c == 0), stop=False)
                        pe.matmul(u_ps[k % 2][:, 0:UP], x_hi[k % 2][:, c, :], low, start=False, stop=False)
                        last = pe.matmul(u_ps[k % 2][:, 0:UP], x_lo[k % 2][:, c, :], high, start=False, stop=(c == DC - 1))
                    last.then_inc(up_ready, 1)

                def turn_hidden(i, k):
                    pe.wait_ge(h_ready, i + 1)
                    for f in range(FC):
                        last = pe.transpose(h_ps[k % 2][:, P * f:P * f + P], h[k % 2][:, P * f:P * f + P], ident)
                    last.then_inc(h_turned, 1)

                def down(i, k, e):
                    pe.wait_ge(scaled, i + 1)
                    pe.wait_ge(h_lo_ready, i + 1)
                    for f in range(FC):
                        cols = slice(W1 + D * f, W1 + D * f + D)
                        high, low = (w[:, bass.ds(e, 1), cols] for w in (w_hi, w_lo))
                        pe.matmul(o_ps[k % 2][:, 0:D], h_hi[k % 2][:, f, :], high, start=(f == 0), stop=False)
                        pe.matmul(o_ps[k % 2][:, 0:D], h_hi[k % 2][:, f, :], low, start=False, stop=False)
                        last = pe.matmul(o_ps[k % 2][:, 0:D], h_lo[k % 2][:, f, :], high, start=False, stop=(f == FC - 1))
                    last.then_inc(down_ready, 1)

                of = load(rt.expert_of, mybir.EngineType.PE, 0, 2, E - 1)
                turn_rows(0, 0, 0)
                turn_rows(1, 0, 1)
                if w_in:
                    pe.wait_ge(w_lo_ready, E)
                up(0, 0, of[0])
                turn_rows(2, 0, 2)
                up(1, 1, of[1])
                turn_hidden(0, 0)

                def body(g):
                    of = load(rt.expert_of, mybir.EngineType.PE, g, BUFS + 2, E - 1)
                    for k in range(BUFS):
                        if not exists(g, k):
                            continue
                        i = BUFS * g + k
                        if exists(g, k + 3):
                            turn_rows(i + 3, g, k + 3)
                        if exists(g, k + 2):
                            up(i + 2, k + 2, of[k + 2])
                        if exists(g, k + 1):
                            turn_hidden(i + 1, k + 1)
                        down(i, k, of[k])
                bodies(pe, body)


TILES = [t for j in range(QT // 2) for _ in range(B) for t in (QT - 1 - j, j)]
LATE_TILES = range(QT // 4, 3 * QT // 4)


class Unit:

    def __init__(self, u):
        self.u = u
        self.tile = TILES[u]
        self.batch = u // 2 % B
        self.round = u // 4
        self.short = u % 2
        self.half = 0 if self.tile in LATE_TILES else 1
        place = self.tile - QT // 4 if self.half == 0 else self.tile if self.tile < QT // 4 else self.tile - QT // 2
        self.query = S * self.batch + CW * self.half + P * place
        self.blocks = self.tile + 1
        self.chunks = [(c * 4, min(4, self.blocks - c * 4)) for c in range((self.blocks + 3) // 4)]
        two = 2 if self.blocks != 2 else 1
        self.slots = [(k, min(two, self.blocks - k)) for k in range(0, self.blocks, two)]


class Slot:

    def __init__(self, u, first, n, start):
        self.u, self.first, self.n, self.start = u, first, n, start


UNITS = QT * B
BODY = [Unit(u) for u in range(UNITS)]
FIRST_CHUNK = [sum(2 * len(x.chunks) for x in BODY[:u]) for u in range(UNITS + 1)]
SCORES = FIRST_CHUNK[UNITS]
FIRST_SLOT = [sum(len(x.slots) for x in BODY[:u]) for u in range(UNITS + 1)]
FIRST_BLOCK = [sum(x.blocks for x in BODY[:u]) for u in range(UNITS + 1)]
SLOTS = [Slot(x.u, k, n, FIRST_BLOCK[x.u] + k) for x in BODY for k, n in x.slots]
NS = len(SLOTS)
ROW_BLOCKS = (QT, QT, QT // 2, QT // 2)
ROW_BUFFER = (0, 2, 1, 3) * (UNITS // 4)
LEAD = 14
CHUNKS_AT = [[] for _ in range(NS)]
EXPS_AT = [[] for _ in range(NS)]
for _x in BODY:
    _rows = len(_x.chunks)
    for _i in range(2 * _rows):
        _block = FIRST_BLOCK[_x.u] + _x.blocks * _i / (2 * _rows) - LEAD
        _unit = _x.u if _block >= 0 else _x.u + UNITS
        _slot = max(t for t in range(NS) if SLOTS[t].start <= _block % FIRST_BLOCK[UNITS])
        CHUNKS_AT[_slot].append((_unit, _i))
        if _i % _rows == _rows - 1:
            EXPS_AT[(_slot + 1) % NS].append((_unit - UNITS * ((_slot + 1) // NS), _i // _rows))

QUERIES_AT = {4: (0, 2), 14: (1, 1), 20: (2, 3), 40: (3, 0)}
PROJECT_AT = {}
_t = -3
for _u in range(-2, UNITS - 2):
    _t = max(_t + 2, FIRST_SLOT[_u % UNITS + 1] + 1 - (NS if _u < 0 else 0))
    _t += _t % 2
    while _t in QUERIES_AT:
        _t += 2
    PROJECT_AT[_t] = _u
assert max(PROJECT_AT) < NS and min(PROJECT_AT) >= 0


def apart(eng, marks):
    eng.sem_inc(marks, 1)


def wait(eng, sem, value):
    if isinstance(value, int) and value <= 0:
        return
    eng.wait_ge(sem, value)


def program(nc, x, bias, cond, mask, g_in, nab, Wq, Wkv, Wo, out, routed_rows, mixed, **aps):
    outer = ExitStack()
    with outer:
        def sbuf(stack, name, shape, dt=F32):
            return stack.enter_context(nc.sbuf_tensor(name, shape, dt))

        def psum(stack, name, shape, dt=F32):
            return stack.enter_context(nc.psum_tensor(name, shape, dt))

        early = outer.enter_context(ExitStack())
        stage_sems = [early]
        used = []

        def sem(name):
            handle = stage_sems[-1].enter_context(nc.semaphore(name))
            used.append(handle.num)
            return handle

        xs = sbuf(outer, "xs", [P, NT, D])
        ident = sbuf(outer, "ident", [P, P])
        yacc = sbuf(outer, "yacc", [P, NT, D])

        null_wo = sbuf(outer, "null_wo", [H, D])
        null_w = sbuf(outer, "null_w", [P, UNITS, H])

        attn = ExitStack()
        xnT = sbuf(attn, "xnT", [P, DC, T])
        k_hi = sbuf(attn, "k_hi", [P, T], F32R)
        k_lo = sbuf(attn, "k_lo", [P, T], F32R)
        values = sbuf(attn, "values", [P, NT, P], F32R)
        wo = sbuf(attn, "wo", [P, H, D])
        neg_null = sbuf(attn, "neg_null", [P, UNITS, H])

        with ExitStack() as st:
            xh = sbuf(st, "xh", [P, 4, 4, D])
            mv = sbuf(st, "mv", [P, NT, 2])
            stats = sbuf(st, "stats", [P, NT, 6])
            rstd = sbuf(st, "rstd", [P, NT])
            power = sbuf(st, "power", [P, 4])
            gcol = sbuf(st, "gcol", [P, DC])
            wk = sbuf(st, "wk", [P, DC, P])
            wv = sbuf(st, "wv", [P, DC, DH])
            wq_all = sbuf(st, "wq_all", [P, DC, H, DH])
            nk_b = sbuf(st, "nk_b", [P, DH])
            nab_b = sbuf(st, "nab_b", [P, H])
            nv = sbuf(st, "nv", [DH, 1])
            nv_at = sbuf(st, "nv_at", [DH, H, H])
            nk_prod = sbuf(st, "nk_prod", [P, DC, H, DH])
            w_null = sbuf(st, "w_null", [P, DC, H])
            mask8 = sbuf(st, "mask8", [P, T], U8)
            turn = [psum(st, f"turn{i}", [P, CW]) for i in range(2)]
            kps = [psum(st, f"kps{i}", [P, CW]) for i in range(2)]
            vps = [psum(st, f"vps{i}", [P, QT, DH]) for i in range(B)]
            nps = psum(st, "nps", [P, CW])
            null_ps = nps[:, 0:UNITS * H].rearrange("p (u h) -> p u h", h=H)
            nwps = psum(st, "nwps", [P, CW])
            x_in = [sem(f"x_in{g}") for g in range(4)]
            w_in, small_in = sem("w_in"), sem("small_in")
            const_ready, var_ready, rstd_ready = sem("const_ready"), sem("var_ready"), sem("rstd_ready")
            xh_ready, turned, xnT_ready = sem("xh_ready"), sem("turned"), sem("xnT_ready")
            k_ready, khi_ready, klo_ready, v_ready, v_out = (sem(n) for n in ("k_ready", "khi_ready", "klo_ready", "v_ready", "v_out"))
            wq_all_in, wo_in, nv_ready, w_null_ready, null_ready, null_wo_ready = (
                sem(n) for n in ("wq_all_in", "wo_in", "nv_ready", "w_null_ready", "null_ready", "null_wo_ready"))
            step0 = sem("step0")
            zeroed = sem("zeroed")
            with nc.Block() as block:
                @block.sync
                def _(sp):
                    xt = x.rearrange("(t p) d -> p t d", p=P)
                    for g in range(4):
                        sp.dma_start(xs[:, 4 * g:4 * g + 4, :], xt[:, 4 * g:4 * g + 4, :]).then_inc(x_in[g], 16)
                    wkv = Wkv.rearrange("(c p) n -> p c n", p=P)
                    sp.dma_start(wk[:, :, 0:DH], wkv[:, :, 0:DH]).then_inc(w_in, 16)
                    sp.dma_start(wk[:, :, DH:P], wkv[:, :, 0:DH]).then_inc(w_in, 16)
                    sp.dma_start(wv[:], wkv[:, :, DH:2 * DH]).then_inc(w_in, 16)
                    sp.dma_start(wq_all[:].rearrange("p c h d -> p c (h d)"), Wq.rearrange("(c p) n -> p c n", p=P)).then_inc(wq_all_in, 16)
                    wo_h = Wo.rearrange("(h d) n -> d h n", d=DH)
                    for half in range(2):
                        sp.dma_start(wo[DH * half:DH * half + DH, :, :], wo_h).then_inc(wo_in, 16)

                @block.scalar
                def _(act):
                    act.dma_start(gcol[:], g_in).then_inc(small_in, 16)
                    act.dma_start(nk_b[:], cond[0:1, :].broadcast_to([P, DH])).then_inc(small_in, 16)
                    act.dma_start(nv[:], cond[1:2, :].rearrange("o d -> d o")).then_inc(small_in, 16)
                    act.dma_start(nab_b[:], nab.rearrange("(o h) -> o h", o=1).broadcast_to([P, H])).then_inc(small_in, 16)
                    act.dma_start(mask8[DH:DH + 1, :], mask).then_inc(small_in, 16)
                    act.wait_ge(small_in, 16 * 5)
                    for g in range(4):
                        for c in range(DC):
                            act.wait_ge(turned, DC * g + c + 1)
                            act.activation(xnT[:, c, CW * g:CW * g + CW], turn[c][:], ACT.Copy,
                                           scale=gcol[:, c:c + 1]).then_inc(xnT_ready, 1)
                        act.wait_ge(k_ready, g + 1)
                        act.activation(k_hi[:, CW * g:CW * g + CW], kps[g % 2][:], ACT.Copy).then_inc(khi_ready, 1)
                    for b in range(B):
                        act.wait_ge(v_ready, b + 1)
                        act.activation(values[:, QT * b:QT * b + QT, 0:DH], vps[b][:], ACT.Copy).then_inc(v_out, 1)
                    act.wait_ge(null_wo_ready, 1)
                    act.activation(null_wo[:], nwps[0:H, 0:D], ACT.Copy)

                @block.gpsimd
                def _(pool):
                    pool.memset(ident[:], 0.0).then_inc(zeroed, 1)
                    pool.memset(power[:], -0.5).then_inc(const_ready, 1)
                    pool.wait_ge(zeroed, 1)
                    pool.affine_select(out=ident[:], in_=ident[:], compare_op=ALU.not_equal, fill=1.0, base=0,
                                       pattern=[[-1, P]], channel_multiplier=1).then_inc(const_ready, 1)
                    pool.wait_ge(const_ready, 1)
                    for g in range(4):
                        pool.wait_ge(var_ready, g + 1)
                        pool.tensor_tensor(rstd[:, 4 * g:4 * g + 4], rstd[:, 4 * g:4 * g + 4], power[:],
                                           ALU.pow).then_inc(rstd_ready, 1)

                @block.vector
                def _(dve):
                    dve.memset(k_lo[DH:P, :].bitcast(F32), 0.0).then_inc(step0, 1)
                    for g in range(4):
                        dve.wait_ge(x_in[g], 16)
                        for t in range(4 * g, 4 * g + 4):
                            last = dve.bn_stats(stats[:, t, :], xs[:, t, :])
                        last.then_inc(step0, 1)
                        dve.wait_ge(step0, 2 + 2 * g)
                        for t in range(4 * g, 4 * g + 4):
                            last = dve.bn_aggr(mv[:, t, :], stats[:, t, :])
                        last.then_inc(step0, 1)
                        dve.wait_ge(step0, 3 + 2 * g)
                        dve.tensor_scalar(rstd[:, 4 * g:4 * g + 4], mv[:, 4 * g:4 * g + 4, 1], EPS, None,
                                          ALU.add).then_inc(var_ready, 1)
                    for g in range(4):
                        dve.wait_ge(rstd_ready, g + 1)
                        for t in range(4):
                            tt = 4 * g + t
                            last = dve.tensor_scalar(xh[:, g, t, :], xs[:, tt, :], mv[:, tt, 0:1], rstd[:, tt:tt + 1],
                                                     ALU.subtract, ALU.mult)
                        last.then_inc(xh_ready, 1)
                    dve.memset(yacc[:], 0.0).then_inc(step0, 1)
                    dve.wait_ge(small_in, 16 * 5)
                    dve.tensor_scalar(k_lo[DH:DH + 1, 0:T], mask8[DH:DH + 1, :], MASKED, -MASKED, ALU.mult, ALU.add)
                    dve.memset(nv_at[:], 0.0).then_inc(step0, 1)
                    dve.wait_ge(step0, 11)
                    dve.tensor_copy(nv_at[:].rearrange("d a b -> d (a b)")[:, 0:H * H:H + 1],
                                    nv[:].broadcast_to([DH, H])).then_inc(nv_ready, 1)
                    dve.wait_ge(wq_all_in, 16)
                    for c in range(DC):
                        last = dve.tensor_tensor(nk_prod[:, c], wq_all[:, c], nk_b[:].unsqueeze(1).broadcast_to([P, H, DH]), ALU.mult)
                    last.then_inc(step0, 1)
                    dve.wait_ge(step0, 12)
                    dve.tensor_reduce(w_null[:], nk_prod[:], AX.X, ALU.add).then_inc(w_null_ready, 1)
                    for g in range(4):
                        dve.wait_ge(khi_ready, g + 1)
                        cols = slice(CW * g, CW * g + CW)
                        dve.tensor_tensor(k_lo[0:DH, cols], kps[g % 2][0:DH, :], k_hi[0:DH, cols].bitcast(F32),
                                          ALU.subtract).then_inc(klo_ready, 1)
                    for b in range(B):
                        dve.wait_ge(v_out, b + 1)
                        rows = slice(QT * b, QT * b + QT)
                        dve.tensor_tensor(values[:, rows, DH:P], vps[b][:], values[:, rows, 0:DH].bitcast(F32), ALU.subtract)
                    dve.wait_ge(null_ready, 1)
                    dve.scalar_tensor_tensor(neg_null[:], null_ps, -DH ** -0.5, nab_b[:].unsqueeze(1).broadcast_to([P, UNITS, H]),
                                             ALU.mult, ALU.subtract)

                @block.tensor
                def _(pe):
                    def null_scores(g):
                        for x in BODY:
                            t = QT * x.batch + x.tile
                            if t // 4 != g:
                                continue
                            for c in range(DC):
                                last = pe.matmul(null_ps[:, x.u, :], xnT[:, c, P * t:P * t + P], w_null[:, c, :],
                                                 start=(c == 0), stop=(c == DC - 1))
                        return last

                    pe.wait_ge(const_ready, 2)
                    pe.wait_ge(w_in, 48)
                    for g in range(4):
                        pe.wait_ge(xh_ready, g + 1)
                        for c in range(DC):
                            if g:
                                pe.wait_ge(xnT_ready, DC * (g - 1) + c + 1)
                            for t in range(4):
                                last = pe.transpose(turn[c][:, P * t:P * t + P], xh[:, g, t, P * c:P * c + P], ident[:])
                            last.then_inc(turned, 1)
                        if g == 1:
                            pe.wait_ge(nv_ready, 1)
                            pe.wait_ge(wo_in, 32)
                        if g == 2:
                            pe.wait_ge(w_null_ready, 1)
                        for h in range(H * (g - 1) // 3, H * g // 3) if g else ():
                            last = pe.matmul(nwps[0:H, 0:D], nv_at[:, h, :], wo[0:DH, h, :], start=(h == 0), stop=(h == H - 1))
                        if g == 3:
                            last.then_inc(null_wo_ready, 1)
                        if g >= 2:
                            null_scores(g - 2)
                        pe.wait_ge(xnT_ready, DC * (g + 1))
                        if g >= 2:
                            pe.wait_ge(klo_ready, g - 1)
                        for c in range(DC):
                            last = pe.matmul(kps[g % 2][:], wk[:, c, :], xnT[:, c, CW * g:CW * g + CW],
                                             start=(c == 0), stop=(c == DC - 1))
                        last.then_inc(k_ready, 1)
                        for t in range(4 * g, 4 * g + 4):
                            for c in range(DC):
                                last = pe.matmul(vps[t // QT][:, t % QT, :], xnT[:, c, P * t:P * t + P], wv[:, c, :],
                                                 start=(c == 0), stop=(c == DC - 1))
                        if g % 2:
                            last.then_inc(v_ready, 1)
                    null_scores(2)
                    null_scores(3).then_inc(null_ready, 1)

        with ExitStack() as st:
            wq = sbuf(st, "wq", [P, DC, P])
            q_hi = sbuf(st, "q_hi", [P, B, CW], F32R)
            q_lo = sbuf(st, "q_lo", [P, B, CW], F32R)
            q_hilo = [sbuf(st, f"q_hilo{h}", [P, T], F32R) for h in range(2)]
            q_one = [sbuf(st, f"q_one{h}", [P, T], F32R) for h in range(2)]
            bias_row = [[[sbuf(st, f"bias_row{i}_{s}_{h}", [P, P * ((QT - i), (QT // 2 - 1 + i))[s]]) for h in range(2)]
                         for s in range(2)] for i in range(2)]
            probs = [[sbuf(st, f"probs{i}_{h}", [P, P * n]) for h in range(2)] for i, n in enumerate(ROW_BLOCKS)]
            pT_hi = [sbuf(st, f"pT_hi{i}", [P, 2, 2 * P], F32R) for i in range(3)]
            pT_lo = [sbuf(st, f"pT_lo{i}", [P, 2, 2 * P], F32R) for i in range(3)]
            oT = [sbuf(st, f"oT{i}", [P, 2 * P]) for i in range(2)]
            neg_pair = sbuf(st, "neg_pair", [P, UNITS, 2])
            neg_max = sbuf(st, "neg_max", [P, UNITS, 2])
            part_max = sbuf(st, "part_max", [P, UNITS, 2])
            null_arg = sbuf(st, "null_arg", [P, UNITS, 2])
            null_exp = sbuf(st, "null_exp", [P, UNITS, 2])
            row_sum = sbuf(st, "row_sum", [P, UNITS, 2])
            full_sum = sbuf(st, "full_sum", [P, UNITS, 2])
            inv_sum = sbuf(st, "inv_sum", [P, UNITS, 2])
            y_head = [sbuf(st, f"y_head{i}", [P, 2, D]) for i in range(2)]
            s_ps = [psum(st, f"s_ps{i}", [P, CW]) for i in range(2)]
            t_ps = [psum(st, f"t_ps{i}", [P, CW]) for i in range(3)]
            o_ps = [psum(st, f"o_ps{i}", [P, CW])[:, 0:2 * P] for i in range(2)]
            m_ps = psum(st, "m_ps", [P, CW])

            wq_in = sem("wq_in")
            bias_in = [sem(f"bias_in{i}") for i in range(2)]
            bias_ready = sem("bias_ready")
            scores_ready, scores_read, probs_ready = sem("scores_ready"), sem("scores_read"), sem("probs_ready")
            turn_ready, hi_out, lo_out, pv_done = sem("turn_ready"), sem("hi_out"), sem("lo_out"), sem("pv_done")
            oT_ready, projected, scaled, added = sem("oT_ready"), sem("projected"), sem("scaled"), sem("added")
            q_ready, q_hi_ready, q_lo_ready, q_in = sem("q_ready"), sem("q_hi_ready"), sem("q_lo_ready"), sem("q_in")
            neg_ready, null_arg_ready, null_exp_ready = sem("neg_ready"), sem("null_arg_ready"), sem("null_exp_ready")
            sum_ready, inv_ready, null_w_ready = sem("sum_ready"), sem("inv_ready"), sem("null_w_ready")
            ones_ready = sem("ones_ready")
            marks_dve, marks_pool, marks_sp = sem("marks_dve"), sem("marks_pool"), sem("marks_sp")
            LAST = PAIRS - 1
            MOVES = 16 * 6

            def pairs(eng, body):
                body(0)
                with eng.Fori(1, LAST) as p:
                    body(p)
                body(LAST)

            def is_first(p):
                return isinstance(p, int) and p == 0

            def is_last(p):
                return isinstance(p, int) and p == LAST

            def unit_at(p, u):
                if u >= UNITS:
                    return None if is_last(p) else (p + 1, BODY[u - UNITS])
                if u < 0:
                    return None if is_first(p) else (p - 1, BODY[u + UNITS])
                return p, BODY[u]

            def slot_at(p, t):
                if t >= NS:
                    return None if is_last(p) else (p + 1, t - NS)
                return p, t

            def query_step(p, t):
                if t not in QUERIES_AT or (QUERIES_AT[t][0] and is_last(p)):
                    return None
                k, j = QUERIES_AT[t]
                return 4 * p + 3 + k, j, 2 * p + (1, 2, 2, 3)[k]

            AHEAD = ((0, 1, 0), (1, 3, 0), (2, 0, 1))

            with nc.Block() as block:
                @block.sync
                def _(sp):
                    wq_h = Wq.rearrange("(c p) (r n) -> r p c n", p=P, n=P)
                    sp.dma_start(wq[:], wq_h[0]).then_inc(wq_in, 16)

                    def move(half, chunks, scores):
                        wait(sp, scores_ready, scores)
                        apart(sp, marks_sp)
                        sp.wait_ge(q_lo_ready, chunks)
                        apart(sp, marks_sp)
                        for h in range(2):
                            mine = slice(DH * h, DH * h + DH)
                            for to, part in ((q_hilo[h][0:DH], q_hi), (q_hilo[h][DH:P], q_lo), (q_one[h][0:DH], q_hi)):
                                to = to.rearrange("p (b n) -> p b n", b=B)[:, :, CW * half:CW * half + CW]
                                sp.dma_start(to.bitcast(F32), part[mine].bitcast(F32)).then_inc(q_in, 16)

                    def bias_round(p, j):
                        if j >= QT // 2:
                            if is_last(p):
                                return
                            p, j = p + 1, j - QT // 2
                        wait(sp, scores_read, SCORES * p + (FIRST_CHUNK[4 * (j - 1)] if j >= 2 else FIRST_CHUNK[4 * (j + 3)] - SCORES))
                        apart(sp, marks_sp)
                        for s, tile in enumerate((QT - 1 - j, j)):
                            width = P * (tile + 1)
                            for h in range(2):
                                rows = bias[2 * p + h]
                                sp.dma_start(bias_row[j % 2][s][h][:, 0:width],
                                             rows[P * tile:P * tile + P, 0:width]).then_inc(bias_in[j % 2], 16)

                    def body(p):
                        bias_round(p, 2)
                        move(0, 4 * p + 4, SCORES * p)
                        if not is_last(p):
                            sp.dma_start(wq[:], wq_h[p + 1]).then_inc(wq_in, 16)
                        bias_round(p, 3)
                        if not is_last(p):
                            move(1, 4 * p + 6, SCORES * p + FIRST_CHUNK[8])
                        bias_round(p, 4)
                        bias_round(p, 5)
                    for j in range(2):
                        bias_round(0, j)
                    move(1, 2, 0)
                    pairs(sp, body)

                @block.gpsimd
                def _(pool):
                    for h in range(2):
                        pool.memset(q_one[h][DH:P, :].bitcast(F32), 0.0).then_inc(ones_ready, 1)
                    pool.wait_ge(ones_ready, 2)
                    for h in range(2):
                        pool.memset(q_one[h][DH:DH + 1, :].bitcast(F32), 1.0).then_inc(ones_ready, 1)

                    def diagonal(p, j):
                        if j >= QT // 2:
                            if is_last(p):
                                return
                            p, j = p + 1, j - QT // 2
                        pool.wait_ge(bias_in[j % 2], 64 * (2 * p + j // 2 + 1))
                        for s, tile in enumerate((QT - 1 - j, j)):
                            for h in range(2):
                                d = bias_row[j % 2][s][h][:, P * tile:P * tile + P]
                                apart(pool, marks_pool)
                                pool.affine_select(out=d, in_=d, compare_op=ALU.is_ge, fill=-MASKED, base=0,
                                                   pattern=[[-1, P]], channel_multiplier=1).then_inc(bias_ready, 1)

                    def add(p, u):
                        at = unit_at(p, u)
                        if at is None:
                            return
                        p, x = at
                        y = yacc[:, QT * x.batch + x.tile, :]
                        pool.wait_ge(scaled, 2 * (UNITS * p + x.u + 1))
                        for h in range(2):
                            if h:
                                pool.wait_ge(added, 2 * (UNITS * p + x.u) + 1)
                            pool.tensor_tensor(y, y, y_head[x.u % 2][:, h, :], ALU.add).then_inc(added, 1)

                    def body(p):
                        for u in range(UNITS):
                            add(p, u - 2)
                            if u % 4 == 3:
                                diagonal(p, u // 4 + 2)
                    pool.wait_ge(ones_ready, 4)
                    for j in range(2):
                        diagonal(0, j)
                    pairs(pool, body)
                    for u in range(UNITS - 2, UNITS):
                        add(LAST, u)

                @block.scalar
                def _(act):
                    def high(p, t):
                        at = slot_at(p, t)
                        if at is None:
                            return
                        p, t = at
                        n = SLOTS[t].n
                        wait(act, pv_done, NS * p + t - 2)
                        act.wait_ge(turn_ready, NS * p + t + 1)
                        act.activation(pT_hi[t % 3][:, 0:n, :], t_ps[t % 3][:, 0:2 * P * n], ACT.Copy).then_inc(hi_out, 1)

                    def exps(p, u, h):
                        at = unit_at(p, u)
                        if at is None:
                            return
                        p, x = at
                        row = probs[ROW_BUFFER[x.u]][h][:, 0:P * x.blocks]
                        act.wait_ge(scores_read, SCORES * p + FIRST_CHUNK[x.u] + (h + 1) * len(x.chunks))
                        act.activation(row, row, ACT.Exp, scale=-1.0, bias=neg_max[:, x.u, h:h + 1],
                                       accum_out=row_sum[:, x.u, h:h + 1]).then_inc(probs_ready, 1)

                    def query(number, j, half):
                        wait(act, q_in, MOVES * half)
                        act.wait_ge(q_ready, number + 1)
                        act.activation(q_hi[:, j // 2, :], m_ps[:], ACT.Copy, scale=DH ** -0.5).then_inc(q_hi_ready, 1)

                    def scale(p, u):
                        at = unit_at(p, u)
                        if at is None:
                            return
                        p, x = at
                        wait(act, added, 2 * (UNITS * p + x.u - 1))
                        act.wait_ge(inv_ready, QT * p + x.u // 2 + 1)
                        act.wait_ge(projected, UNITS * p + x.u + 1)
                        for h in range(2):
                            act.activation(y_head[x.u % 2][:, h, :], m_ps[:, D * h:D * h + D], ACT.Copy,
                                           scale=inv_sum[:, x.u, h:h + 1]).then_inc(scaled, 1)

                    def body(p):
                        for t, slot in enumerate(SLOTS):
                            u = slot.u
                            high(p, t + 1)
                            if t - 1 in PROJECT_AT:
                                scale(p, PROJECT_AT[t - 1])
                            q = query_step(p, t - 1)
                            if q:
                                query(*q)
                            for v, h in EXPS_AT[t]:
                                exps(p, v, h)
                            if u % 2 and t == FIRST_SLOT[u]:
                                act.wait_ge(null_arg_ready, QT * p + u // 2 + 1)
                                act.activation(null_exp[:, u - 1:u + 1, :], null_arg[:, u - 1:u + 1, :], ACT.Exp).then_inc(null_exp_ready, 1)

                    for q in AHEAD[:2]:
                        query(*q)
                    for at in EXPS_AT:
                        for v, h in at:
                            if v >= UNITS:
                                exps(0, v - UNITS, h)
                    query(*AHEAD[2])
                    high(0, 0)
                    pairs(act, body)
                    for u in range(UNITS - 2, UNITS):
                        scale(LAST, u)

                @block.vector
                def _(dve):
                    def scores(p, u, i):
                        at = unit_at(p, u)
                        if at is None:
                            return
                        p, x = at
                        h, n = i // len(x.chunks), i % len(x.chunks)
                        first, k = x.chunks[n]
                        c = FIRST_CHUNK[x.u] + i
                        cols = slice(P * first, P * (first + k))
                        if i == 0:
                            dve.wait_ge(bias_ready, 4 * (QT // 2 * p + x.round + 1))
                            before = max(v for v in range(x.u - UNITS, x.u) if ROW_BUFFER[v] == ROW_BUFFER[x.u])
                            wait(dve, turn_ready, NS * p + (FIRST_SLOT[before + 1] if before >= 0 else FIRST_SLOT[before + UNITS + 1] - NS))
                        start = part_max[:, x.u, h:h + 1] if n else neg_pair[:, x.u, h:h + 1]
                        to = neg_max if n == len(x.chunks) - 1 else part_max
                        if n:
                            dve.wait_ge(scores_read, SCORES * p + c)
                        dve.wait_ge(scores_ready, SCORES * p + c + 1)
                        apart(dve, marks_dve)
                        dve.tensor_tensor_reduce(probs[ROW_BUFFER[x.u]][h][:, cols], s_ps[c % 2][:, 0:P * k],
                                                 bias_row[x.round % 2][x.short][h][:, cols], -1.0, start, ALU.add, ALU.min,
                                                 to[:, x.u, h:h + 1]).then_inc(scores_read, 1)

                    def low(p, t):
                        at = slot_at(p, t)
                        if at is None:
                            return
                        p, t = at
                        n = SLOTS[t].n
                        dve.wait_ge(hi_out, NS * p + t + 1)
                        dve.tensor_tensor(pT_lo[t % 3][:, 0:n, :], t_ps[t % 3][:, 0:2 * P * n].rearrange("p (n q) -> p n q", n=n),
                                          pT_hi[t % 3][:, 0:n, :].bitcast(F32), ALU.subtract).then_inc(lo_out, 1)

                    def outputs(p, u):
                        at = unit_at(p, u)
                        if at is None:
                            return
                        p, x = at
                        wait(dve, projected, UNITS * p + x.u - 1)
                        dve.wait_ge(pv_done, NS * p + FIRST_SLOT[x.u + 1])
                        dve.tensor_copy(oT[x.u % 2][:], o_ps[x.u % 2]).then_inc(oT_ready, 1)

                    def query(number, j, half):
                        dve.wait_ge(q_hi_ready, number + 1)
                        dve.scalar_tensor_tensor(q_lo[:, j // 2, :], m_ps[:], DH ** -0.5, q_hi[:, j // 2, :].bitcast(F32),
                                                 ALU.mult, ALU.subtract).then_inc(q_lo_ready, 1)

                    def null_scores(p, half, count):
                        rows = slice(8 * half, 8 * half + 8)
                        apart(dve, marks_dve)
                        dve.tensor_copy(neg_pair[:, rows, :], neg_null[:, rows, bass.ds(2 * p, 2)]).then_inc(neg_ready, 1)
                        dve.wait_ge(neg_ready, count)

                    def body(p):
                        for t, slot in enumerate(SLOTS):
                            u = slot.u
                            if t == FIRST_SLOT[u]:
                                outputs(p, u - 1)
                            if t == FIRST_SLOT[2]:
                                null_scores(p, 1, 2 * p + 2)
                            if t == FIRST_SLOT[8] and not is_last(p):
                                null_scores(p + 1, 0, 2 * p + 3)
                            for v, i in CHUNKS_AT[t]:
                                scores(p, v, i)
                            q = query_step(p, t - 1)
                            if q:
                                query(*q)
                            low(p, t + 1)
                            rows = slice(u // 2 * 2, u // 2 * 2 + 2)
                            n = QT * p + u // 2 + 1
                            if u % 2 == 0 and t == FIRST_SLOT[u + 1] - 1:
                                dve.wait_ge(scores_read, SCORES * p + FIRST_CHUNK[u + 2])
                                dve.tensor_tensor(null_arg[:, rows, :], neg_max[:, rows, :], neg_pair[:, rows, :],
                                                  ALU.subtract).then_inc(null_arg_ready, 1)
                            if u % 2 and t == FIRST_SLOT[u]:
                                dve.wait_ge(null_exp_ready, n)
                                dve.wait_ge(probs_ready, 2 * UNITS * p + 2 * u + 2)
                                dve.tensor_tensor(full_sum[:, rows, :], row_sum[:, rows, :], null_exp[:, rows, :], ALU.add).then_inc(sum_ready, 1)
                                dve.wait_ge(sum_ready, n)
                                dve.reciprocal(inv_sum[:, rows, :], full_sum[:, rows, :]).then_inc(inv_ready, 1)
                                dve.wait_ge(inv_ready, n)
                                dve.tensor_tensor(null_w[:, rows, bass.ds(2 * p, 2)], null_exp[:, rows, :], inv_sum[:, rows, :],
                                                  ALU.mult).then_inc(null_w_ready, 1)

                    dve.wait_ge(ones_ready, 4)
                    null_scores(0, 0, 1)
                    for q in AHEAD[:2]:
                        query(*q)
                    for at in CHUNKS_AT:
                        for v, i in at:
                            if v >= UNITS:
                                scores(0, v - UNITS, i)
                    query(*AHEAD[2])
                    low(0, 0)
                    pairs(dve, body)
                    outputs(LAST, UNITS - 1)

                @block.tensor
                def _(pe):
                    def scores(p, u, i):
                        at = unit_at(p, u)
                        if at is None:
                            return
                        p, x = at
                        h, n = i // len(x.chunks), i % len(x.chunks)
                        first, k = x.chunks[n]
                        c = FIRST_CHUNK[x.u] + i
                        cols = slice(S * x.batch + P * first, S * x.batch + P * (first + k))
                        rows = slice(x.query, x.query + P)
                        if i == 0:
                            pe.wait_ge(q_in, MOVES * (2 * p + 1 + x.u // 8))
                        wait(pe, scores_read, SCORES * p + c - 1)
                        pe.matmul(s_ps[c % 2][:, 0:P * k], q_hilo[h][:, rows], k_hi[:, cols], start=True, stop=False)
                        pe.matmul(s_ps[c % 2][:, 0:P * k], q_one[h][:, rows], k_lo[:, cols],
                                  start=False, stop=True).then_inc(scores_ready, 1)

                    def turn(p, t):
                        at = slot_at(p, t)
                        if at is None:
                            return
                        p, t = at
                        slot = SLOTS[t]
                        x = BODY[slot.u]
                        if t == FIRST_SLOT[slot.u]:
                            pe.wait_ge(probs_ready, 2 * (UNITS * p + slot.u + 1))
                        wait(pe, lo_out, NS * p + t - 2)
                        for n in range(slot.n):
                            for h in range(2):
                                last = pe.transpose(t_ps[t % 3][:, P * (2 * n + h):P * (2 * n + h) + P],
                                                    probs[ROW_BUFFER[x.u]][h][:, P * (slot.first + n):P * (slot.first + n) + P], ident[:])
                        last.then_inc(turn_ready, 1)

                    def weigh(p, t):
                        slot = SLOTS[t]
                        x = BODY[slot.u]
                        if slot.first == 0:
                            wait(pe, oT_ready, UNITS * p + x.u - 1)
                        pe.wait_ge(lo_out, NS * p + t + 1)
                        for n in range(slot.n):
                            k = slot.first + n
                            v = values[:, QT * x.batch + k, :]
                            pe.matmul(o_ps[x.u % 2], v, pT_hi[t % 3][:, n, :], start=(k == 0), stop=False)
                            last = pe.matmul(o_ps[x.u % 2], v, pT_lo[t % 3][:, n, :], start=False, stop=(k == x.blocks - 1))
                        last.then_inc(pv_done, 1)

                    def project(p, u, queries):
                        at = unit_at(p, u)
                        if at is None:
                            return
                        p, x = at
                        pe.wait_ge(oT_ready, UNITS * p + x.u + 1)
                        wait(pe, scaled, 2 * (UNITS * p + x.u))
                        wait(pe, q_lo_ready, queries)
                        for h in range(2):
                            last = pe.matmul(m_ps[:, D * h:D * h + D], oT[x.u % 2][:, P * h:P * h + P], wo[:, bass.ds(2 * p + h, 1), :],
                                             start=True, stop=True)
                        last.then_inc(projected, 1)

                    def query(number, j, pair, units):
                        pe.wait_ge(wq_in, 16 * (pair + 1))
                        wait(pe, q_lo_ready, number)
                        wait(pe, scaled, 2 * units)
                        b, half = j // 2, j % 2
                        for c in range(DC):
                            tokens = xnT[:, c, S * b:S * b + S].rearrange("p (q n) -> p q n", q=4)
                            tokens = tokens[:, 0::3, :] if half else tokens[:, 1:3, :]
                            last = pe.matmul(m_ps[:], wq[:, c, :], tokens, start=(c == 0), stop=(c == DC - 1))
                        last.then_inc(q_ready, 1)

                    def body(p):
                        queries = 4 * p + 3
                        units = UNITS * p - 2
                        for t in range(NS):
                            for v, i in CHUNKS_AT[t][:1]:
                                scores(p, v, i)
                            turn(p, t + 2)
                            for v, i in CHUNKS_AT[t][1:]:
                                scores(p, v, i)
                            weigh(p, t)
                            if t in PROJECT_AT:
                                project(p, PROJECT_AT[t], queries)
                                units = UNITS * p + PROJECT_AT[t] + 1
                            q = query_step(p, t)
                            if q:
                                query(q[0], q[1], p + (t > min(QUERIES_AT)), units)
                                queries = q[0] + 1

                    for number, j, _ in AHEAD[:2]:
                        query(number, j, 0, 0)
                    pe.wait_ge(ones_ready, 4)
                    for at in CHUNKS_AT:
                        for v, i in at:
                            if v >= UNITS:
                                scores(0, v - UNITS, i)
                    query(AHEAD[2][0], AHEAD[2][1], 0, 0)
                    for t in range(2):
                        turn(0, t)
                    pairs(pe, body)
                    for u in range(UNITS - 2, UNITS):
                        project(LAST, u, 0)

        attn.close()
        later, first = ExitStack(), ExitStack()
        rt = Routing(sbuf, later)
        ident_bf = sbuf(later, "ident_bf", [P, P], BF16)
        power4 = sbuf(later, "power4", [P, 4])
        inputs = FeedForwardInputs(sbuf, first)
        first_sem, last_sem = min(used), max(used)
        assert len(used) == last_sem - first_sem + 1
        stage_sems.append(later)
        ff_loaded = sem("ff_loaded")
        with ExitStack() as st:
            null_wT = sbuf(st, "null_wT", [H, UNITS, P])
            nt_ps = [psum(st, f"nt_ps{i}", [P, CW]) for i in range(4)]
            ny_ps = [psum(st, f"ny_ps{i}", [P, B, D]) for i in range(4)]
            null_turned, null_wT_ready, null_projected, null_added = (
                sem(n) for n in ("null_turned", "null_wT_ready", "null_projected", "null_added"))
            with nc.Block() as block:
                @block.sync
                def _(sp):
                    inputs.load(sp, aps, ff_loaded)
                    rt.load(sp, aps, ff_loaded)

                @block.tensor
                def _(pe):
                    for i in range(4):
                        for n in range(4):
                            last = pe.transpose(nt_ps[i][0:H, P * n:P * n + P], null_w[:, 4 * i + n, :], ident[:])
                        last.then_inc(null_turned, 1)
                    for i in range(QT):
                        pe.wait_ge(null_wT_ready, i // 2 + 1)
                        wait(pe, null_added, i - 3)
                        for b in range(B):
                            last = pe.matmul(ny_ps[i % 4][:, b, :], null_wT[:, 2 * i + b, :], null_wo[:], start=True, stop=True)
                        last.then_inc(null_projected, 1)

                @block.scalar
                def _(act):
                    for i in range(4):
                        act.wait_ge(null_turned, i + 1)
                        act.activation(null_wT[:, 4 * i:4 * i + 4, :], nt_ps[i][0:H, :], ACT.Copy).then_inc(null_wT_ready, 1)

                @block.vector
                def _(dve):
                    for i in range(QT):
                        dve.wait_ge(null_projected, i + 1)
                        for b in range(B):
                            x = BODY[2 * i + b]
                            y = yacc[:, QT * x.batch + x.tile, :]
                            last = dve.tensor_tensor(y, ny_ps[i % 4][:, b, :], y, ALU.add)
                        last.then_inc(null_added, 1)

        with later:
            set_up = sem("set_up")
            with nc.Block() as block:
                @block.gpsimd
                def _(pool):
                    pool.sem_clear(range(first_sem, last_sem + 1))

                @block.vector
                def _(dve):
                    dve.memset(power4[:], -0.5).then_inc(set_up, 1)
                    dve.tensor_copy(ident_bf[:], ident[:]).then_inc(set_up, 1)
            early.close()
            first_scattered, second_scattered, w1_in, w2_in = (sem(n) for n in ("first_scattered", "second_scattered", "w1_in", "w2_in"))
            with first:
                w1 = sbuf(first, "w1", [P, E, W1COLS], F32R)
                w1_hi = sbuf(first, "w1_hi", [P, E, W1COLS], F32R)
                shared_raw = [sbuf(first, f"shared_raw{i}", [P, W1COLS]) for i in range(2)]
                rows = [sbuf(first, f"m1_rows{i}", [P, ROW])[:] for i in range(BUFS)]
                rows_in = [sem(f"m1_rows_in{i}") for i in range(BUFS)]
                shared_in = [sem(f"shared_in{i}") for i in range(2)]
                with ExitStack() as turned:
                    xT_hi = sbuf(turned, "xT_hi", [P, DC, T], F32R)
                    xT_lo = sbuf(turned, "xT_lo", [P, DC, T], F32R)
                    feed_forward_stage(nc, sbuf, psum, sem, aps, (xs, yacc, ident[:], ident_bf[:], xT_hi, xT_lo, power4[:]),
                                       (inputs, ff_loaded, shared_raw, shared_in, w1, w1_in), rt, routed_rows, first_scattered)
                    shared_expert_stage(nc, sbuf, psum, sem, aps, (yacc, xT_hi, xT_lo, shared_raw, shared_in, w1_hi, w1, w1_in, rows, rows_in),
                                        rt, routed_rows, mixed, first_scattered)
                routed_mixture_stage(nc, sbuf, psum, sem, "m1_", (ident[:], w1_hi, w1, None, rows, rows_in, [yacc[:, i, :] for i in range(BUFS)], None),
                                     None, rt, routed_rows, mixed, False)
            with ExitStack() as second:
                w2 = sbuf(second, "w2", [P, E, W2COLS], F32R)
                pair_attention_stage(nc, sbuf, psum, sem, aps, (xs, yacc, ident[:], power4[:], w2, w2_in, second_scattered),
                                     rt, routed_rows, mixed, out)
                w2_hi = sbuf(second, "w2_hi", [P, E, W2COLS], F32R)
                rows = [flat(xs)[:, ROW * i:ROW * i + ROW] for i in range(BUFS)]
                rows_in = [sem(f"m2_rows_in{i}") for i in range(BUFS)]
                routed_mixture_stage(nc, sbuf, psum, sem, "m2_", (ident[:], w2_hi, w2, w2_in, rows, rows_in, [yacc[:, i, :] for i in range(BUFS)], second_scattered),
                                     (aps["ln2_w"], aps["ln2_b"]), rt, routed_rows, out, True)


def kernel(**inputs):
    import numpy as np
    import concourse.bacc as bacc
    from concourse.bass_utils import run_bass_kernel_spmd

    def by_partition(w):
        e, k, n = w.shape
        return w.reshape(e, k // P, P, n).transpose(0, 2, 1, 3).reshape(e, P, k // P * n)

    def halves(w, axis):
        return np.stack(np.split(w, 2, axis=axis))

    gate = np.concatenate([inputs["L1_cond_w_gate"], halves(inputs["L1_cond_sw_gate"], 1)])
    up = np.concatenate([inputs["L1_cond_w_up"], halves(inputs["L1_cond_sw_up"], 1)])
    down = np.concatenate([inputs["L1_cond_w_down"], halves(inputs["L1_cond_sw_down"], 0)])
    first_weights = np.concatenate([by_partition(np.concatenate([gate, up], 2)), by_partition(down)], 2)
    second_weights = np.concatenate([by_partition(inputs["L1_ffn_moe_w1"]), by_partition(inputs["L1_ffn_moe_w2"])], 2)
    nc = bacc.Bacc("TRN2", target_bir_lowering=False, num_devices=1)
    laid = {
        "x": inputs["x"].reshape(T, D),
        "bias": inputs["fside_16xSxS_0"],
        "cond": inputs["cond_64"],
        "mask": inputs["mask_BxS_bk0"].reshape(1, T),
        "g_in": inputs["L0_cond_g_in"].reshape(DC, P).T,
        "nab": inputs["L0_cond_null_attn_bias"],
        "Wq": inputs["L0_cond_Wq"],
        "Wkv": inputs["L0_cond_Wkv"],
        "Wo": inputs["L0_cond_Wo"],
        "g_out": inputs["L0_cond_g_out"].reshape(1, D),
        "ffT": inputs["L0_ffn_weight"].T,
        "wtT": inputs["L1_cond_wt"].T,
        "wgT": inputs["L1_cond_wg"].T,
        "condT": inputs["cond_64"].T,
        "order": np.tril(np.ones((E, E), np.float32), -1).reshape(1, E * E),
        "m1_w": first_weights,
        "ln1_w": inputs["L1_ffn_ln1_weight"].reshape(DC, P).T,
        "ln1_b": inputs["L1_ffn_ln1_bias"].reshape(DC, P).T,
        "ln2_w": inputs["L1_ffn_ln2_weight"].reshape(DC, P).T,
        "ln2_b": inputs["L1_ffn_ln2_bias"].reshape(DC, P).T,
        "qkvT": inputs["L1_ffn_qkv_weight"].T,
        "projT": inputs["L1_ffn_proj_weight"].T,
        "routerT": inputs["L1_ffn_router_weight"].T,
        "m2_w": second_weights,
        "slabs": (SLAB * np.arange(E, dtype=np.float32)).reshape(1, E),
        "ids": np.arange(T, dtype=np.int32).reshape(NT, P).T,
        "before": np.triu(np.ones((P, P), np.float32), 1),
        "numbers": np.arange(ROUTED, dtype=np.float32).reshape(1, ROUTED),
        "spare_rows": (E * SLAB + P * (np.arange(ROUTED, dtype=np.float32) - TOP * T // P)).reshape(1, ROUTED),
        "all_before": (16.0 * ((np.arange(ROUTED) + 1) // 2)).astype(np.float32).reshape(1, ROUTED),
    }
    laid = {n: np.ascontiguousarray(a) for n, a in laid.items()}
    aps = {n: nc.dram_tensor(n + "_dram", a.shape, mybir.dt.from_np(a.dtype), kind="ExternalInput").ap() for n, a in laid.items()}
    out = nc.dram_tensor("out_dram", (OUT_ROWS, D), F32, kind="ExternalOutput").ap()
    routed_rows = nc.dram_tensor("routed_rows", (E * SLAB + P * SPARES, ROW), F32, kind="Internal").ap()
    mixed = nc.dram_tensor("mixed", (OUT_ROWS, D), F32, kind="Internal").ap()
    program(nc, **aps, out=out, routed_rows=routed_rows, mixed=mixed)
    r = run_bass_kernel_spmd(nc, [{n + "_dram": a for n, a in laid.items()}], core_ids=[0])
    return r.results[0]["out_dram"][:T].reshape(B, S, D)
```
